# Optimizing a Trainium2 kernel written in Bass

```python
import numpy as np
import jax
import jax.numpy as jnp

def _softmax(x, axis=-1):
    return jax.nn.softmax(x, axis=axis)

def _gelu(x):
    return jax.nn.gelu(x, approximate=True)

def _silu(x):
    return jax.nn.silu(x)

def _sigmoid(x):
    return jax.nn.sigmoid(x)

def _layernorm(x, axis=-1, eps=1e-05):
    m = jnp.mean(x, axis=axis, keepdims=True)
    v = jnp.var(x, axis=axis, keepdims=True)
    return (x - m) / jnp.sqrt(v + eps)

def _scatter_add(tgt, idx, src, axis=0):
    return tgt.at[idx].add(src)

def _segment_sum(src, seg, n):
    return jax.ops.segment_sum(src, seg, n)
kernel_name = 'mk_adj_preln_d2_adj_r2_ed5572'

def setup_inputs(seed: int=0):
    np.random.seed(seed)
    _w = jnp.asarray

    def _rec_inputs():
        import jax
        import jax.numpy as jnp
        _gk = jax.random.key(seed)
        x = 0.0001732 + 1 * jax.random.normal(jax.random.fold_in(_gk, 1), (5120, 64), jnp.float32)
        _w = (1.0 + jnp.arange(5120, dtype=jnp.float32)) ** (-0.5)
        _w = _w / _w.mean()
        _pij = jnp.clip(0.000390625 * _w[:, None] * _w[None, :], 0.0, 1.0)
        _a = jax.random.uniform(jax.random.fold_in(_gk, 2), (5120, 5120)) < _pij
        _af = _a.astype(jnp.float32)
        _af = _af * jax.random.uniform(jax.random.fold_in(_gk, 3), (5120, 5120), jnp.float32, 0.05, 0.02)
        adj = _af
        return (x, adj)
    x, adj = _rec_inputs()

    def _L0_gnn_setup():
        import jax, jax.numpy as jnp
        import numpy as np
        N_USERS = 2048
        N_ITEMS = 3072
        EMB = 64
        LN_EPS = 1e-05
        key = jax.random.key(seed)
        ks = jax.random.split(key, 10)
        N = N_USERS + N_ITEMS
        ego = jax.random.normal(ks[0], (N, EMB), jnp.float32)
        adj = (jax.random.uniform(ks[1], (N, N), jnp.float32) < 0.01).astype(jnp.float32) * 0.02
        xav = float(np.sqrt(6.0 / (EMB + EMB)))
        W_u = jax.random.uniform(ks[2], (EMB, EMB), jnp.float32, -xav, xav)
        W_i = jax.random.uniform(ks[3], (EMB, EMB), jnp.float32, -xav, xav)
        diag_u = jax.random.uniform(ks[4], (N_USERS,), jnp.float32, 0.99, 1.01)
        diag_i = jax.random.uniform(ks[5], (N_ITEMS,), jnp.float32, 0.99, 1.01)
        par_u = jax.random.uniform(ks[6], (2,), jnp.float32, 0.0, 0.99)
        par_i = jax.random.uniform(ks[7], (2,), jnp.float32, 0.0, 0.99)
        ln_gamma = jnp.ones((EMB,), jnp.float32)
        ln_beta = jnp.zeros((EMB,), jnp.float32)
        return {'ego_embeddings': ego, 'adj': adj, 'W_u': W_u, 'diag_u': diag_u, 'par_u': par_u, 'W_i': W_i, 'diag_i': diag_i, 'par_i': par_i, 'ln_gamma': ln_gamma, 'ln_beta': ln_beta}
    _L0_gnn_all = _L0_gnn_setup()
    _L0_gnn_in = {k: v for k, v in _L0_gnn_all.items() if k in ('W_u', 'diag_u', 'par_u', 'W_i', 'diag_i', 'par_i', 'ln_gamma', 'ln_beta')}
    del _L0_gnn_all

    def _L1_gnn_setup():
        import jax, jax.numpy as jnp
        import numpy as np
        N = 2048
        D = 64
        NUM_LAYERS = 2
        THETA0 = 0.000244
        THETA_MAX = 0.0003
        LAM = 0.1
        TAU = 1.0
        EPS = 1e-06
        H_DENSITY = 0.005

        def _safe_norm(x, axis):
            return jnp.sqrt(jnp.maximum(jnp.sum(x * x, axis=axis), 1e-16))

        def _layer(x, H, W, Theta, Wq, bq, Wv, bv, iteration):
            scale = D ** (-0.5)
            theta_base = THETA0 + (1.0 - np.exp(-LAM * iteration)) * (THETA_MAX - THETA0)
            th_comp = theta_base
            th_edge = min(theta_base, 0.8)
            th_node = min(theta_base, 0.7)
            structural = _safe_norm(x @ W, axis=1)
            Q = x @ Wq + bq
            V = x @ Wv + bv
            edge_feat = H.T @ V
            att = Q @ edge_feat.T * scale * H
            att = jax.nn.softmax(att, axis=1)
            att_scores = att.mean(axis=0)
            importance = 0.5 * structural + 0.5 * att_scores
            comp_scores = jax.nn.softmax(importance / TAU)
            comp_mask = comp_scores >= th_comp
            x_comp = x * comp_mask[:, None]
            nrm = jnp.maximum(_safe_norm(x_comp, axis=1), 1e-08)
            xn = x_comp / nrm[:, None]
            cos = xn @ xn.T
            edge_scores = jax.nn.softmax(cos * H / TAU, axis=1)
            edge_mask = (edge_scores >= th_edge) & comp_mask[:, None]
            H_pruned = H * edge_mask
            connectivity = H_pruned.sum(axis=1)
            feat_mag = _safe_norm(x_comp, axis=1)
            node_scores = jax.nn.softmax(connectivity * feat_mag / TAU)
            connected = (H_pruned * edge_mask).sum(axis=1) > 0
            node_mask = (node_scores >= th_node) & connected
            x_final = x_comp * node_mask[:, None]
            vdeg = jnp.maximum(H_pruned.sum(axis=1), EPS)
            edeg = jnp.maximum(H_pruned.sum(axis=0), EPS)
            dv_isqrt = 1.0 / jnp.sqrt(vdeg)
            de_inv = 1.0 / edeg
            transformed = x_final @ W
            agg = H_pruned.T * dv_isqrt[None, :] @ transformed
            agg = agg * de_inv[:, None]
            msg = dv_isqrt[:, None] * (H_pruned @ agg)
            msg = msg @ Theta
            return jax.nn.relu(msg)
        key = jax.random.key(seed)
        ks = jax.random.split(key, 8)
        xav = 0.125
        X = jax.random.normal(ks[0], (N, D), jnp.float32) * 0.05
        W = jax.random.normal(ks[1], (D, D), jnp.float32) * xav
        Theta = jax.random.normal(ks[2], (D, D), jnp.float32) * xav
        Wq = jax.random.normal(ks[3], (D, D), jnp.float32) * xav
        bq = jnp.zeros((D,), jnp.float32)
        Wv = jax.random.normal(ks[4], (D, D), jnp.float32) * xav
        bv = jnp.zeros((D,), jnp.float32)
        H = (jax.random.uniform(ks[7], (N, N)) < H_DENSITY).astype(jnp.float32)
        return {'X': X, 'W': W, 'Theta': Theta, 'Wq': Wq, 'bq': bq, 'Wv': Wv, 'bv': bv, 'H': H}
    _L1_gnn_all = _L1_gnn_setup()
    _L1_gnn_in = {k: v for k, v in _L1_gnn_all.items() if k in ('W', 'Theta', 'Wq', 'bq', 'Wv', 'bv')}
    del _L1_gnn_all
    return {'x': x, 'adj': adj, 'L0_gnn_W_u': _L0_gnn_in['W_u'], 'L0_gnn_diag_u': _L0_gnn_in['diag_u'], 'L0_gnn_par_u': _L0_gnn_in['par_u'], 'L0_gnn_W_i': _L0_gnn_in['W_i'], 'L0_gnn_diag_i': _L0_gnn_in['diag_i'], 'L0_gnn_par_i': _L0_gnn_in['par_i'], 'L0_gnn_ln_gamma': _L0_gnn_in['ln_gamma'], 'L0_gnn_ln_beta': _L0_gnn_in['ln_beta'], 'L1_gnn_W': _L1_gnn_in['W'], 'L1_gnn_Theta': _L1_gnn_in['Theta'], 'L1_gnn_Wq': _L1_gnn_in['Wq'], 'L1_gnn_bq': _L1_gnn_in['bq'], 'L1_gnn_Wv': _L1_gnn_in['Wv'], 'L1_gnn_bv': _L1_gnn_in['bv']}

def reference(x, adj, L0_gnn_W_u, L0_gnn_diag_u, L0_gnn_par_u, L0_gnn_W_i, L0_gnn_diag_i, L0_gnn_par_i, L0_gnn_ln_gamma, L0_gnn_ln_beta, L1_gnn_W, L1_gnn_Theta, L1_gnn_Wq, L1_gnn_bq, L1_gnn_Wv, L1_gnn_bv):
    import jax
    import jax.numpy as jnp

    def _L0_gnn_ref(ego_embeddings, adj, W_u, diag_u, par_u, W_i, diag_i, par_i, ln_gamma, ln_beta):
        import jax, jax.numpy as jnp
        import numpy as np
        N_USERS = 2048
        N_ITEMS = 3072
        EMB = 64
        LN_EPS = 1e-05
        nu = diag_u.shape[0]
        res = ego_embeddings
        ego_u = ego_embeddings[:nu]
        ego_i = ego_embeddings[nu:]
        u = par_u[0] * par_u[1] * (diag_u[:, None] * ego_u @ W_u) + ego_u
        i = par_i[0] * par_i[1] * (diag_i[:, None] * ego_i @ W_i) + ego_i
        e = jnp.concatenate([u, i], axis=0)
        h = adj @ (adj.T @ e)
        mu = jnp.mean(h, axis=-1, keepdims=True)
        var = jnp.var(h, axis=-1, keepdims=True)
        out = (h - mu) * jax.lax.rsqrt(var + LN_EPS) * ln_gamma + ln_beta + res
        return out

    def _L1_gnn_ref(X, W, Theta, Wq, bq, Wv, bv, H):
        import jax, jax.numpy as jnp
        import numpy as np
        N = 2048
        D = 64
        NUM_LAYERS = 2
        THETA0 = 0.000244
        THETA_MAX = 0.0003
        LAM = 0.1
        TAU = 1.0
        EPS = 1e-06
        H_DENSITY = 0.005

        def _safe_norm(x, axis):
            return jnp.sqrt(jnp.maximum(jnp.sum(x * x, axis=axis), 1e-16))

        def _layer(x, H, W, Theta, Wq, bq, Wv, bv, iteration):
            scale = D ** (-0.5)
            theta_base = THETA0 + (1.0 - np.exp(-LAM * iteration)) * (THETA_MAX - THETA0)
            th_comp = theta_base
            th_edge = min(theta_base, 0.8)
            th_node = min(theta_base, 0.7)
            structural = _safe_norm(x @ W, axis=1)
            Q = x @ Wq + bq
            V = x @ Wv + bv
            edge_feat = H.T @ V
            att = Q @ edge_feat.T * scale * H
            att = jax.nn.softmax(att, axis=1)
            att_scores = att.mean(axis=0)
            importance = 0.5 * structural + 0.5 * att_scores
            comp_scores = jax.nn.softmax(importance / TAU)
            comp_mask = comp_scores >= th_comp
            x_comp = x * comp_mask[:, None]
            nrm = jnp.maximum(_safe_norm(x_comp, axis=1), 1e-08)
            xn = x_comp / nrm[:, None]
            cos = xn @ xn.T
            edge_scores = jax.nn.softmax(cos * H / TAU, axis=1)
            edge_mask = (edge_scores >= th_edge) & comp_mask[:, None]
            H_pruned = H * edge_mask
            connectivity = H_pruned.sum(axis=1)
            feat_mag = _safe_norm(x_comp, axis=1)
            node_scores = jax.nn.softmax(connectivity * feat_mag / TAU)
            connected = (H_pruned * edge_mask).sum(axis=1) > 0
            node_mask = (node_scores >= th_node) & connected
            x_final = x_comp * node_mask[:, None]
            vdeg = jnp.maximum(H_pruned.sum(axis=1), EPS)
            edeg = jnp.maximum(H_pruned.sum(axis=0), EPS)
            dv_isqrt = 1.0 / jnp.sqrt(vdeg)
            de_inv = 1.0 / edeg
            transformed = x_final @ W
            agg = H_pruned.T * dv_isqrt[None, :] @ transformed
            agg = agg * de_inv[:, None]
            msg = dv_isqrt[:, None] * (H_pruned @ agg)
            msg = msg @ Theta
            return jax.nn.relu(msg)
        x = X
        for it in range(NUM_LAYERS):
            x = _layer(x, H, W, Theta, Wq, bq, Wv, bv, it)
        return x
    h = jnp.maximum(_layernorm(x, axis=-1), 0.0)
    x = x + _L0_gnn_ref(h, adj, L0_gnn_W_u, L0_gnn_diag_u, L0_gnn_par_u, L0_gnn_W_i, L0_gnn_diag_i, L0_gnn_par_i, L0_gnn_ln_gamma, L0_gnn_ln_beta)
    h = jnp.maximum(_layernorm(x, axis=-1), 0.0)
    x = x + _L1_gnn_ref(h, L1_gnn_W, L1_gnn_Theta, L1_gnn_Wq, L1_gnn_bq, L1_gnn_Wv, L1_gnn_bv, adj)
    return x

_drawn_inputs = setup_inputs


def setup_inputs(seed=0):
    import zlib

    import numpy as np

    out = dict(_drawn_inputs(seed))
    spreads = {'L0_gnn_ln_gamma': (1.0, 0.2),
     'L0_gnn_ln_beta': (0.0, 0.1),
     'L1_gnn_bq': (0.0, 0.1),
     'L1_gnn_bv': (0.0, 0.1)}
    factors = {'L0_gnn_diag_u': 8.0, 'L0_gnn_W_i': 4.662, 'L0_gnn_diag_i': 8.0}
    for name, (base, spread) in spreads.items():
        noise = np.random.default_rng([zlib.crc32(name.encode()), seed]).standard_normal(out[name].shape)
        drawn = base * np.exp(spread * noise) if base else spread * noise
        out[name] = jnp.asarray(drawn.astype(out[name].dtype))
    for name, factor in factors.items():
        out[name] = (out[name] * factor).astype(out[name].dtype)
    return out
```

```python
import concourse.bass as bass
from concourse import mybir

FP32 = mybir.dt.float32
FP32R = mybir.dt.float32r
INT32 = mybir.dt.int32
ALU = mybir.AluOpType
ACT = mybir.ActivationFunctionType
AX = mybir.AxisListType

P = 128
N = 5120
D = 64
NB = N // P
NU = 2048
UB = NU // P
BANK = 512
NQ = N // BANK
PER = BANK // P
CH = 2 * BANK
NCH = N // CH
RING_A = 6
RING_B = 4
PAIRS = NB // 2
PAIR_SLOTS = RING_A // 2
TGS = NB // 2
T_BUFS = 5
HALF = 4 * N // 2
LN_EPS = 1e-5
EPS = 1e-6
NORM_MIN = 1e-16
THRESHOLDS = (0.000244, 0.000244 + (1.0 - 0.9048374180359595) * (0.0003 - 0.000244))
LOWEST = -3.0e38


def at_least(eng, sem, value):
    if not (isinstance(value, int) and value <= 0):
        eng.wait_ge(sem, value)


def wait_alone(eng, sem, value, other):
    if not isinstance(value, int):
        value = eng.to_reg(value)
        eng.wait_ge(other, 1)
    at_least(eng, sem, value)


class Chain:

    def __init__(self, eng, sem):
        self.eng, self.sem, self.base, self.n = eng, sem, 0, 0

    def restart(self, base):
        self.base, self.n = base, 0

    def __call__(self, ins, other=None):
        self.n += 1
        ins.then_inc(self.sem, 1)
        if other is None:
            self.eng.wait_ge(self.sem, self.base + self.n)
        else:
            wait_alone(self.eng, self.sem, self.base + self.n, other)


def steps(eng, body, unroll, count, peel=None, tail=0):
    peel = unroll if peel is None else peel
    loops = (count - peel - tail) // unroll
    for s in range(peel):
        body(s, s % unroll, s // unroll)
    with eng.Fori(0, loops) as it:
        for r in range(peel, peel + unroll):
            body(it * unroll + r, r % unroll, it + r // unroll)
    for s in range(peel + loops * unroll, count):
        body(s, s % unroll, s // unroll)


def block_of(tensor, b):
    return tensor[:, b, :] if isinstance(b, int) else tensor[:, bass.ds(b, 1), :].rearrange("p a d -> p (a d)")


def columns(tensor, first, size):
    return tensor[:, first:first + size] if isinstance(first, int) else tensor[:, bass.ds(first, size)]


def inv_sqrt(nc, link, out, v, sd, tmp):
    link(nc.vector.reciprocal(out, sd))
    link(nc.vector.tensor_tensor(tmp, v, out, ALU.mult))
    link(nc.vector.tensor_tensor(tmp, tmp, out, ALU.mult))
    link(nc.vector.tensor_scalar(tmp, tmp, -0.5, 1.5, ALU.mult, ALU.add))
    link(nc.vector.tensor_tensor(out, out, tmp, ALU.mult))


class Memory:

    def __init__(self, nc):
        self.nc, self.end = nc, -(-nc.sbuf_base // 32) * 32

    def at(self, name, offset, shape, dt=FP32):
        return self.nc.alloc_sbuf_tensor_at(name, shape, dt, offset=offset)

    def take(self, size):
        offset, self.end = self.end, self.end + -(-size // 32) * 32
        assert self.end <= self.nc.sbuf_usable_end, self.end
        return offset

    def new(self, name, shape, dt=FP32):
        size = 4
        for n in shape[1:]:
            size *= n
        return self.at(name, self.take(size), shape, dt)


class Kernel:

    def __init__(self, nc, ins, out):
        self.nc, self.i = nc, ins
        self.sems, self.spare = {}, []
        self.x_v = ins["x"].rearrange("(b p) d -> p b d", p=P)
        self.out_v = out.rearrange("(b p) d -> p b d", p=P)
        self.adj_v = ins["adj"].rearrange("(b p) n -> b p n", p=P)
        self.hp_v = nc.dram_tensor("pruned", (N, N), FP32).ap().rearrange("(b p) n -> b p n", p=P)
        m = Memory(nc)
        region = [m.take(4 * N) for _ in range(9)]
        self.ring = [m.at(f"ring{r}", region[r], [P, N]) for r in range(RING_A)]
        self.work = [m.at(f"work{r}", region[4 + r], [P, N]) for r in range(2)]
        self.stat_op = m.at("stat_op", region[6], [P, N], FP32R)
        self.mov_hi = m.at("mov_hi", region[7], [P, N], FP32R)
        self.mov_lo = m.at("mov_lo", region[8], [P, N], FP32R)
        self.colsum = m.at("colsum", region[4], [P, 3 * BANK])
        self.colsum_rows = m.at("colsum_rows", region[4] + 12 * BANK, [NB, P])
        self.wide = m.at("wide", region[5], [P, N // 2])
        self.tall = m.at("tall", region[5] + HALF, [P, NB, D])
        self.h = m.at("h", region[6], [P, NB, D])
        self.emb = m.at("emb", region[6] + HALF, [P, NB, D])
        self.xin = m.at("xin", region[7], [P, NB, D])
        self.xc = m.at("xc", region[7] + HALF, [P, NB, D])
        self.sq = m.at("sq", region[8], [P, NB, D])
        self.col_t = m.at("col_t", region[7], [P, N // 2])
        self.col = m.at("col", region[7] + HALF, [P, NB, D])
        self.adj_t = [m.at(f"adj_t{g}", region[6] + g * 4 * BANK, [P, BANK]) for g in range(T_BUFS)]
        o = region[8] + HALF
        self.h_t = [m.at(f"h_t{r}", o + r * 4 * BANK, [D, BANK]) for r in range(2)]
        self.diag_rows = m.at("diag_rows", o + 8 * BANK, [NB, P])
        self.w_ui = [m.at(f"w_{c}", o + 8 * BANK + 4 * P + j * 4 * D, [D, D]) for j, c in enumerate("ui")]
        self.beta = m.at("beta", o + 8 * BANK + 4 * P + 8 * D, [P, D])
        o = region[8]
        self.w_vw = m.at("w_vw", o, [P, 2, 2 * D])
        self.vw = m.at("vw", o + 1024, [P, 2, 2 * D])
        self.h2_t = m.at("h2_t", o + 2560, [P, 2 * P])
        self.n_t = m.at("n_t", o + 3584, [P, P])
        self.ln_in = m.at("ln_in", o + 4096, [P, 2, D])
        self.ln_out = m.at("ln_out", o + 4608, [P, 2, D])
        self.xw_sq = m.at("xw_sq", o + 5120, [P, D])
        self.gamma = m.at("gamma", o + 5376, [P, D])
        self.b_vw = m.at("b_vw", o + 5632, [P, 2 * D])
        self.n_t4 = [m.at(f"n_t4{r}", region[4] + r * 4 * BANK, [D, BANK]) for r in range(2)]
        self.q4 = [m.at(f"q4{r}", region[4] + (2 + r) * 4 * BANK, [P, BANK]) for r in range(2)]
        self.xn4 = [m.at(f"xn4{r}", region[4] + (4 + r) * 4 * BANK, [P, PER, 2, D]) for r in range(2)]
        self.n_sq = m.at("n_sq", region[5], [P, NB, D])
        self.msg = m.at("msg", region[8], [P, NB, D])
        self.g_w = m.at("g_w", region[4] + 24 * BANK, [D, 2 * D])
        self.g_b = m.at("g_b", region[4] + 24 * BANK + 8 * D, [P, D])
        self.g_xw = m.at("g_xw", region[4] + 24 * BANK + 12 * D, [P, PER, D])
        self.g_dv = m.at("g_dv", region[4] + 24 * BANK + 28 * D, [P, 1])
        self.x1 = m.new("x1", [P, NB, D])
        self.n1 = m.new("n1", [P, NB, D])
        self.ident = m.new("ident", [P, P])
        self.sel = m.new("sel", [P, P])
        self.stat_blk = [m.new(f"stat_blk{r}", [P, P], FP32R) for r in range(RING_B)]
        self.e_blk = [m.new(f"e_blk{r}", [P, D]) for r in range(2)]
        self.w_q2 = m.new("w_q2", [D, 2 * D])
        self.b_q2 = m.new("b_q2", [P, 1])
        self.b_q8 = m.new("b_q8", [P, 1])
        self.ones = m.new("ones", [P, 1])
        self.ssq_xw = m.new("ssq_xw", [P, NB])
        self.feat_mag = m.new("feat_mag", [P, NB])
        self.structural = m.new("structural", [P, NB])
        self.rows = m.new("rows", [P, NB])
        self.rows2 = m.new("rows2", [P, NB])
        self.rows3 = m.new("rows3", [P, NB])
        self.comp_mask = m.new("comp_mask", [P, NB])
        self.sq_n = m.new("sq_n", [P, NB])
        self.z = m.new("z", [P, NB])
        self.rz = m.new("rz", [P, NB])
        self.conn = m.new("conn", [P, NB])
        self.par = m.new("par", [P, 4])
        self.parp = m.new("parp", [P, 2])
        self.bn = [m.new(f"bn{j}", [P, 6]) for j in range(2)]
        self.mv = m.new("mv", [P, 2, 2])
        self.pair = [m.new(f"pair{j}", [P, 2, 1]) for j in range(3)]
        self.one = [m.new(f"one{j}", [P, 1]) for j in range(4)]
        self.mx = m.new("mx", [P, NCH])
        self.nmax = [m.new(f"nmax{r}", [P, 1]) for r in range(2)]
        self.rz_blk = [m.new(f"rz_blk{r}", [P, 1]) for r in range(2)]
        self.row1 = m.new("row1", [1, P])
        self.ones_row = m.new("ones_row", [1, P])
        self.theta = m.new("theta", [D, D])
        self.flag = m.new("flag", [1, 1], INT32)
        self.ps = nc.alloc_psum_tensor("ps", [P, 8 * BANK], FP32)
        self.constants = self.sem("constants")

    def sem(self, name):
        assert name not in self.sems, name
        self.sems[name] = self.spare.pop(0) if self.spare else self.nc.alloc_semaphore(name)
        return self.sems[name]

    def fresh_semaphores(self):
        used = {sem.num: sem for name, sem in self.sems.items() if name != "constants"}
        with self.nc.Block() as block:
            @block.gpsimd
            def _(pool):
                first = min(used)
                for n in range(min(used), max(used) + 1):
                    if n + 1 not in used:
                        pool.sem_clear(range(first, n + 1))
                        first = n + 2

            for engine in (block.sync, block.scalar, block.vector, block.tensor):
                @engine
                def _(eng):
                    eng.wait_ge(self.constants, 1)
        self.sems = {"constants": self.constants}
        self.spare = [used[n] for n in sorted(used)]

    def sem_list(self, name, n):
        return [self.sem(f"{name}{j}") for j in range(n)]

    def bank(self, b, cols=BANK, first=0, rows=slice(0, P)):
        return self.ps[rows, b * BANK + first:b * BANK + first + cols]

    def half_acc(self, q, cols=BANK, first=0):
        return self.bank(q // 2, cols, first, slice(D * (q % 2), D * (q % 2) + D))


def load_ring(k, eng, src, loaded, used, ring, down, resident, per=1):
    def load(s, r, turn):
        if isinstance(s, int) and s < ring:
            if resident:
                return
        else:
            wait_alone(eng, used, (s - ring + 1) * per, k.constants)
        b = NB - 1 - s if down else s
        blk = src[b] if isinstance(b, int) else src[bass.ds(b, 1), :, :].rearrange("a p n -> (a p) n")
        eng.dma_start(k.ring[slot_of(r, ring, down)][:], blk).then_inc(loaded[r], 16)
    steps(eng, load, ring, NB)


def slot_of(r, ring, down):
    return (NB - 1 - r if down else r) % ring


def wait_loaded(eng, loaded, r, turn, resident):
    at_least(eng, loaded[r], 16 * turn + (0 if resident else 16))


def column_pass(k, tag, src, operand, ring, down=False, resident=False, degrees=False,
                first=None, last=None):
    nc = k.nc
    loaded, used = k.sem_list(f"{tag}_loaded", ring), k.sem(f"{tag}_used")
    placed = k.sem(f"{tag}_operand_placed")
    first, last = first or {}, last or {}
    with nc.Block() as block:
        @block.sync
        def _(sp):
            if "sync" in first:
                first["sync"](sp)
            load_ring(k, sp, src, loaded, used, ring, down, resident)

        @block.gpsimd
        def _(pool):
            if "gpsimd" in first:
                first["gpsimd"](pool)

        @block.scalar
        def _(act):
            if "scalar" in first:
                first["scalar"](act)

            def place(s, r, turn):
                if not (isinstance(s, int) and s < 2):
                    act.wait_ge(used, s - 1)
                nc.scalar.activation(k.e_blk[r % 2][:], block_of(operand, NB - 1 - s if down else s),
                                     ACT.Copy).then_inc(placed, 1)
            steps(act, place, ring, NB)
            if "scalar" in last:
                act.wait_ge(used, NB)
                last["scalar"](act)

        @block.vector
        def _(dve):
            if "vector" in first:
                first["vector"](dve)
            if "vector" in last:
                dve.wait_ge(used, NB)
                last["vector"](dve)

        @block.tensor
        def _(pe):
            if "tensor" in first:
                first["tensor"](pe)

            def product(s, r, turn):
                pe.wait_ge(placed, s + 1)
                wait_loaded(pe, loaded, r, turn, resident)
                rows = k.ring[slot_of(r, ring, down)]
                begin = isinstance(s, int) and s == 0
                for q in range(NQ):
                    done = nc.tensor.matmul(k.half_acc(q), k.e_blk[r % 2][:], rows[:, q * BANK:(q + 1) * BANK],
                                            start=begin, stop=True, skip_group_check=True)
                if degrees:
                    for q in range(NQ):
                        done = nc.tensor.matmul(k.bank(5 + q // 4, rows=slice(32 * (q % 4), 32 * (q % 4) + 1)),
                                                k.ones[:], rows[:, q * BANK:(q + 1) * BANK],
                                                start=begin, stop=True, skip_group_check=True)
                done.then_inc(used, 1)
            steps(pe, product, ring, NB)
            if "tensor" in last:
                last["tensor"](pe)


def by_blocks(k, tag, wide, tall, scale=None):
    nc = k.nc
    out, turned, read = k.sem(f"{tag}_out"), k.sem(f"{tag}_turned"), k.sem(f"{tag}_read")
    tall_v = tall[:].rearrange("p (q h m) d -> p q h m d", h=2, m=PER)
    with nc.Block() as block:
        @block.scalar
        def _(act):
            for b in range(NQ // 2):
                nc.scalar.activation(wide[:, b * BANK:(b + 1) * BANK], k.bank(b), ACT.Copy).then_inc(out, 1)

        @block.tensor
        def _(pe):
            for b in range(NQ // 2):
                pe.wait_ge(out, b + 1)
                at_least(pe, read, b - 1)
                for m in range(PER):
                    c = b * BANK + m * P
                    done = nc.tensor.transpose(k.bank(6 + b % 2, P, m * P), wide[:, c:c + P], k.ident[:])
                done.then_inc(turned, 1)

        @block.vector
        def _(dve):
            for b in range(NQ // 2):
                dve.wait_ge(turned, b + 1)
                for h in range(2):
                    src = k.bank(6 + b % 2).rearrange("p (m h d) -> p m h d", h=2, d=D)[:, :, h, :]
                    if scale is None:
                        done = nc.vector.tensor_copy(tall_v[:, b, h], src)
                    else:
                        s = scale[:].rearrange("p (q h m) -> p q h m", h=2, m=PER)[:, b, h]
                        done = nc.vector.tensor_tensor(tall_v[:, b, h], src,
                                                       s.unsqueeze(2).to_broadcast([P, PER, D]), ALU.mult)
                done.then_inc(read, 1)
            dve.wait_ge(read, NQ // 2)



def embed_and_columns(k):
    nc, i = k.nc, k.i
    s_x, s_par = k.sem("x_loaded"), k.sem("embed_weights")
    own, pool_own = k.sem("embed_own"), k.sem("constants_own")
    ln_var, ln_sd, h_ready, const_ready = k.sem("embed_var"), k.sem("embed_sd"), k.sem("h_ready"), k.constants
    ht_done, ht_copied, hw_done, e_ready = k.sem("ht_done"), k.sem("ht_copied"), k.sem("hw_done"), k.sem("e_ready")
    diag_t = k.sem("diag_transposed")
    groups = NB // PER
    N_PAR = 7

    def sync(sp):
        sp.dma_start(k.xin[:], k.x_v).then_inc(s_x, 16)

    def gpsimd(pool):
        nc.gpsimd.memset(k.ones[:], 1.0).then_inc(const_ready, 1)
        nc.gpsimd.memset(k.ones_row[:], 1.0).then_inc(const_ready, 1)
        link = Chain(pool, pool_own)
        link(nc.gpsimd.memset(k.ident[:], 0.0))
        link(nc.gpsimd.memset(k.sel[:], 0.0))
        for tensor, base in ((k.ident, 0), (k.sel, 0), (k.sel, D), (k.sel, -D)):
            ins = nc.gpsimd.affine_select(out=tensor[:], in_=tensor[:], compare_op=ALU.not_equal, fill=1.0,
                                          base=base, pattern=[[-1, P]], channel_multiplier=1)
            link(ins)

    def scalar(act):
        for dst, src in ((k.w_ui[0][:], i["W_u"]), (k.w_ui[1][:], i["W_i"]),
                         (k.diag_rows[0:UB, :], i["diag_u"].rearrange("(b p) -> b p", p=P)),
                         (k.diag_rows[UB:NB, :], i["diag_i"].rearrange("(b p) -> b p", p=P)),
                         (k.par[:, 0:2], i["par_u"].partition_broadcast(P)),
                         (k.par[:, 2:4], i["par_i"].partition_broadcast(P)),
                         (k.beta[:], i["ln_beta"].partition_broadcast(P))):
            act.dma_start(dst, src).then_inc(s_par, 16)
        act.wait_ge(ln_var, 1)
        nc.scalar.activation(k.rows2[:], k.rows[:], ACT.Sqrt).then_inc(ln_sd, 1)
        for g in range(groups):
            act.wait_ge(ht_done, g + 1)
            at_least(act, hw_done, g - 1)
            nc.scalar.activation(k.h_t[g % 2][:], k.bank(g % 2, rows=slice(0, D)), ACT.Copy).then_inc(ht_copied, 1)

    def vector(dve):
        link = Chain(dve, own)
        whole = [P, NB, D]
        dve.wait_ge(s_x, 16)
        link(nc.vector.reduce_sum(k.rows3[:], k.xin[:], AX.X))
        link(nc.vector.tensor_scalar(k.rows3[:], k.rows3[:], 1.0 / D, None, ALU.mult))
        link(nc.vector.tensor_tensor(k.xc[:], k.xin[:], k.rows3[:].unsqueeze(2).to_broadcast(whole), ALU.subtract))
        link(nc.vector.tensor_tensor(k.sq[:], k.xc[:], k.xc[:], ALU.mult))
        link(nc.vector.reduce_sum(k.rows[:], k.sq[:], AX.X))
        nc.vector.tensor_scalar(k.rows[:], k.rows[:], 1.0 / D, LN_EPS, ALU.mult, ALU.add).then_inc(ln_var, 1)
        dve.wait_ge(ln_var, 1)
        dve.wait_ge(ln_sd, 1)
        inv_sqrt(nc, link, k.rows2[:], k.rows[:], k.rows2[:], k.rows3[:])
        link(nc.vector.tensor_tensor(k.xc[:], k.xc[:], k.rows2[:].unsqueeze(2).to_broadcast(whole), ALU.mult))
        nc.vector.tensor_scalar(k.h[:], k.xc[:], 0.0, None, ALU.max).then_inc(h_ready, 1)
        dve.wait_ge(s_par, N_PAR * 16)
        link(nc.vector.tensor_tensor(k.parp[:, 0:1], k.par[:, 0:1], k.par[:, 1:2], ALU.mult))
        link(nc.vector.tensor_tensor(k.parp[:, 1:2], k.par[:, 2:3], k.par[:, 3:4], ALU.mult))
        dve.wait_ge(diag_t, 1)
        link(nc.vector.tensor_scalar(k.rows[:, 0:UB], k.bank(6, UB), k.parp[:, 0:1], None, ALU.mult))
        link(nc.vector.tensor_scalar(k.rows[:, UB:NB], k.bank(6, NB - UB, UB), k.parp[:, 1:2], None, ALU.mult))
        for g in range(groups):
            dve.wait_ge(hw_done, g + 1)
            b = slice(g * PER, (g + 1) * PER)
            hw = k.bank(2 + g % 2, PER * D).rearrange("p (b d) -> p b d", d=D)
            link(nc.vector.tensor_tensor(k.emb[:, b, :], hw, k.rows[:, b].unsqueeze(2).to_broadcast([P, PER, D]), ALU.mult))
            nc.vector.tensor_tensor(k.emb[:, b, :], k.emb[:, b, :], k.h[:, b, :], ALU.add).then_inc(e_ready, 1)
        dve.wait_ge(h_ready, 1)
        link(nc.vector.tensor_tensor(k.x1[:], k.xin[:], k.beta[:].unsqueeze(1).to_broadcast(whole), ALU.add))
        link(nc.vector.tensor_tensor(k.x1[:], k.x1[:], k.h[:], ALU.add))

    def tensor(pe):
        pe.wait_ge(pool_own, 3)
        pe.wait_ge(s_par, N_PAR * 16)
        nc.tensor.transpose(k.bank(6, NB), k.diag_rows[:], k.ident[0:NB, 0:NB]).then_inc(diag_t, 1)
        pe.wait_ge(h_ready, 1)
        for g in range(groups + 1):
            if g < groups:
                at_least(pe, ht_copied, g - 1)
                for j in range(PER):
                    done = nc.tensor.transpose(k.bank(g % 2, P, j * P, slice(0, D)), k.h[:, g * PER + j, :], k.ident[:])
                done.then_inc(ht_done, 1)
            if g >= 1:
                f = g - 1
                pe.wait_ge(ht_copied, f + 1)
                at_least(pe, e_ready, f - 1)
                for j in range(PER):
                    w = k.w_ui[0 if f * PER + j < UB else 1]
                    done = nc.tensor.matmul(k.bank(2 + f % 2, D, j * D), k.h_t[f % 2][:, j * P:(j + 1) * P], w[:],
                                            start=True, stop=True)
                done.then_inc(hw_done, 1)
        pe.wait_ge(e_ready, groups)

    def scalar_first(act):
        scalar(act)
        act.wait_ge(e_ready, groups)

    column_pass(k, "a1", k.adj_v, k.emb, RING_A,
                first={"sync": sync, "gpsimd": gpsimd, "scalar": scalar_first, "vector": vector, "tensor": tensor})
    by_blocks(k, "col", k.col_t, k.col)


def network_and_features(k):
    nc, i = k.nc, k.i
    s_par, zeroed = k.sem("feature_weights"), k.sem("feature_zeros")
    loaded, used = k.sem_list("pair_loaded", RING_A), k.sem("pair_used")
    t_ready, t_copied = k.sem("transposed"), k.sem("transposed_copied")
    h2_done, h2_copied = k.sem("h2_done"), k.sem("h2_copied")
    back, back_read = k.sem("h2_back"), k.sem("h2_back_read")
    var, sd, own = k.sem("pair_var"), k.sem("pair_sd"), k.sem("pair_own")
    n_ready, n_saved = k.sem("n_ready"), k.sem("n_saved")
    nt_done, nt_copied = k.sem("nt_done"), k.sem("nt_copied")
    v_done, v_ready, xw_own = k.sem("v_done"), k.sem("v_ready"), k.sem("xw_own")
    N_PAR = 11
    t_bank = [5, 6, 5] + [5, 6, 5, 6] + [6] + [6 if g % 2 == 0 else 5 for g in range(8, TGS)]
    BACK_BANK, NT_BANK, V_BANK, H2_BANK = 6, 5, 5, 7

    def pair_of(tensor, p):
        b = NB - 2 - 2 * p
        return tensor[:, b:b + 2, :] if isinstance(b, int) else tensor[:, bass.ds(b, 2), :]

    with nc.Block() as block:
        @block.sync
        def _(sp):
            sp.wait_ge(zeroed, 2)
            for dst, src in ((k.gamma[:], i["ln_gamma"].partition_broadcast(P)),
                             (k.w_vw[0:D, 0, 0:D], i["Wv"]), (k.w_vw[0:D, 0, D:2 * D], i["W"]),
                             (k.w_vw[D:P, 1, 0:D], i["Wv"]), (k.w_vw[D:P, 1, D:2 * D], i["W"]),
                             (k.b_vw[:, 0:D], i["bv"].partition_broadcast(P)),
                             (k.w_q2[:, 0:D], i["Wq"]), (k.w_q2[:, D:2 * D], i["Wq"]),
                             (k.b_q2[0:D, :], i["bq"].rearrange("(d a) -> d a", a=1)),
                             (k.b_q2[D:P, :], i["bq"].rearrange("(d a) -> d a", a=1)),
                             (k.theta[:], i["Theta"])):
                sp.dma_start(dst, src).then_inc(s_par, 16)
            load_ring(k, sp, k.adj_v, loaded, used, RING_A, True, True)

        @block.gpsimd
        def _(pool):
            nc.gpsimd.memset(k.w_vw[:], 0.0).then_inc(zeroed, 1)
            nc.gpsimd.memset(k.b_vw[:], 0.0).then_inc(zeroed, 1)

            def save(t, r, turn):
                pool.wait_ge(n_ready, t + 1)
                nc.gpsimd.tensor_copy(pair_of(k.n1, t), k.ln_out[:]).then_inc(n_saved, 1)
            steps(pool, save, 1, PAIRS)

        @block.scalar
        def _(act):
            def step(p, r, turn):
                now = not (isinstance(p, int) and p == PAIRS)
                before = not (isinstance(p, int) and p == 0)

                def copy_group(g):
                    act.wait_ge(t_ready, TGS * p + g + 1)
                    nc.scalar.activation(k.adj_t[g % T_BUFS][:], k.bank(t_bank[g]), ACT.Copy).then_inc(t_copied, 1)

                for g in range(TGS):
                    if now:
                        copy_group(g)
                    if not before:
                        continue
                    if g == 1:
                        act.wait_ge(h2_done, p)
                        at_least(act, back, p - 1)
                        nc.scalar.activation(k.h2_t[:], k.bank(H2_BANK, 2 * P), ACT.Copy).then_inc(h2_copied, 1)
                    if g in (4, 5):
                        act.wait_ge(var, 2 * (p - 1) + g - 3)
                        nc.scalar.activation(k.pair[1][:], k.pair[0][:], ACT.Sqrt).then_inc(sd, 1)
                    if g == 6:
                        act.wait_ge(nt_done, p)
                        nc.scalar.activation(k.n_t[:], k.bank(NT_BANK, P), ACT.Copy).then_inc(nt_copied, 1)
                    if g == 10:
                        act.wait_ge(v_ready, p)
                        for j in range(2):
                            b = NB - 2 - 2 * (p - 1) + j
                            nc.scalar.activation(k.xw_sq[:], k.vw[:, j, D:2 * D], ACT.Square,
                                                 accum_out=columns(k.ssq_xw, b, 1)).then_inc(xw_own, 1)
                            act.wait_ge(xw_own, 2 * (p - 1) + j + 1)
            steps(act, step, 1, PAIRS + 1, tail=1)

        @block.vector
        def _(dve):
            link = Chain(dve, own)
            two = [P, 2, D]
            dve.wait_ge(s_par, N_PAR * 16)
            link(nc.vector.tensor_scalar(k.b_q8[:], k.b_q2[:], 1.0 / 8, None, ALU.mult))
            OPS = 29

            def norm(t, which):
                for j in range(2):
                    link(nc.vector.bn_stats(k.bn[j][:], k.ln_in[:, j, :]), k.constants)
                for j in range(2):
                    link(nc.vector.bn_aggr(k.mv[:, j, :], k.bn[j][:]), k.constants)
                link(nc.vector.tensor_scalar(k.pair[0][:], k.mv[:, :, 1:2], LN_EPS, None, ALU.add))
                nc.vector.tensor_copy(k.pair[2][:], k.pair[0][:]).then_inc(var, 1)
                dve.wait_ge(var, 2 * t + which + 1)
                dve.wait_ge(sd, 2 * t + which + 1)
                inv_sqrt(nc, link, k.pair[1][:], k.pair[0][:], k.pair[1][:], k.pair[2][:])
                link(nc.vector.tensor_tensor(k.ln_out[:], k.ln_in[:], k.mv[:, :, 0:1].to_broadcast(two), ALU.subtract))
                link(nc.vector.tensor_tensor(k.ln_out[:], k.ln_out[:], k.pair[1][:].to_broadcast(two), ALU.mult))

            def step(t, r, turn):
                link.restart(1 + OPS * t)
                dve.wait_ge(back, t + 1)
                nc.vector.tensor_copy(k.ln_in[:], k.bank(BACK_BANK, P)).then_inc(back_read, 1)
                dve.wait_ge(back_read, t + 1)
                at_least(dve, n_saved, t)
                at_least(dve, nt_done, t)
                norm(t, 0)
                link(nc.vector.tensor_tensor(k.ln_out[:], k.ln_out[:], k.gamma[:].unsqueeze(1).to_broadcast(two), ALU.mult), k.constants)
                link(nc.vector.tensor_tensor(k.ln_in[:], k.ln_out[:], pair_of(k.x1, t), ALU.add), k.constants)
                link(nc.vector.tensor_copy(pair_of(k.x1, t), k.ln_in[:]))
                link(nc.vector.tensor_copy(k.ln_in[:], k.ln_in[:]))
                norm(t, 1)
                link(nc.vector.tensor_scalar(k.ln_out[:], k.ln_out[:], 0.0, None, ALU.max))
                nc.vector.tensor_copy(k.pair[2][:], k.pair[0][:]).then_inc(n_ready, 1)
                dve.wait_ge(n_ready, t + 1)
                dve.wait_ge(v_done, t + 1)
                at_least(dve, used, 2 * t)
                at_least(dve, xw_own, 2 * t)
                nc.vector.tensor_tensor(k.vw[:], k.bank(V_BANK, 4 * D).rearrange("p (j c) -> p j c", j=2),
                                        k.b_vw[:].unsqueeze(1).to_broadcast([P, 2, 2 * D]), ALU.add).then_inc(v_ready, 1)
                assert link.n == OPS, link.n
            steps(dve, step, 1, PAIRS)

        @block.tensor
        def _(pe):
            pe.wait_ge(s_par, N_PAR * 16)

            def slots(r):
                b = (NB - 2 - 2 * r) % RING_A
                return k.ring[b], k.ring[b + 1]

            def step(p, r, turn):
                now = not (isinstance(p, int) and p == PAIRS)
                before = not (isinstance(p, int) and p == 0)
                blocks, old = slots(r), slots((r - 1) % PAIR_SLOTS)

                def transposes(g):
                    if g == 0:
                        at_least(pe, t_copied, TGS * p)
                        for j in (1, 0):
                            wait_loaded(pe, loaded, 2 * r + 1 - j, turn, True)
                    elif g == 4 and before:
                        pe.wait_ge(back_read, p)
                    elif g == 9 and before:
                        pe.wait_ge(v_ready, p)
                    elif g >= 2:
                        pe.wait_ge(t_copied, TGS * p + (g if g in (3, 7, 8) else g - 1))
                    for c in range(2):
                        for j in range(2):
                            col = (2 * g + c) * P
                            done = nc.tensor.transpose(k.bank(t_bank[g], P, (2 * c + j) * P),
                                                       blocks[j][:, col:col + P], k.ident[:])
                    done.then_inc(t_ready, 1)

                def product(q, g):
                    pe.wait_ge(t_copied, TGS * q + g + 1)
                    if g == 0:
                        at_least(pe, h2_copied, q)
                    for c in range(2):
                        done = nc.tensor.matmul(k.bank(H2_BANK, 2 * P, 0, slice(D * c, D * c + D)), k.col[:, 2 * g + c, :],
                                                k.adj_t[g % T_BUFS][:, 2 * P * c:2 * P * (c + 1)],
                                                start=g == 0, stop=g == TGS - 1)
                    if g == TGS - 1:
                        done.then_inc(h2_done, 1)

                def features(n):
                    j = 1 - n // (NQ // 2)
                    if n == 0:
                        pe.wait_ge(v_ready, p)
                    for q in range(2 * n % NQ, 2 * n % NQ + 2):
                        done = nc.tensor.matmul(k.half_acc(q), k.vw[:, j, 0:D], old[j][:, q * BANK:(q + 1) * BANK],
                                                start=isinstance(p, int) and p == 1 and n < NQ // 2, stop=True,
                                                skip_group_check=True)
                    if n % (NQ // 2) == NQ // 2 - 1:
                        done.then_inc(used, 1)

                for g in range(TGS):
                    if now:
                        transposes(g)
                    if g < 2:
                        if before:
                            product(p - 1, TGS - 2 + g)
                    elif now:
                        product(p, g - 2)
                    if before and g >= TGS - NQ:
                        features(g - (TGS - NQ))
                    if before and g == 2:
                        pe.wait_ge(h2_copied, p)
                        pe.wait_ge(t_copied, TGS * p + (2 if now else 0))
                        for j in range(2):
                            done = nc.tensor.matmul(k.bank(BACK_BANK, D, j * D), k.h2_t[:, j * P:(j + 1) * P],
                                                    k.sel[:, 0:D], start=True, stop=True)
                        done.then_inc(back, 1)
                    if before and g == 6:
                        pe.wait_ge(n_ready, p)
                        if now:
                            pe.wait_ge(t_copied, TGS * p + 6)
                        nc.tensor.transpose(k.bank(NT_BANK, P), k.ln_out[:].rearrange("p j d -> p (j d)"),
                                            k.ident[:]).then_inc(nt_done, 1)
                    if before and g == 7:
                        pe.wait_ge(nt_copied, p)
                        nc.tensor.matmul(k.bank(V_BANK, 4 * D), k.n_t[:], k.w_vw[:].rearrange("p j c -> p (j c)"),
                                         start=True, stop=True).then_inc(v_done, 1)
            steps(pe, step, PAIR_SLOTS, PAIRS + 1, peel=1, tail=1)



def attention_operands(k, tag):
    nc = k.nc
    wide_ready, doubled = k.sem(f"{tag}_wide"), k.sem(f"{tag}_doubled")
    hi_done, lo_done = k.sem(f"{tag}_hi"), k.sem(f"{tag}_lo")
    nt_done, nt_copied, q_done = k.sem(f"{tag}_nt"), k.sem(f"{tag}_nt_copied"), k.sem(f"{tag}_q")
    q_hi, q_lo, q_own = k.sem(f"{tag}_q_hi"), k.sem(f"{tag}_q_lo"), k.sem(f"{tag}_q_own")
    with nc.Block() as block:
        @block.scalar
        def _(act):
            for b in range(NQ // 2):
                nc.scalar.activation(k.wide[:, b * BANK:(b + 1) * BANK], k.bank(b), ACT.Copy).then_inc(wide_ready, 1)
            for q in range(NQ + 1):
                if q < NQ:
                    cols = slice(q * BANK, (q + 1) * BANK)
                    act.wait_ge(doubled, q + 1)
                    nc.scalar.activation(k.mov_hi[:, cols], k.bank(5 + q % 2), ACT.Copy).then_inc(hi_done, 1)
                    act.wait_ge(nt_done, q + 1)
                    at_least(act, q_done, q - 1)
                    nc.scalar.activation(k.n_t4[q % 2][:], k.bank(q % 2, rows=slice(0, D)), ACT.Copy).then_inc(nt_copied, 1)
                if q >= 1:
                    f = q - 1
                    act.wait_ge(q_done, f + 1)
                    nc.scalar.activation(k.stat_op[:, f * BANK:(f + 1) * BANK], k.bank(2 + f % 2), ACT.Identity,
                                         bias=k.b_q8[:], scale=1.0 / 8).then_inc(q_hi, 1)

        @block.tensor
        def _(pe):
            for q in range(NQ + 1):
                if q < NQ:
                    h = q % 2
                    pe.wait_ge(wide_ready, q // 2 + 1)
                    at_least(pe, lo_done, q - 1)
                    nc.tensor.matmul(k.bank(5 + h), k.sel[D * h:D * h + D, :],
                                     k.wide[D * h:D * h + D, q // 2 * BANK:(q // 2 + 1) * BANK],
                                     start=True, stop=True).then_inc(doubled, 1)
                    if q == 0:
                        pe.wait_ge(wide_ready, NQ // 2)
                    at_least(pe, nt_copied, q - 1)
                    for m in range(PER):
                        done = nc.tensor.transpose(k.bank(q % 2, P, m * P, slice(0, D)), k.n1[:, q * PER + m, :], k.ident[:])
                    done.then_inc(nt_done, 1)
                if q >= 1:
                    f = q - 1
                    pe.wait_ge(nt_copied, f + 1)
                    at_least(pe, q_lo, f - 1)
                    nc.tensor.matmul(k.bank(2 + f % 2), k.w_q2[:], k.n_t4[f % 2][:], start=True, stop=True).then_inc(q_done, 1)

        @block.vector
        def _(dve):
            for q in range(NQ + 1):
                if q < NQ:
                    cols = slice(q * BANK, (q + 1) * BANK)
                    dve.wait_ge(hi_done, q + 1)
                    nc.vector.tensor_tensor(k.mov_lo[:, cols], k.bank(5 + q % 2), k.mov_hi[:, cols].bitcast(FP32),
                                            ALU.subtract).then_inc(lo_done, 1)
                if q >= 1:
                    f = q - 1
                    cols, low = slice(f * BANK, (f + 1) * BANK), slice(D, P)
                    dve.wait_ge(q_hi, f + 1)
                    at_least(dve, q_lo, f - 1)
                    nc.vector.tensor_scalar(k.q4[f % 2][low, :], k.bank(2 + f % 2, rows=low), 1.0 / 8, k.b_q8[low, :],
                                            ALU.mult, ALU.add).then_inc(q_own, 1)
                    dve.wait_ge(q_own, f + 1)
                    nc.vector.tensor_tensor(k.stat_op[low, cols], k.q4[f % 2][low, :], k.stat_op[low, cols].bitcast(FP32),
                                            ALU.subtract).then_inc(q_lo, 1)


ATTENTION, EDGES, PRUNE = range(3)


def score_pass(k, tag, mode, down, resident, threshold=0.0, first_sync=None):
    nc = k.nc
    loaded, stat_ready = k.sem_list(f"{tag}_loaded", RING_B), k.sem(f"{tag}_stat")
    scored, masked, neg_max = k.sem(f"{tag}_scored"), k.sem(f"{tag}_times_adj"), k.sem(f"{tag}_max")
    exp_done, rz_ready, summed = k.sem(f"{tag}_exp"), k.sem(f"{tag}_rz"), k.sem(f"{tag}_summed")
    pruned, own, stored = k.sem(f"{tag}_pruned"), k.sem(f"{tag}_own"), k.sem_list(f"{tag}_stored", 2)
    bufs = 2 if mode == ATTENTION else 4

    def node_block(s):
        return NB - 1 - s if down else s

    def scores(r, ch):
        b = 2 * ((r + ch) % bufs)
        return k.ps[:, b * BANK:(b + 2) * BANK]

    with nc.Block() as block:
        @block.sync
        def _(sp):
            if first_sync is not None:
                first_sync(sp)
            if mode != PRUNE:
                load_ring(k, sp, k.adj_v, loaded, masked, RING_B, down, resident, per=NCH)
                return

            def step(s, r, turn):
                if not (isinstance(s, int) and s < RING_B):
                    store(s - RING_B, r)
                b = node_block(s)
                if not (isinstance(s, int) and s < RING_B and resident):
                    blk = k.adj_v[b] if isinstance(b, int) else k.adj_v[bass.ds(b, 1), :, :].rearrange("a p n -> (a p) n")
                    sp.dma_start(k.ring[slot_of(r, RING_B, down)][:], blk).then_inc(loaded[r], 16)

            def store(s, r):
                wait_alone(sp, pruned, s + 1, k.constants)
                b = node_block(s)
                blk = k.hp_v[b] if isinstance(b, int) else k.hp_v[bass.ds(b, 1), :, :].rearrange("a p n -> (a p) n")
                sp.dma_start(blk, k.work[r % 2][:]).then_inc(stored[r % 2], 16)
            steps(sp, step, RING_B, NB)
            for s in range(NB - RING_B, NB):
                store(s, s % RING_B)
            for j in range(2):
                sp.wait_ge(stored[j], 16 * NB // 2)

        @block.gpsimd
        def _(pool):
            def step(s, r, turn):
                if not (isinstance(s, int) and s < RING_B):
                    pool.wait_ge(scored, NCH * (s - RING_B + 1))
                c = node_block(s) * P
                if mode == ATTENTION:
                    nc.gpsimd.tensor_copy(k.stat_blk[r][:], columns(k.stat_op, c, P)).then_inc(stat_ready, 2)
                else:
                    for half, part in ((slice(0, D), k.mov_hi), (slice(D, P), k.mov_lo)):
                        src = part[half, c:c + P] if isinstance(c, int) else part[half, bass.ds(c, P)]
                        nc.gpsimd.tensor_copy(k.stat_blk[r][half, :], src).then_inc(stat_ready, 1)
            steps(pool, step, RING_B, NB)

        @block.tensor
        def _(pe):
            def step(s, r, turn):
                if not (isinstance(s, int) and s == NB):
                    pe.wait_ge(stat_ready, 2 * s + 2)
                    for ch in range(NCH):
                        at_least(pe, masked, NCH * s + ch - bufs + 1)
                        out = scores(r, ch)
                        for part, begin in ((k.mov_hi, True), (k.mov_lo, False)):
                            for h in range(2):
                                c = ch * CH + h * BANK
                                done = nc.tensor.matmul(out[:, h * BANK:(h + 1) * BANK], k.stat_blk[r][:],
                                                        part[:, c:c + BANK], start=begin, stop=not begin)
                        done.then_inc(scored, 1)
                if mode == ATTENTION and not (isinstance(s, int) and s == 0):
                    pe.wait_ge(rz_ready, s)
                    for q in range(NQ):
                        done = nc.tensor.matmul(k.bank(4 + q // 4, rows=slice(32 * (q % 4), 32 * (q % 4) + 1)),
                                                k.rz_blk[(r - 1) % 2][:],
                                                k.work[(r - 1) % 2][:, q * BANK:(q + 1) * BANK],
                                                start=isinstance(s, int) and s == 1, stop=True, skip_group_check=True)
                    done.then_inc(summed, 1)
            steps(pe, step, RING_B, NB + 1, peel=2, tail=1)

        @block.scalar
        def _(act):
            def step(s, r, turn):
                act.wait_ge(neg_max, s + 1)
                w = k.work[r % 2]
                nc.scalar.activation(w[:], w[:], ACT.Exp, bias=k.nmax[r % 2][:],
                                     accum_out=columns(k.z, node_block(s), 1)).then_inc(exp_done, 1)
            steps(act, step, RING_B, NB)

        @block.vector
        def _(dve):
            def finish(s, r):
                if mode == EDGES:
                    return
                b = node_block(s - 1)
                w, j = k.work[(r - 1) % 2], (r - 1) % 2
                wait_alone(dve, exp_done, s, k.constants)
                if mode == ATTENTION:
                    nc.vector.reciprocal(k.rz_blk[j][:], columns(k.z, b, 1)).then_inc(rz_ready, 1)
                    return
                nc.vector.reciprocal(k.rz_blk[j][:], columns(k.z, b, 1)).then_inc(own, 1)
                wait_alone(dve, own, 2 * s - 1, k.constants)
                nc.vector.tensor_scalar(w[:], w[:], k.rz_blk[j][:], threshold, ALU.mult, ALU.is_ge).then_inc(own, 1)
                wait_alone(dve, own, 2 * s, k.constants)
                nc.vector.scalar_tensor_tensor(w[:], w[:], columns(k.comp_mask, b, 1),
                                               k.ring[slot_of((r - 1) % RING_B, RING_B, down)][:], ALU.mult, ALU.mult,
                                               accum_out=columns(k.conn, b, 1)).then_inc(pruned, 1)

            def step(s, r, turn):
                if isinstance(s, int) and s == NB:
                    finish(s, r)
                    return
                wait_loaded(dve, loaded, r, turn, resident)
                if mode == PRUNE:
                    at_least(dve, stored[r % 2], 32 * turn + 16 * (r // 2))
                else:
                    at_least(dve, summed if mode == ATTENTION else exp_done, s - 1)
                rows = k.ring[slot_of(r, RING_B, down)]
                for ch in range(NCH):
                    cols = slice(ch * CH, (ch + 1) * CH)
                    wait_alone(dve, scored, NCH * s + ch + 1, k.constants)
                    nc.vector.tensor_tensor_reduce(out=k.work[r % 2][:, cols], in0=scores(r, ch), in1=rows[:, cols],
                                                   scale=1.0, scalar=LOWEST, op0=ALU.mult, op1=ALU.max,
                                                   accum_out=k.mx[:, ch:ch + 1]).then_inc(masked, 1)
                if mode == ATTENTION and not (isinstance(s, int) and s == 0):
                    finish(s, r)
                dve.wait_ge(masked, NCH * (s + 1))
                nc.vector.tensor_reduce(k.nmax[r % 2][:], k.mx[:], AX.X, ALU.max, negate=True).then_inc(neg_max, 1)
                dve.wait_ge(neg_max, s + 1)
                if mode == PRUNE and not (isinstance(s, int) and s == 0):
                    finish(s, r)
            steps(dve, step, RING_B, NB + 1, peel=2, tail=1)
            if mode == ATTENTION:
                dve.wait_ge(rz_ready, NB)


class Across:

    def __init__(self, k, tag, op, banks):
        self.k, self.op, self.banks = k, op, banks
        self.column, self.row = k.sem(f"{tag}_column"), k.sem(f"{tag}_row")
        self.one, self.spread, self.out = k.sem(f"{tag}_one"), k.sem(f"{tag}_spread"), k.sem(f"{tag}_out")

    def tensor(self, pe, column):
        k, nc = self.k, self.k.nc
        pe.wait_ge(self.column, 1)
        nc.tensor.transpose(k.bank(self.banks[0], P, rows=slice(0, 1)), column[:], k.ident[:]).then_inc(self.row, 1)
        pe.wait_ge(self.one, 1)
        nc.tensor.matmul(k.bank(self.banks[1], 1), k.ones_row[:], k.row1[0:1, 0:1], start=True, stop=True)\
            .then_inc(self.spread, 1)

    def vector(self, dve, out, sign=1.0):
        k, nc = self.k, self.k.nc
        dve.wait_ge(self.row, 1)
        nc.vector.tensor_reduce(k.row1[0:1, 0:1], k.bank(self.banks[0], P, rows=slice(0, 1)), AX.X, self.op)\
            .then_inc(self.one, 1)
        dve.wait_ge(self.spread, 1)
        nc.vector.tensor_scalar(out[:], k.bank(self.banks[1], 1), sign, None, ALU.mult).then_inc(self.out, 1)
        dve.wait_ge(self.out, 1)


def component_mask(k, tag, layer):
    nc = k.nc
    own, out, moved = k.sem(f"{tag}_own"), k.sem(f"{tag}_colsum_out"), k.sem(f"{tag}_colsum_moved")
    turned, var, root = k.sem(f"{tag}_colsum_turned"), k.sem(f"{tag}_squares"), k.sem(f"{tag}_roots")
    exped = k.sem(f"{tag}_exped")
    top = Across(k, f"{tag}_max", ALU.max, (1, 2))
    total = Across(k, f"{tag}_total", ALU.add, (3, 4))
    xn_ready, xn_turned = k.sem(f"{tag}_xn"), k.sem(f"{tag}_xn_turned")
    hi_done, lo_done = k.sem(f"{tag}_hi"), k.sem(f"{tag}_lo")
    groups = NB // PER
    with nc.Block() as block:
        @block.sync
        def _(sp):
            sp.wait_ge(out, 4)
            for q in range(NQ):
                src = k.colsum[32 * (q % 4):32 * (q % 4) + 1, q // 4 * BANK:(q // 4 + 1) * BANK]
                sp.dma_start(k.colsum_rows[PER * q:PER * (q + 1), :], src.rearrange("p (m c) -> p m c", m=PER))\
                  .then_inc(moved, 16)

        @block.scalar
        def _(act):
            for h in range(4):
                cols = BANK * (3 if h < 2 else 2)
                nc.scalar.activation(k.colsum[32 * h:32 * h + 1, 0:cols], k.bank(4, cols, rows=slice(32 * h, 32 * h + 1)),
                                     ACT.Copy).then_inc(out, 1)
            act.wait_ge(var, 1)
            nc.scalar.activation(k.rows2[:], k.rows[:], ACT.Sqrt).then_inc(root, 1)
            act.wait_ge(var, 2)
            nc.scalar.activation(k.rows2[:], k.rows[:], ACT.Sqrt).then_inc(root, 1)
            act.wait_ge(top.out, 1)
            nc.scalar.activation(k.rows3[:], k.rows[:], ACT.Exp, bias=k.one[1][:], accum_out=k.one[0][:]).then_inc(total.column, 1)
            for g in range(groups):
                act.wait_ge(xn_turned, g + 1)
                nc.scalar.activation(k.mov_hi[:, g * BANK:(g + 1) * BANK], k.bank(6 + g % 2), ACT.Copy).then_inc(hi_done, 1)

        @block.tensor
        def _(pe):
            pe.wait_ge(moved, NQ * 16)
            nc.tensor.transpose(k.bank(0, NB), k.colsum_rows[:], k.ident[0:NB, 0:NB]).then_inc(turned, 1)
            top.tensor(pe, k.one[0])
            total.tensor(pe, k.one[0])
            for g in range(groups):
                pe.wait_ge(xn_ready, g + 1)
                at_least(pe, lo_done, g - 1)
                for m in range(PER):
                    done = nc.tensor.transpose(k.bank(6 + g % 2, P, m * P), k.xn4[g % 2][:, m].rearrange("p t d -> p (t d)"),
                                               k.ident[:])
                done.then_inc(xn_turned, 1)

        @block.vector
        def _(dve):
            link = Chain(dve, own)

            def norms(squares, n):
                link(nc.vector.tensor_scalar(k.rows[:], squares, NORM_MIN, None, ALU.max))
                nc.vector.tensor_copy(k.conn[:], k.rows[:]).then_inc(var, 1)
                dve.wait_ge(var, n)
                dve.wait_ge(root, n)
                inv_sqrt(nc, link, k.rows2[:], k.rows[:], k.rows2[:], k.rows3[:])
                link(nc.vector.tensor_tensor(k.rows3[:], k.rows2[:], k.rows[:], ALU.mult))

            link(nc.vector.tensor_tensor(k.n_sq[:], k.n1[:], k.n1[:], ALU.mult))
            link(nc.vector.reduce_sum(k.sq_n[:], k.n_sq[:], AX.X))
            norms(k.ssq_xw[:], 1)
            link(nc.vector.tensor_copy(k.structural[:], k.rows3[:]))
            norms(k.sq_n[:], 2)
            link(nc.vector.tensor_copy(k.feat_mag[:], k.rows3[:]))
            link(nc.vector.tensor_scalar(k.rows3[:], k.rows3[:], 1e-8, None, ALU.max))
            link(nc.vector.reciprocal(k.rz[:], k.rows3[:]))
            dve.wait_ge(turned, 1)
            link(nc.vector.tensor_scalar(k.rows[:], k.bank(0, NB), 0.5 / N, None, ALU.mult))
            link(nc.vector.tensor_scalar(k.rows2[:], k.structural[:], 0.5, None, ALU.mult))
            link(nc.vector.tensor_tensor(k.rows[:], k.rows[:], k.rows2[:], ALU.add))
            nc.vector.reduce_max(k.one[0][:], k.rows[:], AX.X).then_inc(top.column, 1)
            top.vector(dve, k.one[1], -1.0)
            total.vector(dve, k.one[2])
            link(nc.vector.reciprocal(k.one[3][:], k.one[2][:]))
            link(nc.vector.tensor_scalar(k.comp_mask[:], k.rows3[:], k.one[3][:], THRESHOLDS[layer], ALU.mult, ALU.is_ge))
            link(nc.vector.tensor_tensor(k.rows[:], k.comp_mask[:], k.rz[:], ALU.mult))
            link(nc.vector.tensor_tensor(k.feat_mag[:], k.comp_mask[:], k.feat_mag[:], ALU.mult))
            link(nc.vector.tensor_scalar(k.feat_mag[:], k.feat_mag[:], 1e-8, None, ALU.max))
            for g in range(groups + 1):
                if g < groups:
                    b = slice(g * PER, (g + 1) * PER)
                    shape = [P, PER, 2, D]
                    at_least(dve, xn_turned, g - 1)
                    nc.vector.tensor_tensor(k.xn4[g % 2][:], k.n1[:, b, :].unsqueeze(2).to_broadcast(shape),
                                            k.rows[:, b].unsqueeze(2).unsqueeze(3).to_broadcast(shape), ALU.mult).then_inc(xn_ready, 1)
                if g >= 1:
                    f = g - 1
                    cols = slice(f * BANK, (f + 1) * BANK)
                    dve.wait_ge(hi_done, f + 1)
                    nc.vector.tensor_tensor(k.mov_lo[:, cols], k.bank(6 + f % 2), k.mov_hi[:, cols].bitcast(FP32),
                                            ALU.subtract).then_inc(lo_done, 1)


def any_edge(k, tag, layer):
    nc = k.nc
    own, ready = k.sem(f"{tag}_own"), k.sem(f"{tag}_ready")
    top = Across(k, tag, ALU.max, (0, 1))
    with nc.Block() as block:
        @block.vector
        def _(dve):
            link = Chain(dve, own)
            link(nc.vector.reciprocal(k.rz[:], k.z[:]))
            link(nc.vector.tensor_tensor(k.rows[:], k.rz[:], k.comp_mask[:], ALU.mult))
            nc.vector.reduce_max(k.one[0][:], k.rows[:], AX.X).then_inc(top.column, 1)
            top.vector(dve, k.one[1])
            link(nc.vector.tensor_scalar(k.flag[:], k.one[1][0:1, :], THRESHOLDS[layer] * 0.999, None, ALU.is_ge))

        @block.tensor
        def _(pe):
            top.tensor(pe, k.one[0])



def rows_times(k, tag, src, weights, bank, cols, consume, before=None, scalar_before=None):
    nc = k.nc
    ready, turned, copied = k.sem(f"{tag}_ready"), k.sem(f"{tag}_turned"), k.sem(f"{tag}_copied")
    product, consumed = k.sem(f"{tag}_product"), k.sem(f"{tag}_consumed")
    groups = NB // PER
    with nc.Block() as block:
        @block.scalar
        def _(act):
            if scalar_before is not None:
                scalar_before(act)
            for g in range(groups):
                act.wait_ge(turned, g + 1)
                at_least(act, product, g - 1)
                nc.scalar.activation(k.n_t4[g % 2][:], k.bank(g % 2, rows=slice(0, D)), ACT.Copy).then_inc(copied, 1)

        @block.tensor
        def _(pe):
            pe.wait_ge(ready, 1)
            for g in range(groups + 1):
                if g < groups:
                    at_least(pe, copied, g - 1)
                    for m in range(PER):
                        done = nc.tensor.transpose(k.bank(g % 2, P, m * P, slice(0, D)), src[:, g * PER + m, :], k.ident[:])
                    done.then_inc(turned, 1)
                if g >= 1:
                    f = g - 1
                    pe.wait_ge(copied, f + 1)
                    at_least(pe, consumed, f - 1)
                    for m in range(PER):
                        done = nc.tensor.matmul(k.bank(bank + f % 2, cols, m * cols), k.n_t4[f % 2][:, m * P:(m + 1) * P],
                                                weights, start=True, stop=True)
                    done.then_inc(product, 1)

        @block.vector
        def _(dve):
            if before is not None:
                before(dve)
            nc.vector.tensor_copy(k.one[0][:], k.ones[:]).then_inc(ready, 1)
            for g in range(groups):
                dve.wait_ge(product, g + 1)
                view = k.bank(bank + g % 2, PER * cols).rearrange("p (m c) -> p m c", m=PER)
                consume(dve, g, view).then_inc(consumed, 1)
            dve.wait_ge(consumed, groups)


def values(k, tag):
    nc, i = k.nc, k.i
    weights, own = k.sem(f"{tag}_weights"), k.sem(f"{tag}_own")
    with nc.Block() as block:
        @block.sync
        def _(sp):
            for dst, src in ((k.g_w[:, 0:D], i["Wv"]), (k.g_w[:, D:2 * D], i["W"]),
                             (k.g_b[:], i["bv"].partition_broadcast(P))):
                sp.dma_start(dst, src).then_inc(weights, 16)
            sp.wait_ge(weights, 48)
    state = {}

    def before(dve):
        state["link"] = Chain(dve, own)

    def consume(dve, g, view):
        link, b = state["link"], slice(g * PER, (g + 1) * PER)
        link(nc.vector.tensor_tensor(k.tall[:, b, :], view[:, :, 0:D], k.g_b[:].unsqueeze(1).to_broadcast([P, PER, D]),
                                     ALU.add))
        link(nc.vector.tensor_copy(k.g_xw[:], view[:, :, D:2 * D]))
        link(nc.vector.tensor_tensor(k.g_xw[:], k.g_xw[:], k.g_xw[:], ALU.mult))
        link(nc.vector.reduce_sum(k.ssq_xw[:, b], k.g_xw[:], AX.X))
        return nc.vector.tensor_copy(k.one[0][:], k.ones[:])

    rows_times(k, tag, k.n1, k.g_w[:], 2, 2 * D, consume, before)


def node_operand(k, tag, layer):
    nc, i = k.nc, k.i
    weights, own = k.sem(f"{tag}_weights"), k.sem(f"{tag}_own")
    var, root = k.sem(f"{tag}_degrees"), k.sem(f"{tag}_roots")
    top = Across(k, f"{tag}_max", ALU.max, (4, 5))
    total = Across(k, f"{tag}_total", ALU.add, (6, 7))
    with nc.Block() as block:
        @block.sync
        def _(sp):
            sp.dma_start(k.g_w[:, 0:D], i["W"]).then_inc(weights, 16)
            sp.wait_ge(weights, 16)

        @block.tensor
        def _(pe):
            top.tensor(pe, k.one[0])
            total.tensor(pe, k.one[0])

        @block.scalar
        def _(act):
            act.wait_ge(top.out, 1)
            nc.scalar.activation(k.rows3[:], k.rows[:], ACT.Exp, bias=k.one[1][:], accum_out=k.one[0][:])\
              .then_inc(total.column, 1)
            act.wait_ge(var, 1)
            nc.scalar.activation(k.structural[:], k.z[:], ACT.Sqrt).then_inc(root, 1)

        @block.vector
        def _(dve):
            link = Chain(dve, own)
            link(nc.vector.tensor_tensor(k.rows[:], k.conn[:], k.feat_mag[:], ALU.mult))
            nc.vector.reduce_max(k.one[0][:], k.rows[:], AX.X).then_inc(top.column, 1)
            top.vector(dve, k.one[1], -1.0)
            link(nc.vector.tensor_scalar(k.z[:], k.conn[:], EPS, None, ALU.max))
            nc.vector.tensor_copy(k.mx[:, 0:1], k.z[:, 0:1]).then_inc(var, 1)
            total.vector(dve, k.one[2])
            dve.wait_ge(root, 1)
            inv_sqrt(nc, link, k.structural[:], k.z[:], k.structural[:], k.rows2[:])
            link(nc.vector.reciprocal(k.one[3][:], k.one[2][:]))
            link(nc.vector.tensor_scalar(k.rows3[:], k.rows3[:], k.one[3][:], THRESHOLDS[layer], ALU.mult, ALU.is_ge))
            link(nc.vector.tensor_tensor(k.rows3[:], k.rows3[:], k.comp_mask[:], ALU.mult))
            link(nc.vector.tensor_scalar(k.rows[:], k.conn[:], 0.0, None, ALU.is_gt))
            link(nc.vector.tensor_tensor(k.rows3[:], k.rows3[:], k.rows[:], ALU.mult))
            link(nc.vector.tensor_tensor(k.h[:], k.n1[:], k.rows3[:].unsqueeze(2).to_broadcast([P, NB, D]), ALU.mult))

    def consume(dve, g, view):
        b = slice(g * PER, (g + 1) * PER)
        return nc.vector.tensor_tensor(k.tall[:, b, :], view, k.structural[:, b].unsqueeze(2).to_broadcast([P, PER, D]),
                                       ALU.mult)

    rows_times(k, f"{tag}_w", k.h, k.g_w[:, 0:D], 2, D, consume)


def edge_degrees(k, tag):
    nc = k.nc
    out, moved, turned, own = k.sem(f"{tag}_out"), k.sem(f"{tag}_moved"), k.sem(f"{tag}_turned"), k.sem(f"{tag}_own")
    with nc.Block() as block:
        @block.scalar
        def _(act):
            for h in range(4):
                cols = BANK * (3 if h < 2 else 2)
                nc.scalar.activation(k.colsum[32 * h:32 * h + 1, 0:cols], k.bank(5, cols, rows=slice(32 * h, 32 * h + 1)),
                                     ACT.Copy).then_inc(out, 1)

        @block.sync
        def _(sp):
            sp.wait_ge(out, 4)
            for q in range(NQ):
                src = k.colsum[32 * (q % 4):32 * (q % 4) + 1, q // 4 * BANK:(q // 4 + 1) * BANK]
                sp.dma_start(k.colsum_rows[PER * q:PER * (q + 1), :], src.rearrange("p (m c) -> p m c", m=PER))\
                  .then_inc(moved, 16)

        @block.tensor
        def _(pe):
            pe.wait_ge(moved, NQ * 16)
            nc.tensor.transpose(k.bank(5, NB), k.colsum_rows[:], k.ident[0:NB, 0:NB]).then_inc(turned, 1)

        @block.vector
        def _(dve):
            link = Chain(dve, own)
            dve.wait_ge(turned, 1)
            link(nc.vector.tensor_scalar(k.rows[:], k.bank(5, NB), EPS, None, ALU.max))
            link(nc.vector.reciprocal(k.rz[:], k.rows[:]))


def row_pass(k, tag):
    nc = k.nc
    loaded, used = k.sem_list(f"{tag}_loaded", RING_B), k.sem(f"{tag}_used")
    turned, copied, read = k.sem(f"{tag}_turned"), k.sem(f"{tag}_copied"), k.sem(f"{tag}_read")
    with nc.Block() as block:
        @block.sync
        def _(sp):
            load_ring(k, sp, k.hp_v, loaded, used, RING_B, True, True)

        @block.scalar
        def _(act):
            def step(s, r, turn):
                for q in range(NQ):
                    act.wait_ge(turned, NQ * s + q + 1)
                    nc.scalar.activation(k.adj_t[q % 4][:], k.bank(q % 4), ACT.Copy).then_inc(copied, 1)
            steps(act, step, RING_B, NB)

        @block.vector
        def _(dve):
            def step(s, r, turn):
                wait_alone(dve, used, s + 1, k.constants)
                b = NB - 1 - s
                nc.vector.tensor_copy(k.g_dv[:], columns(k.structural, b, 1)).then_inc(read, 1)
                wait_alone(dve, read, 2 * s + 1, k.constants)
                nc.vector.tensor_scalar(block_of(k.msg, b), k.bank(6 + r % 2, D), k.g_dv[:], None, ALU.mult)\
                  .then_inc(read, 1)
                dve.wait_ge(read, 2 * s + 2)
            steps(dve, step, RING_B, NB)

        @block.tensor
        def _(pe):
            def step(s, r, turn):
                wait_loaded(pe, loaded, r, turn, True)
                rows = k.ring[slot_of(r, RING_B, True)]
                at_least(pe, read, 2 * s - 2)
                for q in range(NQ + 2):
                    if q < NQ:
                        at_least(pe, copied, NQ * s + q - 3)
                        for m in range(PER):
                            c = q * BANK + m * P
                            done = nc.tensor.transpose(k.bank(q % 4, P, m * P), rows[:, c:c + P], k.ident[:])
                        done.then_inc(turned, 1)
                    if q >= 2:
                        f = q - 2
                        pe.wait_ge(copied, NQ * s + f + 1)
                        for m in range(PER):
                            done = nc.tensor.matmul(k.bank(6 + r % 2, D), k.adj_t[f % 4][:, m * P:(m + 1) * P],
                                                    k.tall[:, f * PER + m, :], start=f == 0 and m == 0,
                                                    stop=f == NQ - 1 and m == PER - 1)
                done.then_inc(used, 1)
            steps(pe, step, RING_B, NB)


def remaining_edges(k, tag, layer):
    nc = k.nc
    score_pass(k, f"{tag}_prune", PRUNE, down=False, resident=True, threshold=THRESHOLDS[layer])
    node_operand(k, f"{tag}_node", layer)
    column_pass(k, f"{tag}_agg", k.hp_v, k.tall, RING_B, degrees=True)
    edge_degrees(k, f"{tag}_deg")
    by_blocks(k, f"{tag}_agg", k.wide, k.tall, k.rz)
    row_pass(k, f"{tag}_msg")
    own = k.sem(f"{tag}_out_own")
    state = {}

    def before(dve):
        state["link"] = Chain(dve, own)

    def consume(dve, g, view):
        b = slice(g * PER, (g + 1) * PER)
        if layer == 0:
            return nc.vector.tensor_scalar(k.n1[:, b, :], view, 0.0, None, ALU.max)
        state["link"](nc.vector.tensor_scalar(k.tall[:, b, :], view, 0.0, None, ALU.max))
        return nc.vector.tensor_tensor(k.x1[:, b, :], k.x1[:, b, :], k.tall[:, b, :], ALU.add)

    rows_times(k, f"{tag}_out", k.msg, k.theta[:], 2, D, consume, before)


def program(nc, ins, out):
    k = Kernel(nc, ins, out)
    embed_and_columns(k)
    network_and_features(k)
    attention_operands(k, "att")
    score_pass(k, "att", ATTENTION, down=False, resident=True)
    component_mask(k, "comp", 0)
    stored = k.sem("x1_stored")

    def store(sp):
        sp.dma_start(k.out_v, k.x1[:]).then_inc(stored, 16)
    score_pass(k, "edge", EDGES, down=True, resident=True, first_sync=store)
    any_edge(k, "flag", 0)
    with nc.Block() as block:
        @block.sync
        def _(sp):
            sp.wait_ge(stored, 16)
    edges_left = nc.values_load(k.flag[0:1, 0:1], min_val=0, max_val=1)
    with nc.If(edges_left > 0):
        k.fresh_semaphores()
        remaining_edges(k, "l0", 0)
        k.fresh_semaphores()
        values(k, "l1_v")
        column_pass(k, "l1_edge", k.adj_v, k.tall, RING_B)
        attention_operands(k, "l1_att")
        score_pass(k, "l1_att", ATTENTION, down=True, resident=True)
        component_mask(k, "l1_comp", 1)
        k.fresh_semaphores()
        with nc.Block() as block:
            @block.sync
            def _(sp):
                again = k.sem("l1_first_rows")
                for b in range(RING_B):
                    sp.dma_start(k.ring[b][:], k.adj_v[b]).then_inc(again, 16)
                sp.wait_ge(again, 16 * RING_B)
        remaining_edges(k, "l1", 1)
        result = k.sem("result_stored")
        with nc.Block() as block:
            @block.sync
            def _(sp):
                sp.dma_start(k.out_v, k.x1[:]).then_inc(result, 16)
                sp.wait_ge(result, 16)


_INS = {'x': 'x', 'adj': 'adj', 'L0_gnn_W_u': 'W_u', 'L0_gnn_diag_u': 'diag_u', 'L0_gnn_par_u': 'par_u',
        'L0_gnn_W_i': 'W_i', 'L0_gnn_diag_i': 'diag_i', 'L0_gnn_par_i': 'par_i', 'L0_gnn_ln_gamma': 'ln_gamma',
        'L0_gnn_ln_beta': 'ln_beta', 'L1_gnn_W': 'W', 'L1_gnn_Theta': 'Theta', 'L1_gnn_Wq': 'Wq',
        'L1_gnn_bq': 'bq', 'L1_gnn_Wv': 'Wv', 'L1_gnn_bv': 'bv'}


def kernel(**inputs):
    import numpy as _np
    import concourse.bacc as _bacc
    from concourse import mybir as _mybir
    from concourse.bass_utils import run_bass_kernel_spmd as _run

    nc = _bacc.Bacc("TRN2", target_bir_lowering=False, num_devices=1)
    arrays, ins = {}, {}
    for name, short in _INS.items():
        a = _np.ascontiguousarray(inputs[name])
        arrays[f"in_{name}_dram"] = a
        ins[short] = nc.dram_tensor(f"in_{name}_dram", a.shape, _mybir.dt.from_np(a.dtype), kind="ExternalInput").ap()
    out = nc.dram_tensor("out_0_dram", (5120, 64), _mybir.dt.float32, kind="ExternalOutput").ap()
    program(nc, ins, out)
    r = _run(nc, [arrays], core_ids=[0])
    return r.results[0]["out_0_dram"]
```

```python
import concourse.bass as bass
from concourse import mybir

FP32 = mybir.dt.float32
FP32R = mybir.dt.float32r
INT32 = mybir.dt.int32
ALU = mybir.AluOpType
ACT = mybir.ActivationFunctionType
AX = mybir.AxisListType

P = 128
N = 5120
D = 64
NB = N // P
NU = 2048
UB = NU // P
BANK = 512
NQ = N // BANK
PER = BANK // P
CH = 2 * BANK
NCH = N // CH
RING_A = 6
RING_B = 4
PAIRS = NB // 2
PAIR_SLOTS = RING_A // 2
TGS = NB // 2
T_BUFS = 5
HALF = 4 * N // 2
LN_EPS = 1e-5
EPS = 1e-6
NORM_MIN = 1e-16
THRESHOLDS = (0.000244, 0.000244 + (1.0 - 0.9048374180359595) * (0.0003 - 0.000244))
LOWEST = -3.0e38


def at_least(eng, sem, value):
    if not (isinstance(value, int) and value <= 0):
        eng.wait_ge(sem, value)


def wait_alone(eng, sem, value, other):
    if not isinstance(value, int):
        value = eng.to_reg(value)
        eng.wait_ge(other, 1)
    at_least(eng, sem, value)


class Chain:

    def __init__(self, eng, sem):
        self.eng, self.sem, self.base, self.n = eng, sem, 0, 0

    def restart(self, base):
        self.base, self.n = base, 0

    def __call__(self, ins, other=None):
        self.n += 1
        ins.then_inc(self.sem, 1)
        if other is None:
            self.eng.wait_ge(self.sem, self.base + self.n)
        else:
            wait_alone(self.eng, self.sem, self.base + self.n, other)


def steps(eng, body, unroll, count, peel=None, tail=0):
    peel = unroll if peel is None else peel
    loops = (count - peel - tail) // unroll
    for s in range(peel):
        body(s, s % unroll, s // unroll)
    with eng.Fori(0, loops) as it:
        for r in range(peel, peel + unroll):
            body(it * unroll + r, r % unroll, it + r // unroll)
    for s in range(peel + loops * unroll, count):
        body(s, s % unroll, s // unroll)


def block_of(tensor, b):
    return tensor[:, b, :] if isinstance(b, int) else tensor[:, bass.ds(b, 1), :].rearrange("p a d -> p (a d)")


def columns(tensor, first, size):
    return tensor[:, first:first + size] if isinstance(first, int) else tensor[:, bass.ds(first, size)]


def newton(nc, link, y, v, tmp):
    link(nc.vector.tensor_tensor(tmp, v, y, ALU.mult))
    link(nc.vector.tensor_tensor(tmp, tmp, y, ALU.mult))
    link(nc.vector.tensor_scalar(tmp, tmp, -0.5, 1.5, ALU.mult, ALU.add))
    link(nc.vector.tensor_tensor(y, y, tmp, ALU.mult))


def inv_sqrt(nc, link, out, v, sd, tmp):
    link(nc.vector.reciprocal(out, sd))
    newton(nc, link, out, v, tmp)


class Memory:

    def __init__(self, nc):
        self.nc, self.end = nc, -(-nc.sbuf_base // 32) * 32

    def at(self, name, offset, shape, dt=FP32):
        return self.nc.alloc_sbuf_tensor_at(name, shape, dt, offset=offset)

    def take(self, size):
        offset, self.end = self.end, self.end + -(-size // 32) * 32
        assert self.end <= self.nc.sbuf_usable_end, self.end
        return offset

    def new(self, name, shape, dt=FP32):
        size = 4
        for n in shape[1:]:
            size *= n
        return self.at(name, self.take(size), shape, dt)


class Kernel:

    def __init__(self, nc, ins, out):
        self.nc, self.i = nc, ins
        self.sems, self.spare = {}, []
        self.x_v = ins["x"].rearrange("(b p) d -> p b d", p=P)
        self.out_v = out.rearrange("(b p) d -> p b d", p=P)
        self.adj_v = ins["adj"].rearrange("(b p) n -> b p n", p=P)
        self.hp_v = nc.dram_tensor("pruned", (N, N), FP32).ap().rearrange("(b p) n -> b p n", p=P)
        m = Memory(nc)
        region = [m.take(4 * N) for _ in range(9)]
        self.ring = [m.at(f"ring{r}", region[r], [P, N]) for r in range(RING_A)]
        self.work = [m.at(f"work{r}", region[4 + r], [P, N]) for r in range(2)]
        self.stat_op = m.at("stat_op", region[6], [P, N], FP32R)
        self.mov_hi = m.at("mov_hi", region[7], [P, N], FP32R)
        self.mov_lo = m.at("mov_lo", region[8], [P, N], FP32R)
        self.colsum = m.at("colsum", region[6], [P, 3 * BANK])
        self.colsum_rows = m.at("colsum_rows", region[6] + 12 * BANK, [NB, P])
        self.n_sq = m.at("n_sq", region[6] + 12 * BANK + 4 * P, [P, NB, D])
        self.xn4 = [m.at(f"xn4{r}", region[6] + (12 + 4 * r) * BANK + 4 * P, [P, PER, 2, D]) for r in range(2)]
        self.n_t2 = m.at("n_t2", region[6] + (NQ - 1) * 4 * BANK, [P, BANK])
        self.features_t = m.at("features_t", region[8] + HALF, [P, N // 2])
        self.wide = m.at("wide", region[5], [P, N // 2])
        self.tall = m.at("tall", region[5] + HALF, [P, NB, D])
        self.h = m.at("h", region[6], [P, NB, D])
        self.emb = m.at("emb", region[6] + HALF, [P, NB, D])
        self.xin = m.at("xin", region[7], [P, NB, D])
        self.xc = m.at("xc", region[7] + HALF, [P, NB, D])
        self.sq = m.at("sq", region[8], [P, NB, D])
        self.col_t = m.at("col_t", region[7], [P, N // 2])
        self.col = m.at("col", region[7] + HALF, [P, NB, D])
        self.adj_t = [m.at(f"adj_t{g}", region[6] + g * 4 * BANK, [P, BANK]) for g in range(T_BUFS)]
        o = region[8] + HALF
        self.h_t = [m.at(f"h_t{r}", o + r * 4 * BANK, [D, BANK]) for r in range(2)]
        self.diag_rows = m.at("diag_rows", o + 8 * BANK, [NB, P])
        self.w_ui = [m.at(f"w_{c}", o + 8 * BANK + 4 * P + j * 4 * D, [D, D]) for j, c in enumerate("ui")]
        self.beta = m.at("beta", o + 8 * BANK + 4 * P + 8 * D, [P, D])
        o = region[8]
        self.w_vw = m.at("w_vw", o, [P, 2, 2 * D])
        self.vw = m.at("vw", o + 1024, [P, 2, 2 * D])
        self.h2_t = m.at("h2_t", o + 2560, [P, 2 * P])
        self.n_t = m.at("n_t", o + 3584, [P, P])
        self.ln_in = m.at("ln_in", o + 4096, [P, 2, D])
        self.ln_out = m.at("ln_out", o + 4608, [P, 2, D])
        self.xw_sq = m.at("xw_sq", o + 5120, [P, D])
        self.gamma = m.at("gamma", o + 5376, [P, D])
        self.b_vw = m.at("b_vw", o + 5632, [P, 2 * D])
        self.n_t4 = [m.at(f"n_t4{r}", region[4] + r * 4 * BANK, [D, BANK]) for r in range(2)]
        self.msg = m.at("msg", region[8], [P, NB, D])
        self.g_w = m.at("g_w", region[4] + 24 * BANK, [D, 2 * D])
        self.g_b = m.at("g_b", region[4] + 24 * BANK + 8 * D, [P, D])
        self.g_xw = m.at("g_xw", region[4] + 24 * BANK + 12 * D, [P, PER, D])
        self.g_dv = m.at("g_dv", region[4] + 24 * BANK + 28 * D, [P, 1])
        self.x1 = m.new("x1", [P, NB, D])
        self.n1 = m.new("n1", [P, NB, D])
        self.ident = m.new("ident", [P, P])
        self.sel = m.new("sel", [P, P])
        self.stat_blk = [m.new(f"stat_blk{r}", [P, P], FP32R) for r in range(2)]
        self.e_blk = [m.new(f"e_blk{r}", [P, D]) for r in range(2)]
        self.w_q2 = m.new("w_q2", [P, 2 * D])
        self.b_q2 = m.new("b_q2", [P, 1])
        self.b_q8 = m.new("b_q8", [P, 1])
        self.ones = m.new("ones", [P, 1])
        self.ssq_xw = m.new("ssq_xw", [P, NB])
        self.feat_mag = m.new("feat_mag", [P, NB])
        self.structural = m.new("structural", [P, NB])
        self.rows = m.new("rows", [P, NB])
        self.rows2 = m.new("rows2", [P, NB])
        self.rows3 = m.new("rows3", [P, NB])
        self.comp_mask = m.new("comp_mask", [P, NB])
        self.sq_n = m.new("sq_n", [P, NB])
        self.z = m.new("z", [P, NB])
        self.rz = m.new("rz", [P, NB])
        self.conn = m.new("conn", [P, NB])
        self.par = m.new("par", [P, 4])
        self.parp = m.new("parp", [P, 2])
        self.bn = [m.new(f"bn{j}", [P, 6]) for j in range(2)]
        self.mv = m.new("mv", [P, 2, 2])
        self.pair = [m.new(f"pair{j}", [P, 2, 1]) for j in range(3)]
        self.one = [m.new(f"one{j}", [P, 1]) for j in range(4)]
        self.mx = m.new("mx", [P, NCH])
        self.nmax = [m.new(f"nmax{r}", [P, 1]) for r in range(2)]
        self.rz_blk = [m.new(f"rz_blk{r}", [P, 1]) for r in range(2)]
        self.row1 = m.new("row1", [1, P])
        self.ones_row = m.new("ones_row", [1, P])
        self.theta = m.new("theta", [D, D])
        self.flag = m.new("flag", [1, 1], INT32)
        self.ps = nc.alloc_psum_tensor("ps", [P, 8 * BANK], FP32)
        self.constants = self.sem("constants")

    def sem(self, name):
        assert name not in self.sems, name
        self.sems[name] = self.spare.pop(0) if self.spare else self.nc.alloc_semaphore(name)
        return self.sems[name]

    def fresh_semaphores(self):
        used = {sem.num: sem for name, sem in self.sems.items() if name != "constants"}
        with self.nc.Block() as block:
            @block.gpsimd
            def _(pool):
                first = min(used)
                for n in range(min(used), max(used) + 1):
                    if n + 1 not in used:
                        pool.sem_clear(range(first, n + 1))
                        first = n + 2

            for engine in (block.sync, block.scalar, block.vector, block.tensor):
                @engine
                def _(eng):
                    eng.wait_ge(self.constants, 1)
        self.sems = {"constants": self.constants}
        self.spare = [used[n] for n in sorted(used)]

    def sem_list(self, name, n):
        return [self.sem(f"{name}{j}") for j in range(n)]

    def bank(self, b, cols=BANK, first=0, rows=slice(0, P)):
        return self.ps[rows, b * BANK + first:b * BANK + first + cols]

    def half_acc(self, q, cols=BANK, first=0):
        return self.bank(q // 2, cols, first, slice(D * (q % 2), D * (q % 2) + D))


def load_ring(k, eng, src, loaded, used, ring, down, resident, per=1):
    def load(s, r, turn):
        if isinstance(s, int) and s < ring:
            if resident:
                return
        else:
            wait_alone(eng, used, (s - ring + 1) * per, k.constants)
        b = NB - 1 - s if down else s
        blk = src[b] if isinstance(b, int) else src[bass.ds(b, 1), :, :].rearrange("a p n -> (a p) n")
        eng.dma_start(k.ring[slot_of(r, ring, down)][:], blk).then_inc(loaded[r], 16)
    steps(eng, load, ring, NB)


def slot_of(r, ring, down):
    return (NB - 1 - r if down else r) % ring


def wait_loaded(eng, loaded, r, turn, resident):
    at_least(eng, loaded[r], 16 * turn + (0 if resident else 16))


def column_pass(k, tag, src, operand, ring, down=False, resident=False, degrees=False,
                first=None, last=None):
    nc = k.nc
    loaded, used = k.sem_list(f"{tag}_loaded", ring), k.sem(f"{tag}_used")
    placed = k.sem(f"{tag}_operand_placed")
    first, last = first or {}, last or {}
    with nc.Block() as block:
        @block.sync
        def _(sp):
            if "sync" in first:
                first["sync"](sp)
            load_ring(k, sp, src, loaded, used, ring, down, resident)

        @block.gpsimd
        def _(pool):
            if "gpsimd" in first:
                first["gpsimd"](pool)

        @block.scalar
        def _(act):
            if "scalar" in first:
                first["scalar"](act)

            def place(s, r, turn):
                if not (isinstance(s, int) and s < 2):
                    act.wait_ge(used, s - 1)
                nc.scalar.activation(k.e_blk[r % 2][:], block_of(operand, NB - 1 - s if down else s),
                                     ACT.Copy).then_inc(placed, 1)
            steps(act, place, ring, NB)
            if "scalar" in last:
                act.wait_ge(used, NB)
                last["scalar"](act)

        @block.vector
        def _(dve):
            if "vector" in first:
                first["vector"](dve)
            if "vector" in last:
                dve.wait_ge(used, NB)
                last["vector"](dve)

        @block.tensor
        def _(pe):
            if "tensor" in first:
                first["tensor"](pe)

            def product(s, r, turn):
                pe.wait_ge(placed, s + 1)
                wait_loaded(pe, loaded, r, turn, resident)
                rows = k.ring[slot_of(r, ring, down)]
                begin = isinstance(s, int) and s == 0
                for q in range(NQ):
                    done = nc.tensor.matmul(k.half_acc(q), k.e_blk[r % 2][:], rows[:, q * BANK:(q + 1) * BANK],
                                            start=begin, stop=True, skip_group_check=True)
                if degrees:
                    for q in range(NQ):
                        done = nc.tensor.matmul(k.bank(5 + q // 4, rows=slice(32 * (q % 4), 32 * (q % 4) + 1)),
                                                k.ones[:], rows[:, q * BANK:(q + 1) * BANK],
                                                start=begin, stop=True, skip_group_check=True)
                done.then_inc(used, 1)
            steps(pe, product, ring, NB)
            if "tensor" in last:
                last["tensor"](pe)


def by_blocks(k, tag, wide, tall, scale=None):
    nc = k.nc
    out, turned, read = k.sem(f"{tag}_out"), k.sem(f"{tag}_turned"), k.sem(f"{tag}_read")
    tall_v = tall[:].rearrange("p (q h m) d -> p q h m d", h=2, m=PER)
    with nc.Block() as block:
        @block.scalar
        def _(act):
            for b in range(NQ // 2):
                nc.scalar.activation(wide[:, b * BANK:(b + 1) * BANK], k.bank(b), ACT.Copy).then_inc(out, 1)

        @block.tensor
        def _(pe):
            for b in range(NQ // 2):
                pe.wait_ge(out, b + 1)
                at_least(pe, read, b - 1)
                for m in range(PER):
                    c = b * BANK + m * P
                    done = nc.tensor.transpose(k.bank(6 + b % 2, P, m * P), wide[:, c:c + P], k.ident[:])
                done.then_inc(turned, 1)

        @block.vector
        def _(dve):
            for b in range(NQ // 2):
                dve.wait_ge(turned, b + 1)
                for h in range(2):
                    src = k.bank(6 + b % 2).rearrange("p (m h d) -> p m h d", h=2, d=D)[:, :, h, :]
                    if scale is None:
                        done = nc.vector.tensor_copy(tall_v[:, b, h], src)
                    else:
                        s = scale[:].rearrange("p (q h m) -> p q h m", h=2, m=PER)[:, b, h]
                        done = nc.vector.tensor_tensor(tall_v[:, b, h], src,
                                                       s.unsqueeze(2).to_broadcast([P, PER, D]), ALU.mult)
                done.then_inc(read, 1)
            dve.wait_ge(read, NQ // 2)



def embed_and_columns(k):
    nc, i = k.nc, k.i
    s_x, s_par = k.sem("x_loaded"), k.sem("embed_weights")
    own, pool_own = k.sem("embed_own"), k.sem("constants_own")
    ln_var, ln_sd, h_ready, const_ready = k.sem("embed_var"), k.sem("embed_sd"), k.sem("h_ready"), k.constants
    ht_done, ht_copied, hw_done, e_ready = k.sem("ht_done"), k.sem("ht_copied"), k.sem("hw_done"), k.sem("e_ready")
    diag_t = k.sem("diag_transposed")
    groups = NB // PER
    N_PAR = 7

    def sync(sp):
        sp.dma_start(k.xin[:], k.x_v).then_inc(s_x, 16)

    def gpsimd(pool):
        nc.gpsimd.memset(k.ones[:], 1.0).then_inc(const_ready, 1)
        nc.gpsimd.memset(k.ones_row[:], 1.0).then_inc(const_ready, 1)
        link = Chain(pool, pool_own)
        link(nc.gpsimd.memset(k.ident[:], 0.0))
        link(nc.gpsimd.memset(k.sel[:], 0.0))
        for tensor, base in ((k.ident, 0), (k.sel, 0), (k.sel, D), (k.sel, -D)):
            ins = nc.gpsimd.affine_select(out=tensor[:], in_=tensor[:], compare_op=ALU.not_equal, fill=1.0,
                                          base=base, pattern=[[-1, P]], channel_multiplier=1)
            link(ins)

    def scalar(act):
        for dst, src in ((k.w_ui[0][:], i["W_u"]), (k.w_ui[1][:], i["W_i"]),
                         (k.diag_rows[0:UB, :], i["diag_u"].rearrange("(b p) -> b p", p=P)),
                         (k.diag_rows[UB:NB, :], i["diag_i"].rearrange("(b p) -> b p", p=P)),
                         (k.par[:, 0:2], i["par_u"].partition_broadcast(P)),
                         (k.par[:, 2:4], i["par_i"].partition_broadcast(P)),
                         (k.beta[:], i["ln_beta"].partition_broadcast(P))):
            act.dma_start(dst, src).then_inc(s_par, 16)
        act.wait_ge(ln_var, 1)
        nc.scalar.activation(k.rows2[:], k.rows[:], ACT.Sqrt).then_inc(ln_sd, 1)
        for g in range(groups):
            act.wait_ge(ht_done, g + 1)
            at_least(act, hw_done, g - 1)
            nc.scalar.activation(k.h_t[g % 2][:], k.bank(g % 2, rows=slice(0, D)), ACT.Copy).then_inc(ht_copied, 1)

    def vector(dve):
        link = Chain(dve, own)
        whole = [P, NB, D]
        dve.wait_ge(s_x, 16)
        link(nc.vector.reduce_sum(k.rows3[:], k.xin[:], AX.X))
        link(nc.vector.tensor_scalar(k.rows3[:], k.rows3[:], 1.0 / D, None, ALU.mult))
        link(nc.vector.tensor_tensor(k.xc[:], k.xin[:], k.rows3[:].unsqueeze(2).to_broadcast(whole), ALU.subtract))
        link(nc.vector.tensor_tensor(k.sq[:], k.xc[:], k.xc[:], ALU.mult))
        link(nc.vector.reduce_sum(k.rows[:], k.sq[:], AX.X))
        nc.vector.tensor_scalar(k.rows[:], k.rows[:], 1.0 / D, LN_EPS, ALU.mult, ALU.add).then_inc(ln_var, 1)
        dve.wait_ge(ln_var, 1)
        dve.wait_ge(ln_sd, 1)
        inv_sqrt(nc, link, k.rows2[:], k.rows[:], k.rows2[:], k.rows3[:])
        link(nc.vector.tensor_tensor(k.xc[:], k.xc[:], k.rows2[:].unsqueeze(2).to_broadcast(whole), ALU.mult))
        nc.vector.tensor_scalar(k.h[:], k.xc[:], 0.0, None, ALU.max).then_inc(h_ready, 1)
        dve.wait_ge(s_par, N_PAR * 16)
        link(nc.vector.tensor_tensor(k.parp[:, 0:1], k.par[:, 0:1], k.par[:, 1:2], ALU.mult))
        link(nc.vector.tensor_tensor(k.parp[:, 1:2], k.par[:, 2:3], k.par[:, 3:4], ALU.mult))
        dve.wait_ge(diag_t, 1)
        link(nc.vector.tensor_scalar(k.rows[:, 0:UB], k.bank(6, UB), k.parp[:, 0:1], None, ALU.mult))
        link(nc.vector.tensor_scalar(k.rows[:, UB:NB], k.bank(6, NB - UB, UB), k.parp[:, 1:2], None, ALU.mult))
        for g in range(groups):
            dve.wait_ge(hw_done, g + 1)
            b = slice(g * PER, (g + 1) * PER)
            hw = k.bank(2 + g % 2, PER * D).rearrange("p (b d) -> p b d", d=D)
            link(nc.vector.tensor_tensor(k.emb[:, b, :], hw, k.rows[:, b].unsqueeze(2).to_broadcast([P, PER, D]), ALU.mult))
            nc.vector.tensor_tensor(k.emb[:, b, :], k.emb[:, b, :], k.h[:, b, :], ALU.add).then_inc(e_ready, 1)
        dve.wait_ge(h_ready, 1)
        link(nc.vector.tensor_tensor(k.x1[:], k.xin[:], k.beta[:].unsqueeze(1).to_broadcast(whole), ALU.add))
        link(nc.vector.tensor_tensor(k.x1[:], k.x1[:], k.h[:], ALU.add))

    def tensor(pe):
        pe.wait_ge(pool_own, 3)
        pe.wait_ge(s_par, N_PAR * 16)
        nc.tensor.transpose(k.bank(6, NB), k.diag_rows[:], k.ident[0:NB, 0:NB]).then_inc(diag_t, 1)
        pe.wait_ge(h_ready, 1)
        for g in range(groups + 1):
            if g < groups:
                at_least(pe, ht_copied, g - 1)
                for j in range(PER):
                    done = nc.tensor.transpose(k.bank(g % 2, P, j * P, slice(0, D)), k.h[:, g * PER + j, :], k.ident[:])
                done.then_inc(ht_done, 1)
            if g >= 1:
                f = g - 1
                pe.wait_ge(ht_copied, f + 1)
                at_least(pe, e_ready, f - 1)
                for j in range(PER):
                    w = k.w_ui[0 if f * PER + j < UB else 1]
                    done = nc.tensor.matmul(k.bank(2 + f % 2, D, j * D), k.h_t[f % 2][:, j * P:(j + 1) * P], w[:],
                                            start=True, stop=True)
                done.then_inc(hw_done, 1)
        pe.wait_ge(e_ready, groups)

    def scalar_first(act):
        scalar(act)
        act.wait_ge(e_ready, groups)

    column_pass(k, "a1", k.adj_v, k.emb, RING_A,
                first={"sync": sync, "gpsimd": gpsimd, "scalar": scalar_first, "vector": vector, "tensor": tensor})
    by_blocks(k, "col", k.col_t, k.col)


def network_and_features(k):
    nc, i = k.nc, k.i
    s_par, zeroed = k.sem("feature_weights"), k.sem("feature_zeros")
    loaded, used = k.sem_list("pair_loaded", RING_A), k.sem("pair_used")
    t_ready, t_copied = k.sem("transposed"), k.sem("transposed_copied")
    h2_done, h2_copied = k.sem("h2_done"), k.sem("h2_copied")
    back, back_read = k.sem("h2_back"), k.sem("h2_back_read")
    var, root, own = k.sem("pair_var"), k.sem("pair_root"), k.sem("pair_own")
    n_ready, n_saved = k.sem("n_ready"), k.sem("n_saved")
    nt_done, nt_copied = k.sem("nt_done"), k.sem("nt_copied")
    v_done, v_ready, xw_own = k.sem("v_done"), k.sem("v_ready"), k.sem("xw_own")
    N_PAR = 13
    BACK_AT, ROOTS_AT, N_AT, V_AT = 2, (5, 9), 13, 14
    FEATURE_UNITS = [0] * 15 + [2] * 5
    order = list(range(BACK_AT + 1)) + ["back"] + list(range(BACK_AT + 1, N_AT + 1)) + ["n"] \
        + list(range(N_AT + 1, V_AT + 1)) + ["v"] + list(range(V_AT + 1, TGS))
    bank_of = {event: 5 + j % 2 for j, event in enumerate(order)}

    def last_in_bank(event, before):
        earlier = [e for e in order[:order.index(event)] if bank_of[e] == bank_of[event] and (before or isinstance(e, int))]
        return earlier[-1] if earlier else None

    BACK_BANK, NT_BANK, V_BANK, H2_BANK = bank_of["back"], bank_of["n"], bank_of["v"], 7

    def pair_of(tensor, p):
        b = NB - 2 - 2 * p
        return tensor[:, b:b + 2, :] if isinstance(b, int) else tensor[:, bass.ds(b, 2), :]

    with nc.Block() as block:
        @block.sync
        def _(sp):
            sp.wait_ge(zeroed, 2)
            for dst, src in ((k.gamma[:], i["ln_gamma"].partition_broadcast(P)),
                             (k.w_vw[0:D, 0, 0:D], i["Wv"]), (k.w_vw[0:D, 0, D:2 * D], i["W"]),
                             (k.w_vw[D:P, 1, 0:D], i["Wv"]), (k.w_vw[D:P, 1, D:2 * D], i["W"]),
                             (k.b_vw[:, 0:D], i["bv"].partition_broadcast(P)),
                             (k.w_q2[0:D, 0:D], i["Wq"]), (k.w_q2[0:D, D:2 * D], i["Wq"]),
                             (k.w_q2[D:P, 0:D], i["Wq"]), (k.w_q2[D:P, D:2 * D], i["Wq"]),
                             (k.b_q2[0:D, :], i["bq"].rearrange("(d a) -> d a", a=1)),
                             (k.b_q2[D:P, :], i["bq"].rearrange("(d a) -> d a", a=1)),
                             (k.theta[:], i["Theta"])):
                sp.dma_start(dst, src).then_inc(s_par, 16)
            load_ring(k, sp, k.adj_v, loaded, used, RING_A, True, True)

        @block.gpsimd
        def _(pool):
            nc.gpsimd.memset(k.w_vw[:], 0.0).then_inc(zeroed, 1)
            nc.gpsimd.memset(k.b_vw[:], 0.0).then_inc(zeroed, 1)

            def save(t, r, turn):
                pool.wait_ge(n_ready, t + 1)
                nc.gpsimd.tensor_copy(pair_of(k.n1, t), k.ln_out[:]).then_inc(n_saved, 1)
            steps(pool, save, 1, PAIRS)

        @block.scalar
        def _(act):
            def step(p, r, turn):
                now = not (isinstance(p, int) and p == PAIRS)
                before = not (isinstance(p, int) and p == 0)

                def copy_group(g):
                    act.wait_ge(t_ready, TGS * p + g + 1)
                    nc.scalar.activation(k.adj_t[g % T_BUFS][:], k.bank(bank_of[g]), ACT.Copy).then_inc(t_copied, 1)

                for g in range(TGS):
                    if before and g == 1:
                        act.wait_ge(h2_done, p)
                        at_least(act, back, p - 1)
                        nc.scalar.activation(k.h2_t[:], k.bank(H2_BANK, 2 * P), ACT.Copy).then_inc(h2_copied, 1)
                    if now:
                        copy_group(g)
                    if before and g in ROOTS_AT:
                        act.wait_ge(var, 2 * (p - 1) + ROOTS_AT.index(g) + 1)
                        nc.scalar.activation(k.pair[1][:], k.pair[0][:], ACT.Sqrt).then_inc(root, 1)
                    if before and g == N_AT:
                        act.wait_ge(nt_done, p)
                        nc.scalar.activation(k.n_t[:], k.bank(NT_BANK, P), ACT.Copy).then_inc(nt_copied, 1)
                    if before and g == V_AT + 2:
                        act.wait_ge(v_ready, p)
                        for j in range(2):
                            b = NB - 2 - 2 * (p - 1) + j
                            nc.scalar.activation(k.xw_sq[:], k.vw[:, j, D:2 * D], ACT.Square,
                                                 accum_out=columns(k.ssq_xw, b, 1)).then_inc(xw_own, 1)
                            act.wait_ge(xw_own, 2 * (p - 1) + j + 1)
            steps(act, step, 1, PAIRS + 1, tail=1)

        @block.vector
        def _(dve):
            link = Chain(dve, own)
            two = [P, 2, D]
            dve.wait_ge(s_par, N_PAR * 16)
            link(nc.vector.tensor_scalar(k.b_q8[:], k.b_q2[:], 1.0 / 8, None, ALU.mult))
            link(nc.vector.tensor_scalar(k.w_q2[:], k.w_q2[:], 1.0 / 8, None, ALU.mult))
            OPS = 25

            def norm(t, which):
                for j in range(2):
                    link(nc.vector.bn_stats(k.bn[j][:], k.ln_in[:, j, :]), k.constants)
                for j in range(2):
                    link(nc.vector.bn_aggr(k.mv[:, j, :], k.bn[j][:]), k.constants)
                nc.vector.tensor_scalar(k.pair[0][:], k.mv[:, :, 1:2], LN_EPS, None, ALU.add).then_inc(var, 1)
                dve.wait_ge(root, 2 * t + which + 1)
                inv_sqrt(nc, link, k.pair[1][:], k.pair[0][:], k.pair[1][:], k.pair[2][:])
                link(nc.vector.tensor_tensor(k.ln_out[:], k.ln_in[:], k.mv[:, :, 0:1].to_broadcast(two), ALU.subtract))
                link(nc.vector.tensor_tensor(k.ln_out[:], k.ln_out[:], k.pair[1][:].to_broadcast(two), ALU.mult))

            def step(t, r, turn):
                link.restart(2 + OPS * t)
                dve.wait_ge(back, t + 1)
                nc.vector.tensor_copy(k.ln_in[:], k.bank(BACK_BANK, P)).then_inc(back_read, 1)
                dve.wait_ge(back_read, t + 1)
                at_least(dve, n_saved, t)
                at_least(dve, nt_done, t)
                norm(t, 0)
                link(nc.vector.tensor_tensor(k.ln_out[:], k.ln_out[:], k.gamma[:].unsqueeze(1).to_broadcast(two), ALU.mult), k.constants)
                link(nc.vector.tensor_tensor(k.ln_in[:], k.ln_out[:], pair_of(k.x1, t), ALU.add), k.constants)
                norm(t, 1)
                nc.vector.tensor_scalar(k.ln_out[:], k.ln_out[:], 0.0, None, ALU.max).then_inc(n_ready, 1)
                wait_alone(dve, n_ready, t + 1, k.constants)
                link(nc.vector.tensor_copy(pair_of(k.x1, t), k.ln_in[:]))
                dve.wait_ge(v_done, t + 1)
                at_least(dve, used, 2 * t)
                at_least(dve, xw_own, 2 * t)
                nc.vector.tensor_tensor(k.vw[:], k.bank(V_BANK, 4 * D).rearrange("p (j c) -> p j c", j=2),
                                        k.b_vw[:].unsqueeze(1).to_broadcast([P, 2, 2 * D]), ALU.add).then_inc(v_ready, 1)
                assert link.n == OPS, link.n
            steps(dve, step, 1, PAIRS)

        @block.tensor
        def _(pe):
            pe.wait_ge(s_par, N_PAR * 16)

            def slots(r):
                b = (NB - 2 - 2 * r) % RING_A
                return k.ring[b], k.ring[b + 1]

            def step(p, r, turn):
                now = not (isinstance(p, int) and p == PAIRS)
                before = not (isinstance(p, int) and p == 0)
                blocks, old = slots(r), slots((r - 1) % PAIR_SLOTS)

                def bank_free(event):
                    e = last_in_bank(event, before)
                    if e == "back":
                        pe.wait_ge(back_read, p)
                    elif e == "n":
                        pe.wait_ge(nt_copied, p)
                    elif e == "v":
                        pe.wait_ge(v_ready, p)
                    elif now:
                        at_least(pe, t_copied, TGS * p + (0 if e is None else e + 1))

                def transposes(g):
                    bank_free(g)
                    if g == 0:
                        for j in (1, 0):
                            wait_loaded(pe, loaded, 2 * r + 1 - j, turn, True)
                    for c in range(2):
                        for j in range(2):
                            col = (2 * g + c) * P
                            done = nc.tensor.transpose(k.bank(bank_of[g], P, (2 * c + j) * P),
                                                       blocks[j][:, col:col + P], k.ident[:])
                    done.then_inc(t_ready, 1)

                def product(q, g):
                    pe.wait_ge(t_copied, TGS * q + g + 1)
                    if g == 0:
                        at_least(pe, h2_copied, q)
                    for c in range(2):
                        done = nc.tensor.matmul(k.bank(H2_BANK, 2 * P, 0, slice(D * c, D * c + D)), k.col[:, 2 * g + c, :],
                                                k.adj_t[g % T_BUFS][:, 2 * P * c:2 * P * (c + 1)],
                                                start=g == 0, stop=g == TGS - 1)
                    if g == TGS - 1:
                        done.then_inc(h2_done, 1)

                def features(n):
                    j = 1 - n // (NQ // 2)
                    if n == 0:
                        pe.wait_ge(v_ready, p)
                    for q in range(2 * n % NQ, 2 * n % NQ + 2):
                        done = nc.tensor.matmul(k.half_acc(q), k.vw[:, j, 0:D], old[j][:, q * BANK:(q + 1) * BANK],
                                                start=isinstance(p, int) and p == 1 and n < NQ // 2, stop=True,
                                                skip_group_check=True)
                    if n % (NQ // 2) == NQ // 2 - 1:
                        done.then_inc(used, 1)

                unit = 0
                for g in range(TGS):
                    if g < 2 and before:
                        product(p - 1, TGS - 2 + g)
                    if now:
                        transposes(g)
                    if g >= 2 and now:
                        product(p, g - 2)
                    if before:
                        for _ in range(FEATURE_UNITS[g]):
                            features(unit)
                            unit += 1
                    if before and g == BACK_AT:
                        pe.wait_ge(h2_copied, p)
                        bank_free("back")
                        for j in range(2):
                            done = nc.tensor.matmul(k.bank(BACK_BANK, D, j * D), k.h2_t[:, j * P:(j + 1) * P],
                                                    k.sel[:, 0:D], start=True, stop=True)
                        done.then_inc(back, 1)
                    if before and g == N_AT:
                        pe.wait_ge(n_ready, p)
                        bank_free("n")
                        nc.tensor.transpose(k.bank(NT_BANK, P), k.ln_out[:].rearrange("p j d -> p (j d)"),
                                            k.ident[:]).then_inc(nt_done, 1)
                    if before and g == V_AT:
                        pe.wait_ge(nt_copied, p)
                        bank_free("v")
                        nc.tensor.matmul(k.bank(V_BANK, 4 * D), k.n_t[:], k.w_vw[:].rearrange("p j c -> p (j c)"),
                                         start=True, stop=True).then_inc(v_done, 1)
            steps(pe, step, PAIR_SLOTS, PAIRS + 1, peel=1, tail=1)



def attention_operands(k, tag):
    nc = k.nc
    out, doubled = k.sem(f"{tag}_features_out"), k.sem(f"{tag}_doubled")
    hi_done, lo_done = k.sem(f"{tag}_hi"), k.sem(f"{tag}_lo")
    nt_done, nt_copied, q_done = k.sem(f"{tag}_nt"), k.sem(f"{tag}_nt_copied"), k.sem(f"{tag}_q")
    q_hi, q_lo = k.sem(f"{tag}_q_hi"), k.sem(f"{tag}_q_lo")

    def half(q):
        return slice(D * (q % 2), D * (q % 2) + D)

    with nc.Block() as block:
        @block.scalar
        def _(act):
            for b in range(NQ // 2):
                nc.scalar.activation(k.features_t[:, b * BANK:(b + 1) * BANK], k.bank(b), ACT.Copy).then_inc(out, 1)
            for q in range(NQ + 1):
                if q < NQ:
                    cols = slice(q * BANK, (q + 1) * BANK)
                    act.wait_ge(doubled, q + 1)
                    nc.scalar.activation(k.mov_hi[:, cols], k.bank(5 + q % 2), ACT.Copy).then_inc(hi_done, 1)
                    act.wait_ge(nt_done, q + 1)
                    at_least(act, q_done, q - 1)
                    nc.scalar.activation(k.n_t2[half(q), :], k.bank(q % 2, rows=slice(0, D)), ACT.Copy).then_inc(nt_copied, 1)
                if q >= 1:
                    f = q - 1
                    act.wait_ge(q_done, f + 1)
                    nc.scalar.activation(k.stat_op[:, f * BANK:(f + 1) * BANK], k.bank(2 + f % 2), ACT.Identity,
                                         bias=k.b_q8[:], scale=1.0).then_inc(q_hi, 1)

        @block.tensor
        def _(pe):
            for q in range(NQ + 1):
                if q < NQ:
                    pe.wait_ge(out, q // 2 + 1)
                    at_least(pe, lo_done, q - 1)
                    nc.tensor.matmul(k.bank(5 + q % 2), k.sel[half(q), :],
                                     k.features_t[half(q), q // 2 * BANK:(q // 2 + 1) * BANK],
                                     start=True, stop=True).then_inc(doubled, 1)
                    if q == 0:
                        pe.wait_ge(out, NQ // 2)
                    at_least(pe, nt_copied, q - 1)
                    for m in range(PER):
                        done = nc.tensor.transpose(k.bank(q % 2, P, m * P, slice(0, D)), k.n1[:, q * PER + m, :], k.ident[:])
                    done.then_inc(nt_done, 1)
                if q >= 1:
                    f = q - 1
                    pe.wait_ge(nt_copied, f + 1)
                    at_least(pe, q_lo, f - 1)
                    nc.tensor.matmul(k.bank(2 + f % 2), k.w_q2[half(f), :], k.n_t2[half(f), :], start=True, stop=True)\
                      .then_inc(q_done, 1)

        @block.vector
        def _(dve):
            for q in range(NQ + 1):
                if q < NQ:
                    cols = slice(q * BANK, (q + 1) * BANK)
                    dve.wait_ge(hi_done, q + 1)
                    nc.vector.tensor_tensor(k.mov_lo[:, cols], k.bank(5 + q % 2), k.mov_hi[:, cols].bitcast(FP32),
                                            ALU.subtract).then_inc(lo_done, 1)
                if q >= 1:
                    f = q - 1
                    cols, low = slice(f * BANK, (f + 1) * BANK), slice(D, P)
                    dve.wait_ge(q_hi, f + 1)
                    nc.vector.scalar_tensor_tensor(k.stat_op[low, cols], k.bank(2 + f % 2, rows=low), k.b_q8[low, :],
                                                   k.stat_op[low, cols].bitcast(FP32), ALU.add, ALU.subtract)\
                      .then_inc(q_lo, 1)


def scores(k, r, ch, bufs):
    b = 2 * ((NCH * r + ch) % bufs)
    return k.ps[:, b * BANK:(b + 2) * BANK]


def score_products(k, pe, out, stationary, ch):
    for part, begin in ((k.mov_hi, True), (k.mov_lo, False)):
        for h in range(2):
            c = ch * CH + h * BANK
            done = k.nc.tensor.matmul(out[:, h * BANK:(h + 1) * BANK], stationary[:], part[:, c:c + BANK],
                                      start=begin, stop=not begin)
    return done


def softmax_pass(k, tag, attention, first_slot, loaded, ready, following=None, first_sync=None):
    nc = k.nc
    stat_ready = k.sem(f"{tag}_stat")
    scored, masked, neg_max = k.sem(f"{tag}_scored"), k.sem(f"{tag}_times_adj"), k.sem(f"{tag}_max")
    exp_done, rz_ready, summed = k.sem(f"{tag}_exp"), k.sem(f"{tag}_rz"), k.sem(f"{tag}_summed")
    used = summed if attention else exp_done
    bufs = 2 if attention else 3
    LAG = 2

    def rows_of(r):
        return k.ring[(first_slot + r) % RING_A]

    with nc.Block() as block:
        @block.sync
        def _(sp):
            if first_sync is not None:
                first_sync(sp)

            def load(s, r, turn):
                if isinstance(s, int) and s < RING_A:
                    return
                wait_alone(sp, used, s - RING_A + 1, k.constants)
                blk = k.adj_v[s] if isinstance(s, int) else k.adj_v[bass.ds(s, 1), :, :].rearrange("a p n -> (a p) n")
                sp.dma_start(rows_of(r)[:], blk).then_inc(loaded[r], 16)
            steps(sp, load, RING_A, NB)
            if following is not None:
                for s in range(RING_A):
                    sp.wait_ge(used, NB + s - RING_A + 1)
                    sp.dma_start(rows_of(NB + s)[:], k.adj_v[s]).then_inc(following[s], 16)

        @block.gpsimd
        def _(pool):
            def step(s, r, turn):
                if not (isinstance(s, int) and s < 2):
                    pool.wait_ge(scored, NCH * (s - 1))
                c = s * P
                if attention:
                    nc.gpsimd.tensor_copy(k.stat_blk[r % 2][:], columns(k.stat_op, c, P)).then_inc(stat_ready, 2)
                else:
                    for half, part in ((slice(0, D), k.mov_hi), (slice(D, P), k.mov_lo)):
                        src = part[half, c:c + P] if isinstance(c, int) else part[half, bass.ds(c, P)]
                        nc.gpsimd.tensor_copy(k.stat_blk[r % 2][half, :], src).then_inc(stat_ready, 1)
            steps(pool, step, RING_A, NB)

        @block.tensor
        def _(pe):
            def step(s, r, turn):
                now = not (isinstance(s, int) and s >= NB)
                before = attention and not (isinstance(s, int) and s < LAG)
                if now:
                    pe.wait_ge(stat_ready, 2 * s + 2)
                for ch in range(NCH):
                    if now:
                        at_least(pe, masked, NCH * s + ch - bufs + 1)
                        score_products(k, pe, scores(k, r, ch, bufs), k.stat_blk[r % 2], ch).then_inc(scored, 1)
                    if before and ch % 2 == 0:
                        if ch == 0:
                            pe.wait_ge(rz_ready, s - LAG + 1)
                        for q in range(2 * ch, min(2 * ch + 4, NQ)):
                            done = nc.tensor.matmul(k.bank(4 + q // 4, rows=slice(32 * (q % 4), 32 * (q % 4) + 1)),
                                                    k.rz_blk[(r - LAG) % 2][:],
                                                    rows_of(r - LAG)[:, q * BANK:(q + 1) * BANK],
                                                    start=isinstance(s, int) and s == LAG, stop=True, skip_group_check=True)
                if before:
                    done.then_inc(summed, 1)
            steps(pe, step, RING_A, NB + (LAG if attention else 0), tail=LAG if attention else 0)

        @block.scalar
        def _(act):
            def step(s, r, turn):
                act.wait_ge(neg_max, s + 1)
                w = rows_of(r)
                nc.scalar.activation(w[:], w[:], ACT.Exp, bias=k.nmax[r % 2][:],
                                     accum_out=columns(k.z, s, 1)).then_inc(exp_done, 1)
            steps(act, step, RING_A, NB)

        @block.vector
        def _(dve):
            def inverse(s, r):
                at_least(dve, summed, s - LAG)
                wait_alone(dve, exp_done, s, k.constants)
                nc.vector.reciprocal(k.rz_blk[(r - 1) % 2][:], columns(k.z, s - 1, 1)).then_inc(rz_ready, 1)

            def step(s, r, turn):
                if isinstance(s, int) and s == NB:
                    inverse(s, r)
                    return
                wait_loaded(dve, loaded, r, turn, ready)
                if not attention:
                    at_least(dve, exp_done, s - 1)
                rows = rows_of(r)
                for ch in range(NCH):
                    cols = slice(ch * CH, (ch + 1) * CH)
                    wait_alone(dve, scored, NCH * s + ch + 1, k.constants)
                    nc.vector.tensor_tensor_reduce(out=rows[:, cols], in0=scores(k, r, ch, bufs), in1=rows[:, cols],
                                                   scale=1.0, scalar=LOWEST, op0=ALU.mult, op1=ALU.max,
                                                   accum_out=k.mx[:, ch:ch + 1]).then_inc(masked, 1)
                if attention and not (isinstance(s, int) and s == 0):
                    inverse(s, r)
                dve.wait_ge(masked, NCH * (s + 1))
                nc.vector.tensor_reduce(k.nmax[r % 2][:], k.mx[:], AX.X, ALU.max, negate=True).then_inc(neg_max, 1)
                dve.wait_ge(neg_max, s + 1)
            steps(dve, step, RING_A, NB + (1 if attention else 0), tail=1 if attention else 0)
            if attention:
                dve.wait_ge(rz_ready, NB)


class Across:

    def __init__(self, k, tag, op, banks):
        self.k, self.op, self.banks = k, op, banks
        self.column, self.row = k.sem(f"{tag}_column"), k.sem(f"{tag}_row")
        self.one, self.spread, self.out = k.sem(f"{tag}_one"), k.sem(f"{tag}_spread"), k.sem(f"{tag}_out")

    def tensor(self, pe, column):
        k, nc = self.k, self.k.nc
        pe.wait_ge(self.column, 1)
        nc.tensor.transpose(k.bank(self.banks[0], P, rows=slice(0, 1)), column[:], k.ident[:]).then_inc(self.row, 1)
        pe.wait_ge(self.one, 1)
        nc.tensor.matmul(k.bank(self.banks[1], 1), k.ones_row[:], k.row1[0:1, 0:1], start=True, stop=True)\
            .then_inc(self.spread, 1)

    def vector(self, dve, out, sign=1.0):
        k, nc = self.k, self.k.nc
        dve.wait_ge(self.row, 1)
        nc.vector.tensor_reduce(k.row1[0:1, 0:1], k.bank(self.banks[0], P, rows=slice(0, 1)), AX.X, self.op)\
            .then_inc(self.one, 1)
        dve.wait_ge(self.spread, 1)
        nc.vector.tensor_scalar(out[:], k.bank(self.banks[1], 1), sign, None, ALU.mult).then_inc(self.out, 1)
        dve.wait_ge(self.out, 1)


def component_mask(k, tag, layer):
    nc = k.nc
    own, out, moved = k.sem(f"{tag}_own"), k.sem(f"{tag}_colsum_out"), k.sem(f"{tag}_colsum_moved")
    turned, var, root = k.sem(f"{tag}_colsum_turned"), k.sem(f"{tag}_squares"), k.sem(f"{tag}_roots")
    exped = k.sem(f"{tag}_exped")
    top = Across(k, f"{tag}_max", ALU.max, (1, 2))
    total = Across(k, f"{tag}_total", ALU.add, (3, 4))
    xn_ready, xn_turned = k.sem(f"{tag}_xn"), k.sem(f"{tag}_xn_turned")
    hi_done, lo_done = k.sem(f"{tag}_hi"), k.sem(f"{tag}_lo")
    groups = NB // PER
    with nc.Block() as block:
        @block.sync
        def _(sp):
            sp.wait_ge(out, 4)
            for q in range(NQ):
                src = k.colsum[32 * (q % 4):32 * (q % 4) + 1, q // 4 * BANK:(q // 4 + 1) * BANK]
                sp.dma_start(k.colsum_rows[PER * q:PER * (q + 1), :], src.rearrange("p (m c) -> p m c", m=PER))\
                  .then_inc(moved, 16)

        @block.scalar
        def _(act):
            for h in range(4):
                cols = BANK * (3 if h < 2 else 2)
                nc.scalar.activation(k.colsum[32 * h:32 * h + 1, 0:cols], k.bank(4, cols, rows=slice(32 * h, 32 * h + 1)),
                                     ACT.Copy).then_inc(out, 1)
            act.wait_ge(var, 1)
            nc.scalar.activation(k.rows2[:], k.rows[:], ACT.Sqrt).then_inc(root, 1)
            act.wait_ge(var, 2)
            nc.scalar.activation(k.rows2[:], k.rows[:], ACT.Sqrt).then_inc(root, 1)
            act.wait_ge(top.out, 1)
            nc.scalar.activation(k.rows3[:], k.rows[:], ACT.Exp, bias=k.one[1][:], accum_out=k.one[0][:]).then_inc(total.column, 1)
            for g in range(groups):
                act.wait_ge(xn_turned, g + 1)
                nc.scalar.activation(k.mov_hi[:, g * BANK:(g + 1) * BANK], k.bank(6 + g % 2), ACT.Copy).then_inc(hi_done, 1)

        @block.tensor
        def _(pe):
            pe.wait_ge(moved, NQ * 16)
            nc.tensor.transpose(k.bank(0, NB), k.colsum_rows[:], k.ident[0:NB, 0:NB]).then_inc(turned, 1)
            top.tensor(pe, k.one[0])
            total.tensor(pe, k.one[0])
            for g in range(groups):
                pe.wait_ge(xn_ready, g + 1)
                at_least(pe, lo_done, g - 1)
                for m in range(PER):
                    done = nc.tensor.transpose(k.bank(6 + g % 2, P, m * P), k.xn4[g % 2][:, m].rearrange("p t d -> p (t d)"),
                                               k.ident[:])
                done.then_inc(xn_turned, 1)

        @block.vector
        def _(dve):
            link = Chain(dve, own)

            def norms(squares, n):
                link(nc.vector.tensor_scalar(k.rows[:], squares, NORM_MIN, None, ALU.max))
                nc.vector.tensor_copy(k.conn[:], k.rows[:]).then_inc(var, 1)
                dve.wait_ge(var, n)
                dve.wait_ge(root, n)
                inv_sqrt(nc, link, k.rows2[:], k.rows[:], k.rows2[:], k.rows3[:])
                link(nc.vector.tensor_tensor(k.rows3[:], k.rows2[:], k.rows[:], ALU.mult))

            link(nc.vector.tensor_tensor(k.n_sq[:], k.n1[:], k.n1[:], ALU.mult))
            link(nc.vector.reduce_sum(k.sq_n[:], k.n_sq[:], AX.X))
            norms(k.ssq_xw[:], 1)
            link(nc.vector.tensor_copy(k.structural[:], k.rows3[:]))
            norms(k.sq_n[:], 2)
            link(nc.vector.tensor_copy(k.feat_mag[:], k.rows3[:]))
            link(nc.vector.tensor_scalar(k.rows3[:], k.rows3[:], 1e-8, None, ALU.max))
            link(nc.vector.reciprocal(k.rz[:], k.rows3[:]))
            dve.wait_ge(turned, 1)
            link(nc.vector.tensor_scalar(k.rows[:], k.bank(0, NB), 0.5 / N, None, ALU.mult))
            link(nc.vector.tensor_scalar(k.rows2[:], k.structural[:], 0.5, None, ALU.mult))
            link(nc.vector.tensor_tensor(k.rows[:], k.rows[:], k.rows2[:], ALU.add))
            nc.vector.reduce_max(k.one[0][:], k.rows[:], AX.X).then_inc(top.column, 1)
            top.vector(dve, k.one[1], -1.0)
            total.vector(dve, k.one[2])
            link(nc.vector.reciprocal(k.one[3][:], k.one[2][:]))
            link(nc.vector.tensor_scalar(k.comp_mask[:], k.rows3[:], k.one[3][:], THRESHOLDS[layer], ALU.mult, ALU.is_ge))
            link(nc.vector.tensor_tensor(k.rows[:], k.comp_mask[:], k.rz[:], ALU.mult))
            link(nc.vector.tensor_tensor(k.feat_mag[:], k.comp_mask[:], k.feat_mag[:], ALU.mult))
            link(nc.vector.tensor_scalar(k.feat_mag[:], k.feat_mag[:], 1e-8, None, ALU.max))
            for g in range(groups + 1):
                if g < groups:
                    b = slice(g * PER, (g + 1) * PER)
                    shape = [P, PER, 2, D]
                    at_least(dve, xn_turned, g - 1)
                    nc.vector.tensor_tensor(k.xn4[g % 2][:], k.n1[:, b, :].unsqueeze(2).to_broadcast(shape),
                                            k.rows[:, b].unsqueeze(2).unsqueeze(3).to_broadcast(shape), ALU.mult).then_inc(xn_ready, 1)
                if g >= 1:
                    f = g - 1
                    cols = slice(f * BANK, (f + 1) * BANK)
                    dve.wait_ge(hi_done, f + 1)
                    nc.vector.tensor_tensor(k.mov_lo[:, cols], k.bank(6 + f % 2), k.mov_hi[:, cols].bitcast(FP32),
                                            ALU.subtract).then_inc(lo_done, 1)


def any_edge(k, tag, layer):
    nc = k.nc
    own, ready = k.sem(f"{tag}_own"), k.sem(f"{tag}_ready")
    top = Across(k, tag, ALU.max, (0, 1))
    with nc.Block() as block:
        @block.vector
        def _(dve):
            link = Chain(dve, own)
            link(nc.vector.reciprocal(k.rz[:], k.z[:]))
            link(nc.vector.tensor_tensor(k.rows[:], k.rz[:], k.comp_mask[:], ALU.mult))
            nc.vector.reduce_max(k.one[0][:], k.rows[:], AX.X).then_inc(top.column, 1)
            top.vector(dve, k.one[1])
            link(nc.vector.tensor_scalar(k.flag[:], k.one[1][0:1, :], THRESHOLDS[layer] * 0.999, None, ALU.is_ge))

        @block.tensor
        def _(pe):
            top.tensor(pe, k.one[0])



def prune_pass(k, tag, threshold):
    nc = k.nc
    loaded, stat_ready = k.sem_list(f"{tag}_loaded", RING_B), k.sem(f"{tag}_stat")
    scored, masked, neg_max = k.sem(f"{tag}_scored"), k.sem(f"{tag}_times_adj"), k.sem(f"{tag}_max")
    exp_done, pruned, own = k.sem(f"{tag}_exp"), k.sem(f"{tag}_pruned"), k.sem(f"{tag}_own")
    stored = k.sem_list(f"{tag}_stored", 2)
    bufs = 4

    with nc.Block() as block:
        @block.sync
        def _(sp):
            def store(s, r):
                wait_alone(sp, pruned, s + 1, k.constants)
                blk = k.hp_v[s] if isinstance(s, int) else k.hp_v[bass.ds(s, 1), :, :].rearrange("a p n -> (a p) n")
                sp.dma_start(blk, k.work[r % 2][:]).then_inc(stored[r % 2], 16)

            def step(s, r, turn):
                if not (isinstance(s, int) and s < RING_B):
                    store(s - RING_B, r)
                blk = k.adj_v[s] if isinstance(s, int) else k.adj_v[bass.ds(s, 1), :, :].rearrange("a p n -> (a p) n")
                sp.dma_start(k.ring[r][:], blk).then_inc(loaded[r], 16)
            steps(sp, step, RING_B, NB)
            for s in range(NB - RING_B, NB):
                store(s, s % RING_B)
            for j in range(2):
                sp.wait_ge(stored[j], 16 * NB // 2)

        @block.gpsimd
        def _(pool):
            def step(s, r, turn):
                if not (isinstance(s, int) and s < 2):
                    pool.wait_ge(scored, NCH * (s - 1))
                c = s * P
                for half, part in ((slice(0, D), k.mov_hi), (slice(D, P), k.mov_lo)):
                    src = part[half, c:c + P] if isinstance(c, int) else part[half, bass.ds(c, P)]
                    nc.gpsimd.tensor_copy(k.stat_blk[r % 2][half, :], src).then_inc(stat_ready, 1)
            steps(pool, step, RING_B, NB)

        @block.tensor
        def _(pe):
            def step(s, r, turn):
                pe.wait_ge(stat_ready, 2 * s + 2)
                for ch in range(NCH):
                    at_least(pe, masked, NCH * s + ch - bufs + 1)
                    score_products(k, pe, scores(k, r, ch, bufs), k.stat_blk[r % 2], ch).then_inc(scored, 1)
            steps(pe, step, RING_B, NB)

        @block.scalar
        def _(act):
            def step(s, r, turn):
                act.wait_ge(neg_max, s + 1)
                w = k.work[r % 2]
                nc.scalar.activation(w[:], w[:], ACT.Exp, bias=k.nmax[r % 2][:],
                                     accum_out=columns(k.z, s, 1)).then_inc(exp_done, 1)
            steps(act, step, RING_B, NB)

        @block.vector
        def _(dve):
            def finish(s, r):
                w, inverse = k.work[(r - 1) % 2], k.rz_blk[(r - 1) % 2]
                wait_alone(dve, exp_done, s, k.constants)
                nc.vector.reciprocal(inverse[:], columns(k.z, s - 1, 1)).then_inc(own, 1)
                wait_alone(dve, own, 2 * s - 1, k.constants)
                nc.vector.tensor_scalar(w[:], w[:], inverse[:], threshold, ALU.mult, ALU.is_ge).then_inc(own, 1)
                wait_alone(dve, own, 2 * s, k.constants)
                nc.vector.scalar_tensor_tensor(w[:], w[:], columns(k.comp_mask, s - 1, 1), k.ring[(r - 1) % RING_B][:],
                                               ALU.mult, ALU.mult, accum_out=columns(k.conn, s - 1, 1)).then_inc(pruned, 1)

            def step(s, r, turn):
                if isinstance(s, int) and s == NB:
                    finish(s, r)
                    return
                wait_loaded(dve, loaded, r, turn, False)
                at_least(dve, stored[r % 2], 32 * turn + 16 * (r // 2))
                for ch in range(NCH):
                    cols = slice(ch * CH, (ch + 1) * CH)
                    wait_alone(dve, scored, NCH * s + ch + 1, k.constants)
                    nc.vector.tensor_tensor_reduce(out=k.work[r % 2][:, cols], in0=scores(k, r, ch, bufs),
                                                   in1=k.ring[r][:, cols], scale=1.0, scalar=LOWEST, op0=ALU.mult,
                                                   op1=ALU.max, accum_out=k.mx[:, ch:ch + 1]).then_inc(masked, 1)
                dve.wait_ge(masked, NCH * (s + 1))
                nc.vector.tensor_reduce(k.nmax[r % 2][:], k.mx[:], AX.X, ALU.max, negate=True).then_inc(neg_max, 1)
                dve.wait_ge(neg_max, s + 1)
                if not (isinstance(s, int) and s == 0):
                    finish(s, r)
            steps(dve, step, RING_B, NB + 1, peel=RING_B, tail=1)


def rows_times(k, tag, src, weights, bank, cols, consume, before=None, scalar_before=None):
    nc = k.nc
    ready, turned, copied = k.sem(f"{tag}_ready"), k.sem(f"{tag}_turned"), k.sem(f"{tag}_copied")
    product, consumed = k.sem(f"{tag}_product"), k.sem(f"{tag}_consumed")
    groups = NB // PER
    with nc.Block() as block:
        @block.scalar
        def _(act):
            if scalar_before is not None:
                scalar_before(act)
            for g in range(groups):
                act.wait_ge(turned, g + 1)
                at_least(act, product, g - 1)
                nc.scalar.activation(k.n_t4[g % 2][:], k.bank(g % 2, rows=slice(0, D)), ACT.Copy).then_inc(copied, 1)

        @block.tensor
        def _(pe):
            pe.wait_ge(ready, 1)
            for g in range(groups + 1):
                if g < groups:
                    at_least(pe, copied, g - 1)
                    for m in range(PER):
                        done = nc.tensor.transpose(k.bank(g % 2, P, m * P, slice(0, D)), src[:, g * PER + m, :], k.ident[:])
                    done.then_inc(turned, 1)
                if g >= 1:
                    f = g - 1
                    pe.wait_ge(copied, f + 1)
                    at_least(pe, consumed, f - 1)
                    for m in range(PER):
                        done = nc.tensor.matmul(k.bank(bank + f % 2, cols, m * cols), k.n_t4[f % 2][:, m * P:(m + 1) * P],
                                                weights, start=True, stop=True)
                    done.then_inc(product, 1)

        @block.vector
        def _(dve):
            if before is not None:
                before(dve)
            nc.vector.tensor_copy(k.one[0][:], k.ones[:]).then_inc(ready, 1)
            for g in range(groups):
                dve.wait_ge(product, g + 1)
                view = k.bank(bank + g % 2, PER * cols).rearrange("p (m c) -> p m c", m=PER)
                consume(dve, g, view).then_inc(consumed, 1)
            dve.wait_ge(consumed, groups)


def values(k, tag):
    nc, i = k.nc, k.i
    weights, own = k.sem(f"{tag}_weights"), k.sem(f"{tag}_own")
    with nc.Block() as block:
        @block.sync
        def _(sp):
            for dst, src in ((k.g_w[:, 0:D], i["Wv"]), (k.g_w[:, D:2 * D], i["W"]),
                             (k.g_b[:], i["bv"].partition_broadcast(P))):
                sp.dma_start(dst, src).then_inc(weights, 16)
            sp.wait_ge(weights, 48)
    state = {}

    def before(dve):
        state["link"] = Chain(dve, own)

    def consume(dve, g, view):
        link, b = state["link"], slice(g * PER, (g + 1) * PER)
        link(nc.vector.tensor_tensor(k.tall[:, b, :], view[:, :, 0:D], k.g_b[:].unsqueeze(1).to_broadcast([P, PER, D]),
                                     ALU.add))
        link(nc.vector.tensor_copy(k.g_xw[:], view[:, :, D:2 * D]))
        link(nc.vector.tensor_tensor(k.g_xw[:], k.g_xw[:], k.g_xw[:], ALU.mult))
        link(nc.vector.reduce_sum(k.ssq_xw[:, b], k.g_xw[:], AX.X))
        return nc.vector.tensor_copy(k.one[0][:], k.ones[:])

    rows_times(k, tag, k.n1, k.g_w[:], 2, 2 * D, consume, before)


def node_operand(k, tag, layer):
    nc, i = k.nc, k.i
    weights, own = k.sem(f"{tag}_weights"), k.sem(f"{tag}_own")
    var, root = k.sem(f"{tag}_degrees"), k.sem(f"{tag}_roots")
    top = Across(k, f"{tag}_max", ALU.max, (4, 5))
    total = Across(k, f"{tag}_total", ALU.add, (6, 7))
    with nc.Block() as block:
        @block.sync
        def _(sp):
            sp.dma_start(k.g_w[:, 0:D], i["W"]).then_inc(weights, 16)
            sp.wait_ge(weights, 16)

        @block.tensor
        def _(pe):
            top.tensor(pe, k.one[0])
            total.tensor(pe, k.one[0])

        @block.scalar
        def _(act):
            act.wait_ge(top.out, 1)
            nc.scalar.activation(k.rows3[:], k.rows[:], ACT.Exp, bias=k.one[1][:], accum_out=k.one[0][:])\
              .then_inc(total.column, 1)
            act.wait_ge(var, 1)
            nc.scalar.activation(k.structural[:], k.z[:], ACT.Sqrt).then_inc(root, 1)

        @block.vector
        def _(dve):
            link = Chain(dve, own)
            link(nc.vector.tensor_tensor(k.rows[:], k.conn[:], k.feat_mag[:], ALU.mult))
            nc.vector.reduce_max(k.one[0][:], k.rows[:], AX.X).then_inc(top.column, 1)
            top.vector(dve, k.one[1], -1.0)
            link(nc.vector.tensor_scalar(k.z[:], k.conn[:], EPS, None, ALU.max))
            nc.vector.tensor_copy(k.mx[:, 0:1], k.z[:, 0:1]).then_inc(var, 1)
            total.vector(dve, k.one[2])
            dve.wait_ge(root, 1)
            inv_sqrt(nc, link, k.structural[:], k.z[:], k.structural[:], k.rows2[:])
            link(nc.vector.reciprocal(k.one[3][:], k.one[2][:]))
            link(nc.vector.tensor_scalar(k.rows3[:], k.rows3[:], k.one[3][:], THRESHOLDS[layer], ALU.mult, ALU.is_ge))
            link(nc.vector.tensor_tensor(k.rows3[:], k.rows3[:], k.comp_mask[:], ALU.mult))
            link(nc.vector.tensor_scalar(k.rows[:], k.conn[:], 0.0, None, ALU.is_gt))
            link(nc.vector.tensor_tensor(k.rows3[:], k.rows3[:], k.rows[:], ALU.mult))
            link(nc.vector.tensor_tensor(k.h[:], k.n1[:], k.rows3[:].unsqueeze(2).to_broadcast([P, NB, D]), ALU.mult))

    def consume(dve, g, view):
        b = slice(g * PER, (g + 1) * PER)
        return nc.vector.tensor_tensor(k.tall[:, b, :], view, k.structural[:, b].unsqueeze(2).to_broadcast([P, PER, D]),
                                       ALU.mult)

    rows_times(k, f"{tag}_w", k.h, k.g_w[:, 0:D], 2, D, consume)


def edge_degrees(k, tag):
    nc = k.nc
    out, moved, turned, own = k.sem(f"{tag}_out"), k.sem(f"{tag}_moved"), k.sem(f"{tag}_turned"), k.sem(f"{tag}_own")
    with nc.Block() as block:
        @block.scalar
        def _(act):
            for h in range(4):
                cols = BANK * (3 if h < 2 else 2)
                nc.scalar.activation(k.colsum[32 * h:32 * h + 1, 0:cols], k.bank(5, cols, rows=slice(32 * h, 32 * h + 1)),
                                     ACT.Copy).then_inc(out, 1)

        @block.sync
        def _(sp):
            sp.wait_ge(out, 4)
            for q in range(NQ):
                src = k.colsum[32 * (q % 4):32 * (q % 4) + 1, q // 4 * BANK:(q // 4 + 1) * BANK]
                sp.dma_start(k.colsum_rows[PER * q:PER * (q + 1), :], src.rearrange("p (m c) -> p m c", m=PER))\
                  .then_inc(moved, 16)

        @block.tensor
        def _(pe):
            pe.wait_ge(moved, NQ * 16)
            nc.tensor.transpose(k.bank(5, NB), k.colsum_rows[:], k.ident[0:NB, 0:NB]).then_inc(turned, 1)

        @block.vector
        def _(dve):
            link = Chain(dve, own)
            dve.wait_ge(turned, 1)
            link(nc.vector.tensor_scalar(k.rows[:], k.bank(5, NB), EPS, None, ALU.max))
            link(nc.vector.reciprocal(k.rz[:], k.rows[:]))


def row_pass(k, tag):
    nc = k.nc
    loaded, used = k.sem_list(f"{tag}_loaded", RING_B), k.sem(f"{tag}_used")
    turned, copied, read = k.sem(f"{tag}_turned"), k.sem(f"{tag}_copied"), k.sem(f"{tag}_read")
    with nc.Block() as block:
        @block.sync
        def _(sp):
            load_ring(k, sp, k.hp_v, loaded, used, RING_B, True, True)

        @block.scalar
        def _(act):
            def step(s, r, turn):
                for q in range(NQ):
                    act.wait_ge(turned, NQ * s + q + 1)
                    nc.scalar.activation(k.adj_t[q % 4][:], k.bank(q % 4), ACT.Copy).then_inc(copied, 1)
            steps(act, step, RING_B, NB)

        @block.vector
        def _(dve):
            def step(s, r, turn):
                wait_alone(dve, used, s + 1, k.constants)
                b = NB - 1 - s
                nc.vector.tensor_copy(k.g_dv[:], columns(k.structural, b, 1)).then_inc(read, 1)
                wait_alone(dve, read, 2 * s + 1, k.constants)
                nc.vector.tensor_scalar(block_of(k.msg, b), k.bank(6 + r % 2, D), k.g_dv[:], None, ALU.mult)\
                  .then_inc(read, 1)
                dve.wait_ge(read, 2 * s + 2)
            steps(dve, step, RING_B, NB)

        @block.tensor
        def _(pe):
            def step(s, r, turn):
                wait_loaded(pe, loaded, r, turn, True)
                rows = k.ring[slot_of(r, RING_B, True)]
                at_least(pe, read, 2 * s - 2)
                for q in range(NQ + 2):
                    if q < NQ:
                        at_least(pe, copied, NQ * s + q - 3)
                        for m in range(PER):
                            c = q * BANK + m * P
                            done = nc.tensor.transpose(k.bank(q % 4, P, m * P), rows[:, c:c + P], k.ident[:])
                        done.then_inc(turned, 1)
                    if q >= 2:
                        f = q - 2
                        pe.wait_ge(copied, NQ * s + f + 1)
                        for m in range(PER):
                            done = nc.tensor.matmul(k.bank(6 + r % 2, D), k.adj_t[f % 4][:, m * P:(m + 1) * P],
                                                    k.tall[:, f * PER + m, :], start=f == 0 and m == 0,
                                                    stop=f == NQ - 1 and m == PER - 1)
                done.then_inc(used, 1)
            steps(pe, step, RING_B, NB)


def remaining_edges(k, tag, layer):
    nc = k.nc
    prune_pass(k, f"{tag}_prune", THRESHOLDS[layer])
    node_operand(k, f"{tag}_node", layer)
    column_pass(k, f"{tag}_agg", k.hp_v, k.tall, RING_B, degrees=True)
    edge_degrees(k, f"{tag}_deg")
    by_blocks(k, f"{tag}_agg", k.wide, k.tall, k.rz)
    row_pass(k, f"{tag}_msg")
    own = k.sem(f"{tag}_out_own")
    state = {}

    def before(dve):
        state["link"] = Chain(dve, own)

    def consume(dve, g, view):
        b = slice(g * PER, (g + 1) * PER)
        if layer == 0:
            return nc.vector.tensor_scalar(k.n1[:, b, :], view, 0.0, None, ALU.max)
        state["link"](nc.vector.tensor_scalar(k.tall[:, b, :], view, 0.0, None, ALU.max))
        return nc.vector.tensor_tensor(k.x1[:, b, :], k.x1[:, b, :], k.tall[:, b, :], ALU.add)

    rows_times(k, f"{tag}_out", k.msg, k.theta[:], 2, D, consume, before)


def program(nc, ins, out):
    k = Kernel(nc, ins, out)
    embed_and_columns(k)
    network_and_features(k)
    attention_operands(k, "att")
    edge_loaded = k.sem_list("edge_loaded", RING_A)
    softmax_pass(k, "att", True, 0, k.sem_list("att_loaded", RING_A), True, following=edge_loaded)
    component_mask(k, "comp", 0)
    stored = k.sem("x1_stored")

    def store(sp):
        sp.dma_start(k.out_v, k.x1[:]).then_inc(stored, 16)
    softmax_pass(k, "edge", False, NB % RING_A, edge_loaded, False, first_sync=store)
    any_edge(k, "flag", 0)
    with nc.Block() as block:
        @block.sync
        def _(sp):
            sp.wait_ge(stored, 16)
    edges_left = nc.values_load(k.flag[0:1, 0:1], min_val=0, max_val=1)
    with nc.If(edges_left > 0):
        k.fresh_semaphores()
        remaining_edges(k, "l0", 0)
        k.fresh_semaphores()
        values(k, "l1_v")
        column_pass(k, "l1_edge", k.adj_v, k.tall, RING_B)
        attention_operands(k, "l1_att")
        first_rows = k.sem_list("l1_att_loaded", RING_A)
        with nc.Block() as block:
            @block.sync
            def _(sp):
                for s in range(RING_A):
                    sp.dma_start(k.ring[s][:], k.adj_v[s]).then_inc(first_rows[s], 16)
        softmax_pass(k, "l1_att", True, 0, first_rows, False)
        component_mask(k, "l1_comp", 1)
        k.fresh_semaphores()
        remaining_edges(k, "l1", 1)
        result = k.sem("result_stored")
        with nc.Block() as block:
            @block.sync
            def _(sp):
                sp.dma_start(k.out_v, k.x1[:]).then_inc(result, 16)
                sp.wait_ge(result, 16)


_INS = {'x': 'x', 'adj': 'adj', 'L0_gnn_W_u': 'W_u', 'L0_gnn_diag_u': 'diag_u', 'L0_gnn_par_u': 'par_u',
        'L0_gnn_W_i': 'W_i', 'L0_gnn_diag_i': 'diag_i', 'L0_gnn_par_i': 'par_i', 'L0_gnn_ln_gamma': 'ln_gamma',
        'L0_gnn_ln_beta': 'ln_beta', 'L1_gnn_W': 'W', 'L1_gnn_Theta': 'Theta', 'L1_gnn_Wq': 'Wq',
        'L1_gnn_bq': 'bq', 'L1_gnn_Wv': 'Wv', 'L1_gnn_bv': 'bv'}


def kernel(**inputs):
    import numpy as _np
    import concourse.bacc as _bacc
    from concourse import mybir as _mybir
    from concourse.bass_utils import run_bass_kernel_spmd as _run

    nc = _bacc.Bacc("TRN2", target_bir_lowering=False, num_devices=1)
    arrays, ins = {}, {}
    for name, short in _INS.items():
        a = _np.ascontiguousarray(inputs[name])
        arrays[f"in_{name}_dram"] = a
        ins[short] = nc.dram_tensor(f"in_{name}_dram", a.shape, _mybir.dt.from_np(a.dtype), kind="ExternalInput").ap()
    out = nc.dram_tensor("out_0_dram", (5120, 64), _mybir.dt.float32, kind="ExternalOutput").ap()
    program(nc, ins, out)
    r = _run(nc, [arrays], core_ids=[0])
    return r.results[0]["out_0_dram"]
```

```python
import concourse.bass as bass
from concourse import mybir

FP32 = mybir.dt.float32
FP32R = mybir.dt.float32r
INT32 = mybir.dt.int32
ALU = mybir.AluOpType
ACT = mybir.ActivationFunctionType
AX = mybir.AxisListType

P = 128
N = 5120
D = 64
NB = N // P
NU = 2048
UB = NU // P
BANK = 512
NQ = N // BANK
PER = BANK // P
CHUNKS = [(2 * BANK * c, 2 * BANK, 2 * (c % 4)) for c in range(N // (2 * BANK))]
CHUNKS_BESIDE = [(5 * BANK * h + c, cols, bank) for h in range(2)
                 for c, cols, bank in ((0, 2 * BANK, 0), (2 * BANK, 2 * BANK, 2), (4 * BANK, BANK, 7))]
RING_A = 6
RING_B = 4
PAIRS = NB // 2
PAIR_SLOTS = RING_A // 2
TGS = NB // 2
T_BUFS = 5
HALF = 4 * N // 2
LN_EPS = 1e-5
EPS = 1e-6
NORM_MIN = 1e-16
THRESHOLDS = (0.000244, 0.000244 + (1.0 - 0.9048374180359595) * (0.0003 - 0.000244))
LOWEST = -3.0e38


def at_least(eng, sem, value):
    if not (isinstance(value, int) and value <= 0):
        eng.wait_ge(sem, value)


def wait_alone(eng, sem, value, other):
    if not isinstance(value, int):
        value = eng.to_reg(value)
        eng.wait_ge(other, 1)
    at_least(eng, sem, value)


class Chain:

    def __init__(self, eng, sem):
        self.eng, self.sem, self.base, self.n = eng, sem, 0, 0

    def restart(self, base):
        self.base, self.n = base, 0

    def __call__(self, ins, other=None):
        self.n += 1
        ins.then_inc(self.sem, 1)
        if other is None:
            self.eng.wait_ge(self.sem, self.base + self.n)
        else:
            wait_alone(self.eng, self.sem, self.base + self.n, other)


def steps(eng, body, unroll, count, peel=None, tail=0):
    peel = unroll if peel is None else peel
    loops = (count - peel - tail) // unroll
    for s in range(peel):
        body(s, s % unroll, s // unroll)
    with eng.Fori(0, loops) as it:
        for r in range(peel, peel + unroll):
            body(it * unroll + r, r % unroll, it + r // unroll)
    for s in range(peel + loops * unroll, count):
        body(s, s % unroll, s // unroll)


def block_of(tensor, b):
    return tensor[:, b, :] if isinstance(b, int) else tensor[:, bass.ds(b, 1), :].rearrange("p a d -> p (a d)")


def columns(tensor, first, size):
    return tensor[:, first:first + size] if isinstance(first, int) else tensor[:, bass.ds(first, size)]


def newton(nc, link, y, v, tmp):
    link(nc.vector.tensor_tensor(tmp, v, y, ALU.mult))
    link(nc.vector.tensor_tensor(tmp, tmp, y, ALU.mult))
    link(nc.vector.tensor_scalar(tmp, tmp, -0.5, 1.5, ALU.mult, ALU.add))
    link(nc.vector.tensor_tensor(y, y, tmp, ALU.mult))


def inv_sqrt(nc, link, out, v, sd, tmp):
    link(nc.vector.reciprocal(out, sd))
    newton(nc, link, out, v, tmp)


class Memory:

    def __init__(self, nc):
        self.nc, self.end = nc, -(-nc.sbuf_base // 32) * 32

    def at(self, name, offset, shape, dt=FP32):
        return self.nc.alloc_sbuf_tensor_at(name, shape, dt, offset=offset)

    def take(self, size):
        offset, self.end = self.end, self.end + -(-size // 32) * 32
        assert self.end <= self.nc.sbuf_usable_end, self.end
        return offset

    def new(self, name, shape, dt=FP32):
        size = 4
        for n in shape[1:]:
            size *= n
        return self.at(name, self.take(size), shape, dt)


class Kernel:

    def __init__(self, nc, ins, out):
        self.nc, self.i = nc, ins
        self.sems, self.spare = {}, []
        self.x_v = ins["x"].rearrange("(b p) d -> p b d", p=P)
        self.out_v = out.rearrange("(b p) d -> p b d", p=P)
        self.adj_v = ins["adj"].rearrange("(b p) n -> b p n", p=P)
        self.hp_v = nc.dram_tensor("pruned", (N, N), FP32).ap().rearrange("(b p) n -> b p n", p=P)
        m = Memory(nc)
        region = [m.take(4 * N) for _ in range(9)]
        self.ring = [m.at(f"ring{r}", region[r], [P, N]) for r in range(RING_A)]
        self.work = [m.at(f"work{r}", region[4 + r], [P, N]) for r in range(2)]
        self.stat_op = m.at("stat_op", region[6], [P, N], FP32R)
        self.mov_hi = m.at("mov_hi", region[7], [P, N], FP32R)
        self.mov_lo = m.at("mov_lo", region[8], [P, N], FP32R)
        self.colsum = m.at("colsum", region[6], [P, 3 * BANK])
        self.colsum_rows = m.at("colsum_rows", region[6] + 12 * BANK, [NB, P])
        self.xn4 = [m.at(f"xn4{r}", region[6] + (12 + 4 * r) * BANK + 4 * P, [P, PER, 2, D]) for r in range(4)]
        self.n_t8 = [m.at(f"n_t8{r}", region[6] + (NQ - 2 + r) * 4 * BANK, [P, BANK]) for r in range(2)]
        self.wide = m.at("wide", region[5], [P, N // 2])
        self.tall = m.at("tall", region[5] + HALF, [P, NB, D])
        self.h = m.at("h", region[6], [P, NB, D])
        self.emb = m.at("emb", region[6] + HALF, [P, NB, D])
        self.xin = m.at("xin", region[7], [P, NB, D])
        self.xc = m.at("xc", region[7] + HALF, [P, NB, D])
        self.sq = m.at("sq", region[8], [P, NB, D])
        self.col_t = m.at("col_t", region[7], [P, N // 2])
        self.col = m.at("col", region[7] + HALF, [P, NB, D])
        self.adj_t = [m.at(f"adj_t{g}", region[7] + g * 4 * BANK, [P, BANK]) for g in range(T_BUFS)]
        o = region[8] + HALF
        self.h_t = [m.at(f"h_t{r}", o + r * 4 * BANK, [D, BANK]) for r in range(2)]
        self.diag_rows = m.at("diag_rows", o + 8 * BANK, [NB, P])
        self.w_ui = [m.at(f"w_{c}", o + 8 * BANK + 4 * P + j * 4 * D, [D, D]) for j, c in enumerate("ui")]
        self.beta = m.at("beta", o + 8 * BANK + 4 * P + 8 * D, [P, D])
        o = region[8]
        self.w_vw = m.at("w_vw", o, [P, 2, 2 * D])
        self.vw = m.at("vw", o + 1024, [P, 2, 2 * D])
        self.h2_t = m.at("h2_t", o + 2560, [P, 2 * P])
        self.n_t = m.at("n_t", o + 3584, [P, P])
        self.ln_in = m.at("ln_in", o + 4096, [P, 2, D])
        self.ln_out = m.at("ln_out", o + 4608, [P, 2, D])
        self.xw_sq = m.at("xw_sq", o + 5120, [P, D])
        self.gamma = m.at("gamma", o + 5376, [P, D])
        self.b_vw = m.at("b_vw", o + 5632, [P, 2 * D])
        self.n_t4 = [m.at(f"n_t4{r}", region[4] + r * 4 * BANK, [D, BANK]) for r in range(2)]
        self.msg = m.at("msg", region[8], [P, NB, D])
        self.g_w = m.at("g_w", region[4] + 24 * BANK, [D, 2 * D])
        self.g_b = m.at("g_b", region[4] + 24 * BANK + 8 * D, [P, D])
        self.g_xw = m.at("g_xw", region[4] + 24 * BANK + 12 * D, [P, PER, D])
        self.g_dv = m.at("g_dv", region[4] + 24 * BANK + 28 * D, [P, 1])
        self.x1 = m.new("x1", [P, NB, D])
        self.n1 = m.new("n1", [P, NB, D])
        self.ident = m.new("ident", [P, P])
        self.sel = m.new("sel", [P, P])
        self.stat_blk = [m.new(f"stat_blk{r}", [P, P], FP32R) for r in range(2)]
        self.e_blk = [m.new(f"e_blk{r}", [P, D]) for r in range(2)]
        self.w_q8 = m.new("w_q8", [P, 2, 2 * D])
        self.b_q2 = m.new("b_q2", [P, 1])
        self.b_q8 = m.new("b_q8", [P, 1])
        self.ones = m.new("ones", [P, 1])
        self.squares = m.new("squares", [P, 2, NB])
        self.ssq_xw, self.sq_n = self.squares[:, 0, :], self.squares[:, 1, :]
        self.norms = m.at("norms", region[8] + (NQ - 1) * 4 * BANK, [P, 2, NB])
        self.inv_norms = m.at("inv_norms", region[8] + (NQ - 1) * 4 * BANK + 8 * NB, [P, 2, NB])
        self.feat_mag = m.new("feat_mag", [P, NB])
        self.structural = m.new("structural", [P, NB])
        self.rows = m.new("rows", [P, NB])
        self.rows2 = m.new("rows2", [P, NB])
        self.rows3 = m.new("rows3", [P, NB])
        self.comp_mask = m.new("comp_mask", [P, NB])
        self.z = m.new("z", [P, NB])
        self.rz = m.new("rz", [P, NB])
        self.inv_norm = m.new("inv_norm", [P, NB])
        self.conn = m.new("conn", [P, NB])
        self.par = m.new("par", [P, 4])
        self.parp = m.new("parp", [P, 2])
        self.bn = [m.new(f"bn{j}", [P, 6]) for j in range(2)]
        self.mv = m.new("mv", [P, 2, 2])
        self.pair = [m.new(f"pair{j}", [P, 2, 1]) for j in range(3)]
        self.one = [m.new(f"one{j}", [P, 1]) for j in range(4)]
        self.mx = m.new("mx", [P, len(CHUNKS_BESIDE)])
        self.nmax = [m.new(f"nmax{r}", [P, 1]) for r in range(2)]
        self.rz_blk = [m.new(f"rz_blk{r}", [P, 1]) for r in range(2)]
        self.row1 = m.new("row1", [1, P])
        self.ones_row = m.new("ones_row", [1, P])
        self.theta = m.new("theta", [D, D])
        self.flag = m.new("flag", [1, 1], INT32)
        self.ps = nc.alloc_psum_tensor("ps", [P, 8 * BANK], FP32)
        self.constants = self.sem("constants")

    def sem(self, name):
        assert name not in self.sems, name
        self.sems[name] = self.spare.pop(0) if self.spare else self.nc.alloc_semaphore(name)
        return self.sems[name]

    def fresh_semaphores(self):
        used = {sem.num: sem for name, sem in self.sems.items() if name != "constants"}
        with self.nc.Block() as block:
            @block.gpsimd
            def _(pool):
                first = min(used)
                for n in range(min(used), max(used) + 1):
                    if n + 1 not in used:
                        pool.sem_clear(range(first, n + 1))
                        first = n + 2

            for engine in (block.sync, block.scalar, block.vector, block.tensor):
                @engine
                def _(eng):
                    eng.wait_ge(self.constants, 1)
        self.sems = {"constants": self.constants}
        self.spare = [used[n] for n in sorted(used)]

    def sem_list(self, name, n):
        return [self.sem(f"{name}{j}") for j in range(n)]

    def bank(self, b, cols=BANK, first=0, rows=slice(0, P)):
        return self.ps[rows, b * BANK + first:b * BANK + first + cols]

    def half_acc(self, q, cols=BANK, first=0):
        return self.bank(q // 2, cols, first, slice(D * (q % 2), D * (q % 2) + D))


def load_ring(k, eng, src, loaded, used, ring, down, resident, per=1):
    def load(s, r, turn):
        if isinstance(s, int) and s < ring:
            if resident:
                return
        else:
            wait_alone(eng, used, (s - ring + 1) * per, k.constants)
        b = NB - 1 - s if down else s
        blk = src[b] if isinstance(b, int) else src[bass.ds(b, 1), :, :].rearrange("a p n -> (a p) n")
        eng.dma_start(k.ring[slot_of(r, ring, down)][:], blk).then_inc(loaded[r], 16)
    steps(eng, load, ring, NB)


def slot_of(r, ring, down):
    return (NB - 1 - r if down else r) % ring


def wait_loaded(eng, loaded, r, turn, resident):
    at_least(eng, loaded[r], 16 * turn + (0 if resident else 16))


def column_pass(k, tag, src, operand, ring, down=False, resident=False, degrees=False,
                first=None, between=None):
    nc = k.nc
    loaded, used = k.sem_list(f"{tag}_loaded", ring), k.sem(f"{tag}_used")
    placed = k.sem(f"{tag}_operand_placed")
    first, between = first or {}, between or {}
    with nc.Block() as block:
        @block.sync
        def _(sp):
            if "sync" in first:
                first["sync"](sp)
            load_ring(k, sp, src, loaded, used, ring, down, resident)

        @block.gpsimd
        def _(pool):
            if "gpsimd" in first:
                first["gpsimd"](pool)

        @block.scalar
        def _(act):
            if "scalar" in first:
                first["scalar"](act)

            def place(s, r, turn):
                if "scalar" in between and isinstance(s, int) and s < ring:
                    between["scalar"](act, s)
                if not (isinstance(s, int) and s < 2):
                    act.wait_ge(used, s - 1)
                nc.scalar.activation(k.e_blk[r % 2][:], block_of(operand, NB - 1 - s if down else s),
                                     ACT.Copy).then_inc(placed, 1)
            steps(act, place, ring, NB)

        @block.vector
        def _(dve):
            if "vector" in first:
                first["vector"](dve)

        @block.tensor
        def _(pe):
            if "tensor" in first:
                first["tensor"](pe)

            def product(s, r, turn):
                if "tensor" in between and isinstance(s, int) and s < ring:
                    between["tensor"](pe, s)
                pe.wait_ge(placed, s + 1)
                wait_loaded(pe, loaded, r, turn, resident)
                rows = k.ring[slot_of(r, ring, down)]
                begin = isinstance(s, int) and s == 0
                for q in range(NQ):
                    done = nc.tensor.matmul(k.half_acc(q), k.e_blk[r % 2][:], rows[:, q * BANK:(q + 1) * BANK],
                                            start=begin, stop=True, skip_group_check=True)
                if degrees:
                    for q in range(NQ):
                        done = nc.tensor.matmul(k.bank(5 + q // 4, rows=slice(32 * (q % 4), 32 * (q % 4) + 1)),
                                                k.ones[:], rows[:, q * BANK:(q + 1) * BANK],
                                                start=begin, stop=True, skip_group_check=True)
                done.then_inc(used, 1)
            steps(pe, product, ring, NB)


def by_blocks(k, tag, wide, tall, scale=None):
    nc = k.nc
    out, turned, read = k.sem(f"{tag}_out"), k.sem(f"{tag}_turned"), k.sem(f"{tag}_read")
    tall_v = tall[:].rearrange("p (q h m) d -> p q h m d", h=2, m=PER)
    with nc.Block() as block:
        @block.scalar
        def _(act):
            for b in range(NQ // 2):
                nc.scalar.activation(wide[:, b * BANK:(b + 1) * BANK], k.bank(b), ACT.Copy).then_inc(out, 1)

        @block.tensor
        def _(pe):
            for b in range(NQ // 2):
                pe.wait_ge(out, b + 1)
                at_least(pe, read, b - 1)
                for m in range(PER):
                    c = b * BANK + m * P
                    done = nc.tensor.transpose(k.bank(6 + b % 2, P, m * P), wide[:, c:c + P], k.ident[:])
                done.then_inc(turned, 1)

        @block.vector
        def _(dve):
            for b in range(NQ // 2):
                dve.wait_ge(turned, b + 1)
                for h in range(2):
                    src = k.bank(6 + b % 2).rearrange("p (m h d) -> p m h d", h=2, d=D)[:, :, h, :]
                    if scale is None:
                        done = nc.vector.tensor_copy(tall_v[:, b, h], src)
                    else:
                        s = scale[:].rearrange("p (q h m) -> p q h m", h=2, m=PER)[:, b, h]
                        done = nc.vector.tensor_tensor(tall_v[:, b, h], src,
                                                       s.unsqueeze(2).to_broadcast([P, PER, D]), ALU.mult)
                done.then_inc(read, 1)
            dve.wait_ge(read, NQ // 2)



def embed_and_columns(k):
    nc, i = k.nc, k.i
    PARTS = 5
    BP = NB // PARTS
    s_x, s_par = k.sem_list("x_loaded", PARTS), k.sem("embed_weights")
    own, pool_own = k.sem("embed_own"), k.sem("constants_own")
    ln_var, ln_sd, h_ready, const_ready = k.sem("embed_var"), k.sem("embed_sd"), k.sem("h_ready"), k.constants
    ht_done, ht_copied, hw_done, e_ready = k.sem("ht_done"), k.sem("ht_copied"), k.sem("hw_done"), k.sem("e_ready")
    diag_t = k.sem("diag_transposed")
    N_PAR = 7
    HT_BANKS, HW_BANK, DIAG_BANK = (5, 6), 7, 0

    def blocks(part):
        return slice(part * BP, (part + 1) * BP)

    def sync(sp):
        for part in range(PARTS):
            sp.dma_start(k.xin[:, blocks(part), :], k.x_v[:, blocks(part), :]).then_inc(s_x[part], 16)

    def gpsimd(pool):
        nc.gpsimd.memset(k.ones[:], 1.0).then_inc(const_ready, 1)
        nc.gpsimd.memset(k.ones_row[:], 1.0).then_inc(const_ready, 1)
        link = Chain(pool, pool_own)
        link(nc.gpsimd.memset(k.ident[:], 0.0))
        link(nc.gpsimd.memset(k.sel[:], 0.0))
        for tensor, base in ((k.ident, 0), (k.sel, 0), (k.sel, D), (k.sel, -D)):
            ins = nc.gpsimd.affine_select(out=tensor[:], in_=tensor[:], compare_op=ALU.not_equal, fill=1.0,
                                          base=base, pattern=[[-1, P]], channel_multiplier=1)
            link(ins)

    def root(act, part):
        act.wait_ge(ln_var, part + 1)
        nc.scalar.activation(k.rows2[:, blocks(part)], k.rows[:, blocks(part)], ACT.Sqrt).then_inc(ln_sd, 1)

    def copy_transposes(act, part):
        for j in range(2):
            act.wait_ge(ht_done, 2 * part + j + 1)
            at_least(act, hw_done, part)
            nc.scalar.activation(k.h_t[j][:], k.bank(HT_BANKS[j], rows=slice(0, D)), ACT.Copy).then_inc(ht_copied, 1)

    def scalar(act):
        for dst, src in ((k.w_ui[0][:], i["W_u"]), (k.w_ui[1][:], i["W_i"]),
                         (k.diag_rows[0:UB, :], i["diag_u"].rearrange("(b p) -> b p", p=P)),
                         (k.diag_rows[UB:NB, :], i["diag_i"].rearrange("(b p) -> b p", p=P)),
                         (k.par[:, 0:2], i["par_u"].partition_broadcast(P)),
                         (k.par[:, 2:4], i["par_i"].partition_broadcast(P)),
                         (k.beta[:], i["ln_beta"].partition_broadcast(P))):
            act.dma_start(dst, src).then_inc(s_par, 16)
        root(act, 0)
        copy_transposes(act, 0)
        root(act, 1)
        act.wait_ge(e_ready, 1)

    def scalar_between(act, s):
        if 2 <= s <= PARTS:
            copy_transposes(act, s - 1)
        if 2 <= s < PARTS:
            root(act, s)
        if s == PARTS:
            act.wait_ge(e_ready, PARTS)

    def vector(dve):
        link = Chain(dve, own)

        def norm(part):
            b = blocks(part)
            shape = [P, BP, D]
            x, xc, sq = k.xin[:, b, :], k.xc[:, b, :], k.sq[:, b, :]
            rows, rows2, rows3 = k.rows[:, b], k.rows2[:, b], k.rows3[:, b]
            dve.wait_ge(s_x[part], 16)
            link(nc.vector.reduce_sum(rows3, x, AX.X))
            link(nc.vector.tensor_scalar(rows3, rows3, 1.0 / D, None, ALU.mult))
            link(nc.vector.tensor_tensor(xc, x, rows3.unsqueeze(2).to_broadcast(shape), ALU.subtract))
            link(nc.vector.tensor_tensor(sq, xc, xc, ALU.mult))
            link(nc.vector.reduce_sum(rows, sq, AX.X))
            nc.vector.tensor_scalar(rows, rows, 1.0 / D, LN_EPS, ALU.mult, ALU.add).then_inc(ln_var, 1)
            dve.wait_ge(ln_var, part + 1)
            dve.wait_ge(ln_sd, part + 1)
            inv_sqrt(nc, link, rows2, rows, rows2, rows3)
            link(nc.vector.tensor_tensor(xc, xc, rows2.unsqueeze(2).to_broadcast(shape), ALU.mult))
            nc.vector.tensor_scalar(k.h[:, b, :], xc, 0.0, None, ALU.max).then_inc(h_ready, 1)

        def embed(part):
            dve.wait_ge(hw_done, part + 1)
            b = blocks(part)
            hw = k.bank(HW_BANK).rearrange("p (b d) -> p b d", d=D)
            link(nc.vector.tensor_tensor(k.emb[:, b, :], hw, k.structural[:, b].unsqueeze(2).to_broadcast([P, BP, D]), ALU.mult))
            nc.vector.tensor_tensor(k.emb[:, b, :], k.emb[:, b, :], k.h[:, b, :], ALU.add).then_inc(e_ready, 1)

        norm(0)
        dve.wait_ge(s_par, N_PAR * 16)
        link(nc.vector.tensor_tensor(k.parp[:, 0:1], k.par[:, 0:1], k.par[:, 1:2], ALU.mult))
        link(nc.vector.tensor_tensor(k.parp[:, 1:2], k.par[:, 2:3], k.par[:, 3:4], ALU.mult))
        dve.wait_ge(diag_t, 1)
        link(nc.vector.tensor_scalar(k.structural[:, 0:UB], k.bank(DIAG_BANK, UB), k.parp[:, 0:1], None, ALU.mult))
        link(nc.vector.tensor_scalar(k.structural[:, UB:NB], k.bank(DIAG_BANK, NB - UB, UB), k.parp[:, 1:2], None, ALU.mult))
        for part in range(1, PARTS):
            norm(part)
            embed(part - 1)
        embed(PARTS - 1)
        dve.wait_ge(h_ready, PARTS)
        whole = [P, NB, D]
        link(nc.vector.tensor_tensor(k.x1[:], k.xin[:], k.beta[:].unsqueeze(1).to_broadcast(whole), ALU.add))
        link(nc.vector.tensor_tensor(k.x1[:], k.x1[:], k.h[:], ALU.add))

    def weights_products(pe, part):
        pe.wait_ge(h_ready, part + 1)
        at_least(pe, ht_copied, 2 * part)
        for j in range(2):
            for m in range(PER):
                done = nc.tensor.transpose(k.bank(HT_BANKS[j], P, m * P, slice(0, D)),
                                           k.h[:, part * BP + j * PER + m, :], k.ident[:])
            done.then_inc(ht_done, 1)
        pe.wait_ge(ht_copied, 2 * part + 2)
        at_least(pe, e_ready, part)
        for n in range(BP):
            done = nc.tensor.matmul(k.bank(HW_BANK, D, n * D), k.h_t[n // PER][:, n % PER * P:(n % PER + 1) * P],
                                    k.w_ui[0 if part * BP + n < UB else 1][:], start=True, stop=True)
        done.then_inc(hw_done, 1)

    def tensor(pe):
        pe.wait_ge(pool_own, 3)
        pe.wait_ge(s_par, N_PAR * 16)
        nc.tensor.transpose(k.bank(DIAG_BANK, NB), k.diag_rows[:], k.ident[0:NB, 0:NB]).then_inc(diag_t, 1)
        weights_products(pe, 0)

    def tensor_between(pe, s):
        if 1 <= s < PARTS:
            weights_products(pe, s)

    column_pass(k, "a1", k.adj_v, k.emb, RING_A,
                first={"sync": sync, "gpsimd": gpsimd, "scalar": scalar, "vector": vector, "tensor": tensor},
                between={"scalar": scalar_between, "tensor": tensor_between})
    by_blocks(k, "col", k.col_t, k.col)


def network_and_features(k):
    nc, i = k.nc, k.i
    s_par, zeroed = k.sem("feature_weights"), k.sem("feature_zeros")
    loaded, used = k.sem_list("pair_loaded", RING_A), k.sem("pair_used")
    t_ready, t_copied = k.sem("transposed"), k.sem("transposed_copied")
    h2_done, h2_copied = k.sem("h2_done"), k.sem("h2_copied")
    back, back_read = k.sem("h2_back"), k.sem("h2_back_read")
    var, root, own = k.sem("pair_var"), k.sem("pair_root"), k.sem("pair_own")
    n_ready, n_saved = k.sem("n_ready"), k.sem("n_saved")
    nt_done, nt_copied = k.sem("nt_done"), k.sem("nt_copied")
    q_done, q_hi, q_lo, scaled = k.sem("q_done"), k.sem("q_hi"), k.sem("q_lo"), k.sem("wq_scaled")
    v_done, v_ready, xw_own = k.sem("v_done"), k.sem("v_ready"), k.sem("xw_own")
    N_PAR = 13
    BACK_AT, ROOTS_AT, N_AT, V_AT, Q_AT = 2, (5, 9), 13, 14, 16
    FEATURE_UNITS = [0] * 15 + [2] * 5
    order = list(range(BACK_AT + 1)) + ["back"] + list(range(BACK_AT + 1, N_AT + 1)) + ["n"] \
        + list(range(N_AT + 1, V_AT + 1)) + ["v"] + list(range(V_AT + 1, Q_AT + 1)) + ["q"] \
        + list(range(Q_AT + 1, TGS))
    assert len(order) % 2 == 0
    bank_of = {event: 5 + j % 2 for j, event in enumerate(order)}

    def last_in_bank(event, before):
        earlier = [e for e in order[:order.index(event)] if bank_of[e] == bank_of[event] and (before or isinstance(e, int))]
        return earlier[-1] if earlier else None

    BACK_BANK, NT_BANK, V_BANK, Q_BANK, H2_BANK = bank_of["back"], bank_of["n"], bank_of["v"], bank_of["q"], 7

    def pair_of(tensor, p):
        b = NB - 2 - 2 * p
        return tensor[:, b:b + 2, :] if isinstance(b, int) else tensor[:, bass.ds(b, 2), :]

    with nc.Block() as block:
        @block.sync
        def _(sp):
            sp.wait_ge(zeroed, 3)
            for dst, src in ((k.gamma[:], i["ln_gamma"].partition_broadcast(P)),
                             (k.w_vw[0:D, 0, 0:D], i["Wv"]), (k.w_vw[0:D, 0, D:2 * D], i["W"]),
                             (k.w_vw[D:P, 1, 0:D], i["Wv"]), (k.w_vw[D:P, 1, D:2 * D], i["W"]),
                             (k.b_vw[:, 0:D], i["bv"].partition_broadcast(P)),
                             (k.w_q8[0:D, 0, 0:D], i["Wq"]), (k.w_q8[0:D, 0, D:2 * D], i["Wq"]),
                             (k.w_q8[D:P, 1, 0:D], i["Wq"]), (k.w_q8[D:P, 1, D:2 * D], i["Wq"]),
                             (k.b_q2[0:D, :], i["bq"].rearrange("(d a) -> d a", a=1)),
                             (k.b_q2[D:P, :], i["bq"].rearrange("(d a) -> d a", a=1)),
                             (k.theta[:], i["Theta"])):
                sp.dma_start(dst, src).then_inc(s_par, 16)
            load_ring(k, sp, k.adj_v, loaded, used, RING_A, True, True)

        @block.gpsimd
        def _(pool):
            nc.gpsimd.memset(k.w_vw[:], 0.0).then_inc(zeroed, 1)
            nc.gpsimd.memset(k.b_vw[:], 0.0).then_inc(zeroed, 1)
            nc.gpsimd.memset(k.w_q8[:], 0.0).then_inc(zeroed, 1)

            def save(t, r, turn):
                pool.wait_ge(n_ready, t + 1)
                nc.gpsimd.tensor_copy(pair_of(k.n1, t), k.ln_out[:]).then_inc(n_saved, 1)
            steps(pool, save, 1, PAIRS)

        @block.scalar
        def _(act):
            def step(p, r, turn):
                now = not (isinstance(p, int) and p == PAIRS)
                before = not (isinstance(p, int) and p == 0)

                def copy_group(g):
                    act.wait_ge(t_ready, TGS * p + g + 1)
                    nc.scalar.activation(k.adj_t[g % T_BUFS][:], k.bank(bank_of[g]), ACT.Copy).then_inc(t_copied, 1)

                for g in range(TGS):
                    if before and g == 1:
                        act.wait_ge(h2_done, p)
                        at_least(act, back, p - 1)
                        nc.scalar.activation(k.h2_t[:], k.bank(H2_BANK, 2 * P), ACT.Copy).then_inc(h2_copied, 1)
                    if now:
                        copy_group(g)
                    if before and g in ROOTS_AT:
                        act.wait_ge(var, 2 * (p - 1) + ROOTS_AT.index(g) + 1)
                        nc.scalar.activation(k.pair[1][:], k.pair[0][:], ACT.Sqrt).then_inc(root, 1)
                    if before and g == N_AT:
                        act.wait_ge(nt_done, p)
                        nc.scalar.activation(k.n_t[:], k.bank(NT_BANK, P), ACT.Copy).then_inc(nt_copied, 1)
                    if before and g == V_AT + 2:
                        act.wait_ge(v_ready, p)
                        for j in range(2):
                            b = NB - 2 - 2 * (p - 1) + j
                            nc.scalar.activation(k.xw_sq[:, 0:D], k.vw[:, j, D:2 * D], ACT.Square,
                                                 accum_out=columns(k.ssq_xw, b, 1)).then_inc(xw_own, 1)
                            act.wait_ge(xw_own, 4 * (p - 1) + 2 * j + 1)
                            nc.scalar.activation(k.xw_sq[:, 0:D], k.ln_out[:, j, :], ACT.Square,
                                                 accum_out=columns(k.sq_n, b, 1)).then_inc(xw_own, 1)
                            act.wait_ge(xw_own, 4 * (p - 1) + 2 * j + 2)
                    if before and g == Q_AT + 1:
                        act.wait_ge(q_done, p)
                        nc.scalar.activation(columns(k.stat_op, (NB - 2 * p) * P, 2 * P), k.bank(Q_BANK, 2 * P), ACT.Identity,
                                             bias=k.b_q8[:], scale=1.0).then_inc(q_hi, 1)
            steps(act, step, 1, PAIRS + 1, peel=2, tail=1)

        @block.vector
        def _(dve):
            link = Chain(dve, own)
            two = [P, 2, D]
            dve.wait_ge(s_par, N_PAR * 16)
            link(nc.vector.tensor_scalar(k.b_q8[:], k.b_q2[:], 1.0 / 8, None, ALU.mult))
            link(nc.vector.tensor_scalar(k.w_q8[:], k.w_q8[:], 1.0 / 8, None, ALU.mult))
            nc.vector.tensor_copy(k.pair[2][:], k.ones[:].unsqueeze(1).to_broadcast([P, 2, 1])).then_inc(scaled, 1)
            OPS = 25

            def norm(t, which):
                for j in range(2):
                    link(nc.vector.bn_stats(k.bn[j][:], k.ln_in[:, j, :]), k.constants)
                for j in range(2):
                    link(nc.vector.bn_aggr(k.mv[:, j, :], k.bn[j][:]), k.constants)
                nc.vector.tensor_scalar(k.pair[0][:], k.mv[:, :, 1:2], LN_EPS, None, ALU.add).then_inc(var, 1)
                dve.wait_ge(root, 2 * t + which + 1)
                inv_sqrt(nc, link, k.pair[1][:], k.pair[0][:], k.pair[1][:], k.pair[2][:])
                link(nc.vector.tensor_tensor(k.ln_out[:], k.ln_in[:], k.mv[:, :, 0:1].to_broadcast(two), ALU.subtract))
                link(nc.vector.tensor_tensor(k.ln_out[:], k.ln_out[:], k.pair[1][:].to_broadcast(two), ALU.mult))

            def step(t, r, turn):
                link.restart(2 + OPS * t)
                dve.wait_ge(back, t + 1)
                nc.vector.tensor_copy(k.ln_in[:], k.bank(BACK_BANK, P)).then_inc(back_read, 1)
                dve.wait_ge(back_read, t + 1)
                at_least(dve, n_saved, t)
                at_least(dve, nt_done, t)
                at_least(dve, xw_own, 4 * t)
                norm(t, 0)
                link(nc.vector.tensor_tensor(k.ln_out[:], k.ln_out[:], k.gamma[:].unsqueeze(1).to_broadcast(two), ALU.mult), k.constants)
                link(nc.vector.tensor_tensor(k.ln_in[:], k.ln_out[:], pair_of(k.x1, t), ALU.add), k.constants)
                norm(t, 1)
                nc.vector.tensor_scalar(k.ln_out[:], k.ln_out[:], 0.0, None, ALU.max).then_inc(n_ready, 1)
                wait_alone(dve, n_ready, t + 1, k.constants)
                link(nc.vector.tensor_copy(pair_of(k.x1, t), k.ln_in[:]))
                dve.wait_ge(v_done, t + 1)
                at_least(dve, used, 2 * t)
                at_least(dve, xw_own, 4 * t)
                nc.vector.tensor_tensor(k.vw[:], k.bank(V_BANK, 4 * D).rearrange("p (j c) -> p j c", j=2),
                                        k.b_vw[:].unsqueeze(1).to_broadcast([P, 2, 2 * D]), ALU.add).then_inc(v_ready, 1)
                wait_alone(dve, q_hi, t + 1, k.constants)
                low, cols = slice(D, P), (NB - 2 - 2 * t) * P
                op = k.stat_op[low, cols:cols + 2 * P] if isinstance(cols, int) else k.stat_op[low, bass.ds(cols, 2 * P)]
                nc.vector.scalar_tensor_tensor(op, k.bank(Q_BANK, 2 * P, rows=low), k.b_q8[low, :], op.bitcast(FP32),
                                               ALU.add, ALU.subtract).then_inc(q_lo, 1)
                assert link.n == OPS, link.n
            steps(dve, step, 1, PAIRS)

        @block.tensor
        def _(pe):
            def slots(r):
                b = (NB - 2 - 2 * r) % RING_A
                return k.ring[b], k.ring[b + 1]

            def step(p, r, turn):
                now = not (isinstance(p, int) and p == PAIRS)
                before = not (isinstance(p, int) and p == 0)
                blocks = slots(r)
                late = isinstance(p, int) and p == PAIRS - 1

                def bank_free(event):
                    e = last_in_bank(event, before)
                    if e == "back":
                        pe.wait_ge(back_read, p)
                    elif e == "n":
                        pe.wait_ge(nt_copied, p)
                    elif e == "v":
                        pe.wait_ge(v_ready, p)
                    elif e == "q":
                        pe.wait_ge(q_lo, p)
                    elif now:
                        at_least(pe, t_copied, TGS * p + (event - 1 if e is None else e + 1))

                def transposes(g, c):
                    if c == 0:
                        bank_free(g)
                    if g == 0 and c == 0:
                        for j in (1, 0):
                            wait_loaded(pe, loaded, 2 * r + 1 - j, turn, True)
                    for j in range(2):
                        col = (2 * g + c) * P
                        done = nc.tensor.transpose(k.bank(bank_of[g], P, (2 * c + j) * P),
                                                   blocks[j][:, col:col + P], k.ident[:])
                    if c == 1:
                        done.then_inc(t_ready, 1)

                def product(q, g):
                    pe.wait_ge(t_copied, TGS * q + g + 1)
                    if g == 0:
                        at_least(pe, h2_copied, q)
                    for c in range(2):
                        done = nc.tensor.matmul(k.bank(H2_BANK, 2 * P, 0, slice(D * c, D * c + D)), k.col[:, 2 * g + c, :],
                                                k.adj_t[g % T_BUFS][:, 2 * P * c:2 * P * (c + 1)],
                                                start=g == 0, stop=g == TGS - 1)
                    if g == TGS - 1:
                        done.then_inc(h2_done, 1)

                def features(n, ago=1):
                    old = slots((r - ago) % PAIR_SLOTS)
                    j = 1 - n // (NQ // 2)
                    if n == 0:
                        pe.wait_ge(v_ready, p - ago + 1)
                    for q in range(2 * n % NQ, 2 * n % NQ + 2):
                        done = nc.tensor.matmul(k.half_acc(q), k.vw[:, j, 0:D], old[j][:, q * BANK:(q + 1) * BANK],
                                                start=isinstance(p, int) and p == 1 and n < NQ // 2, stop=True,
                                                skip_group_check=True)
                    if n % (NQ // 2) == NQ // 2 - 1:
                        done.then_inc(used, 1)

                unit = 0
                for g in range(TGS):
                    if g < 2 and before:
                        product(p - 1, TGS - 2 + g)
                    if now:
                        transposes(g, 0)
                        transposes(g, 1)
                    if g >= 2 and now:
                        product(p, g - 2)
                    if before and not late:
                        for _ in range(FEATURE_UNITS[g]):
                            features(unit)
                            unit += 1
                    if before and g == BACK_AT:
                        pe.wait_ge(h2_copied, p)
                        bank_free("back")
                        for j in range(2):
                            done = nc.tensor.matmul(k.bank(BACK_BANK, D, j * D), k.h2_t[:, j * P:(j + 1) * P],
                                                    k.sel[:, 0:D], start=True, stop=True)
                        done.then_inc(back, 1)
                        if not now:
                            for n in range(NQ):
                                features(n, ago=2)
                    if before and g == N_AT:
                        pe.wait_ge(n_ready, p)
                        bank_free("n")
                        nc.tensor.transpose(k.bank(NT_BANK, P), k.ln_out[:].rearrange("p j d -> p (j d)"),
                                            k.ident[:]).then_inc(nt_done, 1)
                    if before and g == V_AT:
                        pe.wait_ge(nt_copied, p)
                        bank_free("v")
                        nc.tensor.matmul(k.bank(V_BANK, 4 * D), k.n_t[:], k.w_vw[:].rearrange("p j c -> p (j c)"),
                                         start=True, stop=True).then_inc(v_done, 1)
                    if before and g == Q_AT:
                        bank_free("q")
                        for j in range(2):
                            done = nc.tensor.matmul(k.bank(Q_BANK, P, j * P), k.w_q8[:, j, :], k.n_t[:], start=True, stop=True)
                        done.then_inc(q_done, 1)
                if not before:
                    pe.wait_ge(s_par, N_PAR * 16)
                    pe.wait_ge(scaled, 1)
            steps(pe, step, PAIR_SLOTS, PAIRS + 1, tail=2)



def features_operand(k, tag):
    nc = k.nc
    hi_done, lo_done, moved = k.sem(f"{tag}_hi"), k.sem(f"{tag}_lo"), k.sem(f"{tag}_lo_moved")
    own, root = k.sem(f"{tag}_own"), k.sem(f"{tag}_roots")

    def half(q):
        return slice(D * (q % 2), D * (q % 2) + D)

    def chunk(q):
        return slice(q * BANK, (q + 1) * BANK)

    with nc.Block() as block:
        @block.scalar
        def _(act):
            act.wait_ge(own, 1)
            nc.scalar.activation(k.inv_norms[:], k.squares[:], ACT.Sqrt).then_inc(root, 1)
            for q in range(NQ):
                for rows in (half(q), half(q + 1)):
                    nc.scalar.activation(k.mov_hi[rows, chunk(q)], k.half_acc(q), ACT.Copy).then_inc(hi_done, 1)

        @block.gpsimd
        def _(pool):
            for q in range(1, NQ, 2):
                pool.wait_ge(lo_done, q + 1)
                nc.gpsimd.tensor_copy(k.mov_lo[half(q + 1), chunk(q)], k.mov_lo[half(q), chunk(q)]).then_inc(moved, 1)

        @block.vector
        def _(dve):
            link = Chain(dve, own)
            link(nc.vector.tensor_scalar(k.squares[:], k.squares[:], NORM_MIN, None, ALU.max))
            dve.wait_ge(root, 1)
            inv_sqrt(nc, link, k.inv_norms[:], k.squares[:], k.inv_norms[:], k.norms[:])
            link(nc.vector.tensor_tensor(k.norms[:], k.inv_norms[:], k.squares[:], ALU.mult))
            link(nc.vector.tensor_scalar(k.structural[:], k.norms[:, 0, :], 0.5, None, ALU.mult))
            link(nc.vector.tensor_copy(k.feat_mag[:], k.norms[:, 1, :]))
            link(nc.vector.tensor_scalar(k.rows3[:], k.feat_mag[:], 1e-8, None, ALU.max))
            link(nc.vector.reciprocal(k.inv_norm[:], k.rows3[:]))
            for q in range(NQ):
                dve.wait_ge(hi_done, 2 * q + 2)
                nc.vector.tensor_tensor(k.mov_lo[half(q), chunk(q)], k.half_acc(q),
                                        k.mov_hi[half(q), chunk(q)].bitcast(FP32), ALU.subtract).then_inc(lo_done, 1)
                if q % 2 == 0:
                    dve.wait_ge(lo_done, q + 1)
                    nc.vector.tensor_copy(k.mov_lo[half(q + 1), chunk(q)], k.mov_lo[half(q), chunk(q)]).then_inc(moved, 1)


def scores(k, chunks, bufs, r, ch):
    return k.bank(chunks[(len(chunks) * r + ch) % bufs][2], chunks[ch][1])


def score_products(k, pe, out, stationary, first, cols):
    for part, begin in ((k.mov_hi, True), (k.mov_lo, False)):
        for c in range(0, cols, BANK):
            done = k.nc.tensor.matmul(out[:, c:c + BANK], stationary[:], part[:, first + c:first + c + BANK],
                                      start=begin, stop=not begin)
    return done


SUM_BANKS = ((0, 4), (16, 3), (28, 3))


def softmax_pass(k, tag, attention, first_slot, loaded, ready, following=None, first_sync=None):
    nc = k.nc
    stat_ready = k.sem(f"{tag}_stat")
    scored, masked, neg_max = k.sem(f"{tag}_scored"), k.sem(f"{tag}_times_adj"), k.sem(f"{tag}_max")
    exp_done, rz_ready, summed = k.sem(f"{tag}_exp"), k.sem(f"{tag}_rz"), k.sem(f"{tag}_summed")
    zeroed = k.sem(f"{tag}_sums_zeroed")
    used = summed if attention else exp_done
    chunks = CHUNKS_BESIDE if attention else CHUNKS
    NCH, bufs = len(chunks), 3
    LAG = 2

    def rows_of(r):
        return k.ring[(first_slot + r) % RING_A]

    with nc.Block() as block:
        @block.sync
        def _(sp):
            if first_sync is not None:
                first_sync(sp)

            def load(s, r, turn):
                if isinstance(s, int) and s < RING_A:
                    return
                wait_alone(sp, used, s - RING_A + 1, k.constants)
                blk = k.adj_v[s] if isinstance(s, int) else k.adj_v[bass.ds(s, 1), :, :].rearrange("a p n -> (a p) n")
                sp.dma_start(rows_of(r)[:], blk).then_inc(loaded[r], 16)
            steps(sp, load, RING_A, NB)
            if following is not None:
                for s in range(RING_A):
                    sp.wait_ge(used, NB + s - RING_A + 1)
                    sp.dma_start(rows_of(NB + s)[:], k.adj_v[s]).then_inc(following[s], 16)

        @block.gpsimd
        def _(pool):
            def step(s, r, turn):
                if not (isinstance(s, int) and s < 2):
                    pool.wait_ge(scored, NCH * (s - 1))
                c = s * P
                if attention:
                    nc.gpsimd.tensor_copy(k.stat_blk[r % 2][:], columns(k.stat_op, c, P)).then_inc(stat_ready, 2)
                else:
                    for half, part in ((slice(0, D), k.mov_hi), (slice(D, P), k.mov_lo)):
                        src = part[half, c:c + P] if isinstance(c, int) else part[half, bass.ds(c, P)]
                        nc.gpsimd.tensor_copy(k.stat_blk[r % 2][half, :], src).then_inc(stat_ready, 1)
            steps(pool, step, RING_A, NB)

        @block.tensor
        def _(pe):
            def step(s, r, turn):
                now = not (isinstance(s, int) and s >= NB)
                before = attention and not (isinstance(s, int) and s < LAG)
                if now:
                    pe.wait_ge(stat_ready, 2 * s + 2)
                for ch, (start, cols, _) in enumerate(chunks):
                    if now:
                        at_least(pe, masked, NCH * s + ch - bufs + 1)
                        score_products(k, pe, scores(k, chunks, bufs, r, ch), k.stat_blk[r % 2], start, cols).then_inc(scored, 1)
                    if before and ch % 2 == 1:
                        if ch == 1:
                            pe.wait_ge(rz_ready, s - LAG + 1)
                            if isinstance(s, int) and s == LAG:
                                pe.wait_ge(zeroed, 1)
                        first_block, per = SUM_BANKS[ch // 2]
                        for h in range(4):
                            c = (first_block + h * per) * P
                            done = nc.tensor.matmul(k.bank(4 + ch // 2, per * P, rows=slice(32 * h, 32 * h + 1)),
                                                    k.rz_blk[(r - LAG) % 2][:], rows_of(r - LAG)[:, c:c + per * P],
                                                    start=isinstance(s, int) and s == LAG, stop=True, skip_group_check=True)
                if before:
                    done.then_inc(summed, 1)
            steps(pe, step, RING_A, NB + (LAG if attention else 0), tail=LAG if attention else 0)

        @block.scalar
        def _(act):
            def step(s, r, turn):
                act.wait_ge(neg_max, s + 1)
                w = rows_of(r)
                nc.scalar.activation(w[:], w[:], ACT.Exp, bias=k.nmax[r % 2][:],
                                     accum_out=columns(k.z, s, 1)).then_inc(exp_done, 1)
            steps(act, step, RING_A, NB)

        @block.vector
        def _(dve):
            if attention:
                nc.vector.memset(k.bank(4, 3 * BANK), 0.0).then_inc(zeroed, 1)

            def inverse(s, r):
                at_least(dve, summed, s - LAG)
                wait_alone(dve, exp_done, s, k.constants)
                nc.vector.reciprocal(k.rz_blk[(r - 1) % 2][:], columns(k.z, s - 1, 1)).then_inc(rz_ready, 1)

            def step(s, r, turn):
                if isinstance(s, int) and s == NB:
                    inverse(s, r)
                    return
                wait_loaded(dve, loaded, r, turn, ready)
                if not attention:
                    at_least(dve, exp_done, s - 1)
                rows = rows_of(r)
                for ch, (start, width, _) in enumerate(chunks):
                    cols = slice(start, start + width)
                    wait_alone(dve, scored, NCH * s + ch + 1, k.constants)
                    nc.vector.tensor_tensor_reduce(out=rows[:, cols], in0=scores(k, chunks, bufs, r, ch), in1=rows[:, cols],
                                                   scale=1.0, scalar=LOWEST, op0=ALU.mult, op1=ALU.max,
                                                   accum_out=k.mx[:, ch:ch + 1]).then_inc(masked, 1)
                    if attention and ch == NCH - 2 and not (isinstance(s, int) and s == 0):
                        inverse(s, r)
                dve.wait_ge(masked, NCH * (s + 1))
                nc.vector.tensor_reduce(k.nmax[r % 2][:], k.mx[:, 0:NCH], AX.X, ALU.max, negate=True).then_inc(neg_max, 1)
                dve.wait_ge(neg_max, s + 1)
            steps(dve, step, RING_A, NB + (1 if attention else 0), tail=1 if attention else 0)
            if attention:
                dve.wait_ge(rz_ready, NB)


class Across:

    def __init__(self, k, tag, op, banks):
        self.k, self.op, self.banks = k, op, banks
        self.column, self.row = k.sem(f"{tag}_column"), k.sem(f"{tag}_row")
        self.one, self.spread, self.out = k.sem(f"{tag}_one"), k.sem(f"{tag}_spread"), k.sem(f"{tag}_out")

    def tensor(self, pe, column):
        k, nc = self.k, self.k.nc
        pe.wait_ge(self.column, 1)
        nc.tensor.transpose(k.bank(self.banks[0], P, rows=slice(0, 1)), column[:], k.ident[:]).then_inc(self.row, 1)
        pe.wait_ge(self.one, 1)
        nc.tensor.matmul(k.bank(self.banks[1], 1), k.ones_row[:], k.row1[0:1, 0:1], start=True, stop=True)\
            .then_inc(self.spread, 1)

    def vector(self, dve, out, sign=1.0):
        k, nc = self.k, self.k.nc
        dve.wait_ge(self.row, 1)
        nc.vector.tensor_reduce(k.row1[0:1, 0:1], k.bank(self.banks[0], P, rows=slice(0, 1)), AX.X, self.op)\
            .then_inc(self.one, 1)
        dve.wait_ge(self.spread, 1)
        nc.vector.tensor_scalar(out[:], k.bank(self.banks[1], 1), sign, None, ALU.mult).then_inc(self.out, 1)
        dve.wait_ge(self.out, 1)


def component_mask(k, tag, layer):
    nc = k.nc
    own, out, turned = k.sem(f"{tag}_own"), k.sem(f"{tag}_sums_out"), k.sem(f"{tag}_sums_turned")
    top = Across(k, f"{tag}_max", ALU.max, (3, 7))
    total = Across(k, f"{tag}_total", ALU.add, (3, 7))
    xn_ready, xn_turned = k.sem(f"{tag}_xn"), k.sem(f"{tag}_xn_turned")
    hi_done, lo_done = k.sem(f"{tag}_hi"), k.sem(f"{tag}_lo")
    groups = NB // PER

    with nc.Block() as block:
        @block.scalar
        def _(act):
            for bank in range(2):
                cols = SUM_BANKS[bank][1] * P
                nc.scalar.activation(k.colsum[:, bank * BANK:bank * BANK + cols], k.bank(4 + bank, cols), ACT.Copy)\
                  .then_inc(out, 1)
            act.wait_ge(top.out, 1)
            nc.scalar.activation(k.rows3[:], k.rows[:], ACT.Exp, bias=k.one[1][:], accum_out=k.one[0][:]).then_inc(total.column, 1)
            for g in range(groups):
                act.wait_ge(xn_turned, g + 1)
                nc.scalar.activation(k.mov_hi[:, g * BANK:(g + 1) * BANK], k.bank(4 + g % 4), ACT.Copy).then_inc(hi_done, 1)

        @block.tensor
        def _(pe):
            pe.wait_ge(out, 3)
            for bank, (_, per) in enumerate(SUM_BANKS):
                for m in range(per):
                    c = bank * BANK + m * P
                    done = nc.tensor.transpose(k.bank(bank, P, m * P), k.colsum[:, c:c + P], k.ident[:])
            done.then_inc(turned, 1)
            top.tensor(pe, k.one[0])
            total.tensor(pe, k.one[0])
            for g in range(groups):
                pe.wait_ge(xn_ready, g + 1)
                at_least(pe, lo_done, g - 3)
                for m in range(PER):
                    done = nc.tensor.transpose(k.bank(4 + g % 4, P, m * P), k.xn4[g % 4][:, m].rearrange("p t d -> p (t d)"),
                                               k.ident[:])
                done.then_inc(xn_turned, 1)

        @block.vector
        def _(dve):
            cols = SUM_BANKS[2][1] * P
            nc.vector.tensor_copy(k.colsum[:, 2 * BANK:2 * BANK + cols], k.bank(6, cols)).then_inc(out, 1)
            link = Chain(dve, own)
            dve.wait_ge(turned, 1)
            for bank, (first_block, per) in enumerate(SUM_BANKS):
                src = k.bank(bank, per * P).rearrange("p (m h c) -> p h m c", m=per, h=4)[:, :, :, 0]
                dst = k.rows[:, first_block:first_block + 4 * per].rearrange("p (h m) -> p h m", h=4)
                link(nc.vector.tensor_scalar(dst, src, 0.5 / N, None, ALU.mult))
            link(nc.vector.tensor_tensor(k.rows[:], k.rows[:], k.structural[:], ALU.add))
            nc.vector.reduce_max(k.one[0][:], k.rows[:], AX.X).then_inc(top.column, 1)
            top.vector(dve, k.one[1], -1.0)
            total.vector(dve, k.one[2])
            link(nc.vector.reciprocal(k.one[3][:], k.one[2][:]))
            link(nc.vector.tensor_scalar(k.comp_mask[:], k.rows3[:], k.one[3][:], THRESHOLDS[layer], ALU.mult, ALU.is_ge))
            link(nc.vector.tensor_tensor(k.rows[:], k.comp_mask[:], k.inv_norm[:], ALU.mult))

            def norm_rows(g):
                b = slice(g * PER, (g + 1) * PER)
                shape = [P, PER, 2, D]
                at_least(dve, xn_turned, g - 3)
                nc.vector.tensor_tensor(k.xn4[g % 4][:], k.n1[:, b, :].unsqueeze(2).to_broadcast(shape),
                                        k.rows[:, b].unsqueeze(2).unsqueeze(3).to_broadcast(shape), ALU.mult).then_inc(xn_ready, 1)

            AHEAD = 3
            for g in range(AHEAD):
                norm_rows(g)
            for g in range(groups):
                if g + AHEAD < groups:
                    norm_rows(g + AHEAD)
                cols = slice(g * BANK, (g + 1) * BANK)
                dve.wait_ge(hi_done, g + 1)
                nc.vector.tensor_tensor(k.mov_lo[:, cols], k.bank(4 + g % 4), k.mov_hi[:, cols].bitcast(FP32),
                                        ALU.subtract).then_inc(lo_done, 1)
            link(nc.vector.tensor_tensor(k.feat_mag[:], k.comp_mask[:], k.feat_mag[:], ALU.mult))
            link(nc.vector.tensor_scalar(k.feat_mag[:], k.feat_mag[:], 1e-8, None, ALU.max))


def any_edge(k, tag, layer):
    nc = k.nc
    own = k.sem(f"{tag}_own")
    top = Across(k, tag, ALU.max, (0, 1))
    with nc.Block() as block:
        @block.vector
        def _(dve):
            link = Chain(dve, own)
            link(nc.vector.reciprocal(k.rz[:], k.z[:]))
            link(nc.vector.tensor_tensor(k.rows[:], k.rz[:], k.comp_mask[:], ALU.mult))
            nc.vector.reduce_max(k.one[0][:], k.rows[:], AX.X).then_inc(top.column, 1)
            top.vector(dve, k.one[1])
            link(nc.vector.tensor_scalar(k.flag[:], k.one[1][0:1, :], THRESHOLDS[layer] * 0.999, None, ALU.is_ge))

        @block.tensor
        def _(pe):
            top.tensor(pe, k.one[0])



def prune_pass(k, tag, threshold):
    nc = k.nc
    loaded, stat_ready = k.sem_list(f"{tag}_loaded", RING_B), k.sem(f"{tag}_stat")
    scored, masked, neg_max = k.sem(f"{tag}_scored"), k.sem(f"{tag}_times_adj"), k.sem(f"{tag}_max")
    exp_done, pruned, own = k.sem(f"{tag}_exp"), k.sem(f"{tag}_pruned"), k.sem(f"{tag}_own")
    stored = k.sem_list(f"{tag}_stored", 2)
    NCH, bufs = len(CHUNKS), 4

    with nc.Block() as block:
        @block.sync
        def _(sp):
            def store(s, r):
                wait_alone(sp, pruned, s + 1, k.constants)
                blk = k.hp_v[s] if isinstance(s, int) else k.hp_v[bass.ds(s, 1), :, :].rearrange("a p n -> (a p) n")
                sp.dma_start(blk, k.work[r % 2][:]).then_inc(stored[r % 2], 16)

            def step(s, r, turn):
                if not (isinstance(s, int) and s < RING_B):
                    store(s - RING_B, r)
                blk = k.adj_v[s] if isinstance(s, int) else k.adj_v[bass.ds(s, 1), :, :].rearrange("a p n -> (a p) n")
                sp.dma_start(k.ring[r][:], blk).then_inc(loaded[r], 16)
            steps(sp, step, RING_B, NB)
            for s in range(NB - RING_B, NB):
                store(s, s % RING_B)
            for j in range(2):
                sp.wait_ge(stored[j], 16 * NB // 2)

        @block.gpsimd
        def _(pool):
            def step(s, r, turn):
                if not (isinstance(s, int) and s < 2):
                    pool.wait_ge(scored, NCH * (s - 1))
                c = s * P
                for half, part in ((slice(0, D), k.mov_hi), (slice(D, P), k.mov_lo)):
                    src = part[half, c:c + P] if isinstance(c, int) else part[half, bass.ds(c, P)]
                    nc.gpsimd.tensor_copy(k.stat_blk[r % 2][half, :], src).then_inc(stat_ready, 1)
            steps(pool, step, RING_B, NB)

        @block.tensor
        def _(pe):
            def step(s, r, turn):
                pe.wait_ge(stat_ready, 2 * s + 2)
                for ch, (start, cols, _) in enumerate(CHUNKS):
                    at_least(pe, masked, NCH * s + ch - bufs + 1)
                    score_products(k, pe, scores(k, CHUNKS, bufs, r, ch), k.stat_blk[r % 2], start, cols)\
                        .then_inc(scored, 1)
            steps(pe, step, RING_B, NB)

        @block.scalar
        def _(act):
            def step(s, r, turn):
                act.wait_ge(neg_max, s + 1)
                w = k.work[r % 2]
                nc.scalar.activation(w[:], w[:], ACT.Exp, bias=k.nmax[r % 2][:],
                                     accum_out=columns(k.z, s, 1)).then_inc(exp_done, 1)
            steps(act, step, RING_B, NB)

        @block.vector
        def _(dve):
            def finish(s, r):
                w, inverse = k.work[(r - 1) % 2], k.rz_blk[(r - 1) % 2]
                wait_alone(dve, exp_done, s, k.constants)
                nc.vector.reciprocal(inverse[:], columns(k.z, s - 1, 1)).then_inc(own, 1)
                wait_alone(dve, own, 2 * s - 1, k.constants)
                nc.vector.tensor_scalar(w[:], w[:], inverse[:], threshold, ALU.mult, ALU.is_ge).then_inc(own, 1)
                wait_alone(dve, own, 2 * s, k.constants)
                nc.vector.scalar_tensor_tensor(w[:], w[:], columns(k.comp_mask, s - 1, 1), k.ring[(r - 1) % RING_B][:],
                                               ALU.mult, ALU.mult, accum_out=columns(k.conn, s - 1, 1)).then_inc(pruned, 1)

            def step(s, r, turn):
                if isinstance(s, int) and s == NB:
                    finish(s, r)
                    return
                wait_loaded(dve, loaded, r, turn, False)
                at_least(dve, stored[r % 2], 32 * turn + 16 * (r // 2))
                for ch, (start, width, _) in enumerate(CHUNKS):
                    cols = slice(start, start + width)
                    wait_alone(dve, scored, NCH * s + ch + 1, k.constants)
                    nc.vector.tensor_tensor_reduce(out=k.work[r % 2][:, cols], in0=scores(k, CHUNKS, bufs, r, ch),
                                                   in1=k.ring[r][:, cols], scale=1.0, scalar=LOWEST, op0=ALU.mult,
                                                   op1=ALU.max, accum_out=k.mx[:, ch:ch + 1]).then_inc(masked, 1)
                dve.wait_ge(masked, NCH * (s + 1))
                nc.vector.tensor_reduce(k.nmax[r % 2][:], k.mx[:], AX.X, ALU.max, negate=True).then_inc(neg_max, 1)
                dve.wait_ge(neg_max, s + 1)
                if not (isinstance(s, int) and s == 0):
                    finish(s, r)
            steps(dve, step, RING_B, NB + 1, peel=RING_B, tail=1)


def queries(k, tag):
    nc = k.nc
    nt_done, nt_copied, q_done = k.sem(f"{tag}_nt"), k.sem(f"{tag}_nt_copied"), k.sem(f"{tag}_q")
    q_hi, q_lo = k.sem(f"{tag}_q_hi"), k.sem(f"{tag}_q_lo")
    groups = NB // (2 * PER)

    def q_columns(g, j, rows=slice(0, P)):
        cols = k.stat_op[rows, g * 2 * BANK:(g + 1) * 2 * BANK]
        return cols.rearrange("p (i j c) -> p i j c", i=PER, j=2)[:, :, j, :]

    def q_bank(j, rows=slice(0, P)):
        return k.bank(2 + j, rows=rows).rearrange("p (i c) -> p i c", i=PER)

    with nc.Block() as block:
        @block.scalar
        def _(act):
            for g in range(groups):
                act.wait_ge(nt_done, g + 1)
                at_least(act, q_done, 2 * (g - 1))
                nc.scalar.activation(k.n_t8[g % 2][:], k.bank(g % 2), ACT.Copy).then_inc(nt_copied, 1)
                act.wait_ge(q_done, 2 * (g + 1))
                for j in range(2):
                    nc.scalar.activation(q_columns(g, j), q_bank(j), ACT.Identity, bias=k.b_q8[:], scale=1.0).then_inc(q_hi, 1)

        @block.tensor
        def _(pe):
            for g in range(groups):
                at_least(pe, nt_copied, g - 1)
                for m in range(PER):
                    b = g * 2 * PER + 2 * m
                    done = nc.tensor.transpose(k.bank(g % 2, P, m * P), k.n1[:, b:b + 2, :].rearrange("p j d -> p (j d)"),
                                               k.ident[:])
                done.then_inc(nt_done, 1)
                pe.wait_ge(nt_copied, g + 1)
                at_least(pe, q_lo, 2 * g)
                for j in range(2):
                    nc.tensor.matmul(k.bank(2 + j), k.w_q8[:, j, :], k.n_t8[g % 2][:], start=True, stop=True)\
                      .then_inc(q_done, 1)

        @block.vector
        def _(dve):
            low = slice(D, P)
            for g in range(groups):
                for j in range(2):
                    dve.wait_ge(q_hi, 2 * g + j + 1)
                    nc.vector.scalar_tensor_tensor(q_columns(g, j, low), q_bank(j, low), k.b_q8[low, :],
                                                   q_columns(g, j, low).bitcast(FP32), ALU.add, ALU.subtract)\
                      .then_inc(q_lo, 1)


def rows_times(k, tag, src, weights, bank, cols, consume, before=None, scalar_before=None):
    nc = k.nc
    ready, turned, copied = k.sem(f"{tag}_ready"), k.sem(f"{tag}_turned"), k.sem(f"{tag}_copied")
    product, consumed = k.sem(f"{tag}_product"), k.sem(f"{tag}_consumed")
    groups = NB // PER
    with nc.Block() as block:
        @block.scalar
        def _(act):
            if scalar_before is not None:
                scalar_before(act)
            for g in range(groups):
                act.wait_ge(turned, g + 1)
                at_least(act, product, g - 1)
                nc.scalar.activation(k.n_t4[g % 2][:], k.bank(g % 2, rows=slice(0, D)), ACT.Copy).then_inc(copied, 1)

        @block.tensor
        def _(pe):
            pe.wait_ge(ready, 1)
            for g in range(groups + 1):
                if g < groups:
                    at_least(pe, copied, g - 1)
                    for m in range(PER):
                        done = nc.tensor.transpose(k.bank(g % 2, P, m * P, slice(0, D)), src[:, g * PER + m, :], k.ident[:])
                    done.then_inc(turned, 1)
                if g >= 1:
                    f = g - 1
                    pe.wait_ge(copied, f + 1)
                    at_least(pe, consumed, f - 1)
                    for m in range(PER):
                        done = nc.tensor.matmul(k.bank(bank + f % 2, cols, m * cols), k.n_t4[f % 2][:, m * P:(m + 1) * P],
                                                weights, start=True, stop=True)
                    done.then_inc(product, 1)

        @block.vector
        def _(dve):
            if before is not None:
                before(dve)
            nc.vector.tensor_copy(k.one[0][:], k.ones[:]).then_inc(ready, 1)
            for g in range(groups):
                dve.wait_ge(product, g + 1)
                view = k.bank(bank + g % 2, PER * cols).rearrange("p (m c) -> p m c", m=PER)
                consume(dve, g, view).then_inc(consumed, 1)
            dve.wait_ge(consumed, groups)


def values(k, tag):
    nc, i = k.nc, k.i
    weights, own = k.sem(f"{tag}_weights"), k.sem(f"{tag}_own")
    with nc.Block() as block:
        @block.sync
        def _(sp):
            for dst, src in ((k.g_w[:, 0:D], i["Wv"]), (k.g_w[:, D:2 * D], i["W"]),
                             (k.g_b[:], i["bv"].partition_broadcast(P))):
                sp.dma_start(dst, src).then_inc(weights, 16)
            sp.wait_ge(weights, 48)
    state = {}

    def before(dve):
        state["link"] = Chain(dve, own)

    def consume(dve, g, view):
        link, b = state["link"], slice(g * PER, (g + 1) * PER)
        link(nc.vector.tensor_tensor(k.tall[:, b, :], view[:, :, 0:D], k.g_b[:].unsqueeze(1).to_broadcast([P, PER, D]),
                                     ALU.add))
        link(nc.vector.tensor_copy(k.g_xw[:], view[:, :, D:2 * D]))
        link(nc.vector.tensor_tensor(k.g_xw[:], k.g_xw[:], k.g_xw[:], ALU.mult))
        link(nc.vector.reduce_sum(k.ssq_xw[:, b], k.g_xw[:], AX.X))
        link(nc.vector.tensor_tensor(k.g_xw[:], k.n1[:, b, :], k.n1[:, b, :], ALU.mult))
        link(nc.vector.reduce_sum(k.sq_n[:, b], k.g_xw[:], AX.X))
        return nc.vector.tensor_copy(k.one[0][:], k.ones[:])

    rows_times(k, tag, k.n1, k.g_w[:], 2, 2 * D, consume, before)


def node_operand(k, tag, layer):
    nc, i = k.nc, k.i
    weights, own = k.sem(f"{tag}_weights"), k.sem(f"{tag}_own")
    var, root = k.sem(f"{tag}_degrees"), k.sem(f"{tag}_roots")
    top = Across(k, f"{tag}_max", ALU.max, (4, 5))
    total = Across(k, f"{tag}_total", ALU.add, (6, 7))
    with nc.Block() as block:
        @block.sync
        def _(sp):
            sp.dma_start(k.g_w[:, 0:D], i["W"]).then_inc(weights, 16)
            sp.wait_ge(weights, 16)

        @block.tensor
        def _(pe):
            top.tensor(pe, k.one[0])
            total.tensor(pe, k.one[0])

        @block.scalar
        def _(act):
            act.wait_ge(top.out, 1)
            nc.scalar.activation(k.rows3[:], k.rows[:], ACT.Exp, bias=k.one[1][:], accum_out=k.one[0][:])\
              .then_inc(total.column, 1)
            act.wait_ge(var, 1)
            nc.scalar.activation(k.structural[:], k.z[:], ACT.Sqrt).then_inc(root, 1)

        @block.vector
        def _(dve):
            link = Chain(dve, own)
            link(nc.vector.tensor_tensor(k.rows[:], k.conn[:], k.feat_mag[:], ALU.mult))
            nc.vector.reduce_max(k.one[0][:], k.rows[:], AX.X).then_inc(top.column, 1)
            top.vector(dve, k.one[1], -1.0)
            link(nc.vector.tensor_scalar(k.z[:], k.conn[:], EPS, None, ALU.max))
            nc.vector.tensor_copy(k.mx[:, 0:1], k.z[:, 0:1]).then_inc(var, 1)
            total.vector(dve, k.one[2])
            dve.wait_ge(root, 1)
            inv_sqrt(nc, link, k.structural[:], k.z[:], k.structural[:], k.rows2[:])
            link(nc.vector.reciprocal(k.one[3][:], k.one[2][:]))
            link(nc.vector.tensor_scalar(k.rows3[:], k.rows3[:], k.one[3][:], THRESHOLDS[layer], ALU.mult, ALU.is_ge))
            link(nc.vector.tensor_tensor(k.rows3[:], k.rows3[:], k.comp_mask[:], ALU.mult))
            link(nc.vector.tensor_scalar(k.rows[:], k.conn[:], 0.0, None, ALU.is_gt))
            link(nc.vector.tensor_tensor(k.rows3[:], k.rows3[:], k.rows[:], ALU.mult))
            link(nc.vector.tensor_tensor(k.h[:], k.n1[:], k.rows3[:].unsqueeze(2).to_broadcast([P, NB, D]), ALU.mult))

    def consume(dve, g, view):
        b = slice(g * PER, (g + 1) * PER)
        return nc.vector.tensor_tensor(k.tall[:, b, :], view, k.structural[:, b].unsqueeze(2).to_broadcast([P, PER, D]),
                                       ALU.mult)

    rows_times(k, f"{tag}_w", k.h, k.g_w[:, 0:D], 2, D, consume)


def edge_degrees(k, tag):
    nc = k.nc
    out, moved, turned, own = k.sem(f"{tag}_out"), k.sem(f"{tag}_moved"), k.sem(f"{tag}_turned"), k.sem(f"{tag}_own")
    with nc.Block() as block:
        @block.scalar
        def _(act):
            for h in range(4):
                cols = BANK * (3 if h < 2 else 2)
                nc.scalar.activation(k.colsum[32 * h:32 * h + 1, 0:cols], k.bank(5, cols, rows=slice(32 * h, 32 * h + 1)),
                                     ACT.Copy).then_inc(out, 1)

        @block.sync
        def _(sp):
            sp.wait_ge(out, 4)
            for q in range(NQ):
                src = k.colsum[32 * (q % 4):32 * (q % 4) + 1, q // 4 * BANK:(q // 4 + 1) * BANK]
                sp.dma_start(k.colsum_rows[PER * q:PER * (q + 1), :], src.rearrange("p (m c) -> p m c", m=PER))\
                  .then_inc(moved, 16)

        @block.tensor
        def _(pe):
            pe.wait_ge(moved, NQ * 16)
            nc.tensor.transpose(k.bank(5, NB), k.colsum_rows[:], k.ident[0:NB, 0:NB]).then_inc(turned, 1)

        @block.vector
        def _(dve):
            link = Chain(dve, own)
            dve.wait_ge(turned, 1)
            link(nc.vector.tensor_scalar(k.rows[:], k.bank(5, NB), EPS, None, ALU.max))
            link(nc.vector.reciprocal(k.rz[:], k.rows[:]))


def row_pass(k, tag):
    nc = k.nc
    loaded, used = k.sem_list(f"{tag}_loaded", RING_B), k.sem(f"{tag}_used")
    turned, copied, read = k.sem(f"{tag}_turned"), k.sem(f"{tag}_copied"), k.sem(f"{tag}_read")
    with nc.Block() as block:
        @block.sync
        def _(sp):
            load_ring(k, sp, k.hp_v, loaded, used, RING_B, True, True)

        @block.scalar
        def _(act):
            def step(s, r, turn):
                for q in range(NQ):
                    act.wait_ge(turned, NQ * s + q + 1)
                    nc.scalar.activation(k.adj_t[q % 4][:], k.bank(q % 4), ACT.Copy).then_inc(copied, 1)
            steps(act, step, RING_B, NB)

        @block.vector
        def _(dve):
            def step(s, r, turn):
                wait_alone(dve, used, s + 1, k.constants)
                b = NB - 1 - s
                nc.vector.tensor_copy(k.g_dv[:], columns(k.structural, b, 1)).then_inc(read, 1)
                wait_alone(dve, read, 2 * s + 1, k.constants)
                nc.vector.tensor_scalar(block_of(k.msg, b), k.bank(6 + r % 2, D), k.g_dv[:], None, ALU.mult)\
                  .then_inc(read, 1)
                dve.wait_ge(read, 2 * s + 2)
            steps(dve, step, RING_B, NB)

        @block.tensor
        def _(pe):
            def step(s, r, turn):
                wait_loaded(pe, loaded, r, turn, True)
                rows = k.ring[slot_of(r, RING_B, True)]
                at_least(pe, read, 2 * s - 2)
                for q in range(NQ + 2):
                    if q < NQ:
                        at_least(pe, copied, NQ * s + q - 3)
                        for m in range(PER):
                            c = q * BANK + m * P
                            done = nc.tensor.transpose(k.bank(q % 4, P, m * P), rows[:, c:c + P], k.ident[:])
                        done.then_inc(turned, 1)
                    if q >= 2:
                        f = q - 2
                        pe.wait_ge(copied, NQ * s + f + 1)
                        for m in range(PER):
                            done = nc.tensor.matmul(k.bank(6 + r % 2, D), k.adj_t[f % 4][:, m * P:(m + 1) * P],
                                                    k.tall[:, f * PER + m, :], start=f == 0 and m == 0,
                                                    stop=f == NQ - 1 and m == PER - 1)
                done.then_inc(used, 1)
            steps(pe, step, RING_B, NB)


def remaining_edges(k, tag, layer):
    nc = k.nc
    prune_pass(k, f"{tag}_prune", THRESHOLDS[layer])
    node_operand(k, f"{tag}_node", layer)
    column_pass(k, f"{tag}_agg", k.hp_v, k.tall, RING_B, degrees=True)
    edge_degrees(k, f"{tag}_deg")
    by_blocks(k, f"{tag}_agg", k.wide, k.tall, k.rz)
    row_pass(k, f"{tag}_msg")
    own = k.sem(f"{tag}_out_own")
    state = {}

    def before(dve):
        state["link"] = Chain(dve, own)

    def consume(dve, g, view):
        b = slice(g * PER, (g + 1) * PER)
        if layer == 0:
            return nc.vector.tensor_scalar(k.n1[:, b, :], view, 0.0, None, ALU.max)
        state["link"](nc.vector.tensor_scalar(k.tall[:, b, :], view, 0.0, None, ALU.max))
        return nc.vector.tensor_tensor(k.x1[:, b, :], k.x1[:, b, :], k.tall[:, b, :], ALU.add)

    rows_times(k, f"{tag}_out", k.msg, k.theta[:], 2, D, consume, before)


def program(nc, ins, out):
    k = Kernel(nc, ins, out)
    embed_and_columns(k)
    network_and_features(k)
    features_operand(k, "att")
    edge_loaded = k.sem_list("edge_loaded", RING_A)
    softmax_pass(k, "att", True, 0, k.sem_list("att_loaded", RING_A), True, following=edge_loaded)
    component_mask(k, "comp", 0)
    stored = k.sem("x1_stored")

    def store(sp):
        sp.dma_start(k.out_v, k.x1[:]).then_inc(stored, 16)
    softmax_pass(k, "edge", False, NB % RING_A, edge_loaded, False, first_sync=store)
    any_edge(k, "flag", 0)
    with nc.Block() as block:
        @block.sync
        def _(sp):
            sp.wait_ge(stored, 16)
    edges_left = nc.values_load(k.flag[0:1, 0:1], min_val=0, max_val=1)
    with nc.If(edges_left > 0):
        k.fresh_semaphores()
        remaining_edges(k, "l0", 0)
        k.fresh_semaphores()
        values(k, "l1_v")
        column_pass(k, "l1_edge", k.adj_v, k.tall, RING_B)
        features_operand(k, "l1_att")
        queries(k, "l1_att_q")
        first_rows = k.sem_list("l1_att_loaded", RING_A)
        with nc.Block() as block:
            @block.sync
            def _(sp):
                for s in range(RING_A):
                    sp.dma_start(k.ring[s][:], k.adj_v[s]).then_inc(first_rows[s], 16)
        softmax_pass(k, "l1_att", True, 0, first_rows, False)
        component_mask(k, "l1_comp", 1)
        k.fresh_semaphores()
        remaining_edges(k, "l1", 1)
        result = k.sem("result_stored")
        with nc.Block() as block:
            @block.sync
            def _(sp):
                sp.dma_start(k.out_v, k.x1[:]).then_inc(result, 16)
                sp.wait_ge(result, 16)


_INS = {'x': 'x', 'adj': 'adj', 'L0_gnn_W_u': 'W_u', 'L0_gnn_diag_u': 'diag_u', 'L0_gnn_par_u': 'par_u',
        'L0_gnn_W_i': 'W_i', 'L0_gnn_diag_i': 'diag_i', 'L0_gnn_par_i': 'par_i', 'L0_gnn_ln_gamma': 'ln_gamma',
        'L0_gnn_ln_beta': 'ln_beta', 'L1_gnn_W': 'W', 'L1_gnn_Theta': 'Theta', 'L1_gnn_Wq': 'Wq',
        'L1_gnn_bq': 'bq', 'L1_gnn_Wv': 'Wv', 'L1_gnn_bv': 'bv'}


def kernel(**inputs):
    import numpy as _np
    import concourse.bacc as _bacc
    from concourse import mybir as _mybir
    from concourse.bass_utils import run_bass_kernel_spmd as _run

    nc = _bacc.Bacc("TRN2", target_bir_lowering=False, num_devices=1)
    arrays, ins = {}, {}
    for name, short in _INS.items():
        a = _np.ascontiguousarray(inputs[name])
        arrays[f"in_{name}_dram"] = a
        ins[short] = nc.dram_tensor(f"in_{name}_dram", a.shape, _mybir.dt.from_np(a.dtype), kind="ExternalInput").ap()
    out = nc.dram_tensor("out_0_dram", (5120, 64), _mybir.dt.float32, kind="ExternalOutput").ap()
    program(nc, ins, out)
    r = _run(nc, [arrays], core_ids=[0])
    return r.results[0]["out_0_dram"]
```
